# Optimizing a Trainium2 kernel written in Bass

```python
import numpy as np
import jax
import jax.numpy as jnp

def _softmax(x, axis=-1):
    return jax.nn.softmax(x, axis=axis)

def _gelu(x):
    return jax.nn.gelu(x, approximate=True)

def _silu(x):
    return jax.nn.silu(x)

def _sigmoid(x):
    return jax.nn.sigmoid(x)

def _layernorm(x, axis=-1, eps=1e-05):
    m = jnp.mean(x, axis=axis, keepdims=True)
    v = jnp.var(x, axis=axis, keepdims=True)
    return (x - m) / jnp.sqrt(v + eps)

def _scatter_add(tgt, idx, src, axis=0):
    return tgt.at[idx].add(src)

def _segment_sum(src, seg, n):
    return jax.ops.segment_sum(src, seg, n)
kernel_name = 'mk_xattn_seq_d4_seqx_r4_6b6b76'

def setup_inputs(seed: int=0):
    np.random.seed(seed)
    _w = jnp.asarray

    def _rec_inputs():
        import jax
        import jax.numpy as jnp
        _rk = jax.random.key(seed)
        x = 7.22e-05 + 1 * jax.random.normal(jax.random.fold_in(_rk, 1), (32, 128, 512), jnp.float32)
        _lenS = 128 - jax.random.randint(jax.random.fold_in(_rk, 7), (32,), 0, max(1, 128 // 4) + 1, jnp.int32)
        _lenS2 = 128 - jax.random.randint(jax.random.fold_in(_rk, 8), (32,), 0, max(1, 128 // 4) + 1, jnp.int32)
        _ctx_2048P = jax.random.normal(jax.random.fold_in(_rk, 11), (32, 16, 512), jnp.float32)
        _ctx_2048c = jax.random.dirichlet(jax.random.fold_in(_rk, 511), 0.3 * jnp.ones((16,), jnp.float32), (32, 128))
        _ctx_2048t = jnp.einsum('bsk,bkd->bsd', _ctx_2048c, _ctx_2048P)
        _ctx_2048t = _ctx_2048t * jax.lax.rsqrt(jnp.mean(jnp.square(_ctx_2048t)) + 1e-12) * 0.953939
        ctx_2048 = 4.13588e-05 + 0.999923 * (_ctx_2048t + 0.3 * jax.random.normal(jax.random.fold_in(_rk, 611), (32, 128, 512), jnp.float32))
        _validS = jnp.arange(128)[None, :] < _lenS[:, None]
        _validS2 = jnp.arange(128)[None, :] < _lenS2[:, None]
        _causal = jnp.tril(jnp.ones((128, 128), dtype=bool))
        mask_Bx1xSxS2_ff0 = jnp.where(jnp.ones((32, 1, 128, 128), dtype=bool), 0.0, -1000000000.0).astype(jnp.float32)
        mask_BxS2_bf1 = jnp.ones((32, 128), dtype=bool)
        return (x, ctx_2048, mask_Bx1xSxS2_ff0, mask_BxS2_bf1)
    x, ctx_2048, mask_Bx1xSxS2_ff0, mask_BxS2_bf1 = _rec_inputs()

    def _L0_xattn_setup():
        import jax, jax.numpy as jnp
        import numpy as np
        H = 512
        NH = 32
        KVH = 8
        HD = H // NH
        GROUPS = NH // KVH
        EPS = 1e-06
        B, L, S = (4, 256, 256)

        def _gqa_forward(hidden_state, encoder_hidden_state, encoder_attention_mask, Wq, bq, Wk, bk, Wv, bv, Wo, bo, gamma, beta):
            b, l, _ = hidden_state.shape
            s = encoder_hidden_state.shape[1]
            q = hidden_state @ Wq + bq
            k = encoder_hidden_state @ Wk + bk
            v = encoder_hidden_state @ Wv + bv
            q = q.reshape(b, l, KVH, GROUPS, HD).transpose(0, 2, 3, 1, 4)
            k = k.reshape(b, s, KVH, HD).transpose(0, 2, 1, 3)
            v = v.reshape(b, s, KVH, HD).transpose(0, 2, 1, 3)
            scale = 1.0 / jnp.sqrt(jnp.asarray(HD, q.dtype))
            scores = jnp.einsum('bkgld,bksd->bkgls', q, k) * scale
            scores = scores + encoder_attention_mask[:, :, None, :, :]
            attn = jax.nn.softmax(scores, axis=-1)
            out = jnp.einsum('bkgls,bksd->bkgld', attn, v)
            out = out.transpose(0, 3, 1, 2, 4).reshape(b, l, H)
            out = out @ Wo + bo
            x = out + hidden_state
            mu = jnp.mean(x, axis=-1, keepdims=True)
            var = jnp.var(x, axis=-1, keepdims=True)
            return (x - mu) * jax.lax.rsqrt(var + EPS) * gamma + beta
        key = jax.random.key(seed)
        ks = jax.random.split(key, 12)
        sd = 0.02
        return {'hidden_state': jax.random.normal(ks[0], (B, L, H), jnp.float32), 'encoder_hidden_state': jax.random.normal(ks[1], (B, S, H), jnp.float32), 'encoder_attention_mask': jnp.zeros((B, 1, L, S), jnp.float32), 'Wq': jax.random.normal(ks[2], (H, H), jnp.float32) * sd, 'bq': jnp.zeros((H,), jnp.float32), 'Wk': jax.random.normal(ks[3], (H, KVH * HD), jnp.float32) * sd, 'bk': jnp.zeros((KVH * HD,), jnp.float32), 'Wv': jax.random.normal(ks[4], (H, KVH * HD), jnp.float32) * sd, 'bv': jnp.zeros((KVH * HD,), jnp.float32), 'Wo': jax.random.normal(ks[5], (H, H), jnp.float32) * sd, 'bo': jnp.zeros((H,), jnp.float32), 'gamma': jnp.ones((H,), jnp.float32), 'beta': jnp.zeros((H,), jnp.float32)}
    _L0_xattn_all = _L0_xattn_setup()
    _L0_xattn_in = {k: v for k, v in _L0_xattn_all.items() if k in ('Wq', 'bq', 'Wk', 'bk', 'Wv', 'bv', 'Wo', 'bo', 'gamma', 'beta')}
    del _L0_xattn_all

    def _L1_xattn_setup():
        import jax, jax.numpy as jnp
        import numpy as np
        B, C, CI, T = (8, 128, 64, 512)
        EPS = 1e-05
        key = jax.random.key(seed)
        ks = jax.random.split(key, 8)
        inv_c = 1.0 / np.sqrt(C)
        inv_ci = 1.0 / np.sqrt(CI)
        return {'x_this': jax.random.normal(ks[0], (B, C, T), jnp.float32), 'x_other': jax.random.normal(ks[1], (B, C, T), jnp.float32), 'Wg': jax.random.normal(ks[2], (CI, C), jnp.float32) * inv_c, 'bg': jnp.zeros((CI,), jnp.float32), 'Wtheta': jax.random.normal(ks[3], (CI, C), jnp.float32) * inv_c, 'btheta': jnp.zeros((CI,), jnp.float32), 'Wphi': jax.random.normal(ks[4], (CI, C), jnp.float32) * inv_c, 'bphi': jnp.zeros((CI,), jnp.float32), 'Wz': jax.random.normal(ks[5], (C, CI), jnp.float32) * inv_ci, 'bz': jnp.zeros((C,), jnp.float32), 'gamma': jax.random.normal(ks[6], (C,), jnp.float32), 'beta': jax.random.normal(ks[7], (C,), jnp.float32)}
    _L1_xattn_all = _L1_xattn_setup()
    _L1_xattn_in = {k: v for k, v in _L1_xattn_all.items() if k in ('Wg', 'bg', 'Wtheta', 'btheta', 'Wphi', 'bphi', 'Wz', 'bz', 'gamma', 'beta')}
    del _L1_xattn_all

    def _L2_xattn_setup():
        import jax, jax.numpy as jnp
        import numpy as np
        E, H, L, B = (512, 32, 256, 4)
        S = E // H
        DM, DD = (32, 64)

        def _ln(x, w, b, eps=1e-05):
            m = x.mean(-1, keepdims=True)
            v = ((x - m) ** 2).mean(-1, keepdims=True)
            return (x - m) / jnp.sqrt(v + eps) * w + b

        def _block(x, state, ln1_w, ln1_b, ln2_w, ln2_b, maa_x, maa_w1, maa_w2, maa_stack, time_decay, td_w1, td_w2, u, Wr, Wk, Wv, Wg, Wo, gn_w, gn_b, ffn_maa_k, ffn_maa_r, Wfk, Wfr, Wfv):
            b, l, e = x.shape
            h = u.shape[0]
            s_ = e // h
            xa = _ln(x, ln1_w, ln1_b)
            sx = jnp.concatenate([state[:, 1:2] - xa[:, :1], xa[:, :-1] - xa[:, 1:]], axis=1)
            xxx = jnp.tanh((xa + sx * maa_x) @ maa_w1).reshape(b, l, 5, DM)
            xxx = jnp.einsum('blfd,fde->blfe', xxx, maa_w2)
            xm = xa[:, :, None] + sx[:, :, None] * (maa_stack + xxx)
            xk, xw, xv, xr, xg = (xm[:, :, j] for j in range(5))
            w = jnp.exp(-jnp.exp(time_decay + jnp.tanh(xw @ td_w1) @ td_w2)).reshape(b, l, h, s_)
            r = (xr @ Wr.T).reshape(b, l, h, s_)
            k = (xk @ Wk.T).reshape(b, l, h, s_)
            v = (xv @ Wv.T).reshape(b, l, h, s_)
            g = jax.nn.silu(xg @ Wg.T)
            s0 = state[:, 2:2 + s_].reshape(b, h, s_, s_)

            def step(s, rkvw):
                r_t, k_t, v_t, w_t = rkvw
                a = k_t[..., :, None] * v_t[..., None, :]
                out = jnp.einsum('bhi,bhij->bhj', r_t, u * a + s)
                s = a + w_t[..., :, None] * s
                return (s, out)
            rkvw = tuple((jnp.moveaxis(t, 1, 0) for t in (r, k, v, w)))
            _, out = jax.lax.scan(step, s0, rkvw)
            out = jnp.moveaxis(out, 0, 1).reshape(b, l, e)
            og = out.reshape(b, l, h, s_)
            m = og.mean(-1, keepdims=True)
            va = ((og - m) ** 2).mean(-1, keepdims=True)
            og = ((og - m) / jnp.sqrt(va + 1e-05)).reshape(b, l, e) * gn_w + gn_b
            x1 = x + og * g @ Wo.T
            xc = _ln(x1, ln2_w, ln2_b)
            sx2 = jnp.concatenate([state[:, 0:1] - xc[:, :1], xc[:, :-1] - xc[:, 1:]], axis=1)
            xk2 = xc + sx2 * ffn_maa_k
            xr2 = xc + sx2 * ffn_maa_r
            rr = jax.nn.sigmoid(xr2 @ Wfr.T)
            kk = jnp.square(jax.nn.relu(xk2 @ Wfk.T))
            return x1 + rr * (kk @ Wfv.T)
        key = jax.random.key(seed)
        ks = jax.random.split(key, 24)
        sc = 0.02
        d = {'x': jax.random.normal(ks[0], (B, L, E), jnp.float32), 'state': jax.random.normal(ks[1], (B, 2 + S, E), jnp.float32) * 0.1, 'ln1_w': jnp.ones((E,), jnp.float32), 'ln1_b': jnp.zeros((E,), jnp.float32), 'ln2_w': jnp.ones((E,), jnp.float32), 'ln2_b': jnp.zeros((E,), jnp.float32), 'maa_x': jax.random.normal(ks[2], (E,), jnp.float32) * 0.1, 'maa_w1': jax.random.normal(ks[3], (E, 5 * DM), jnp.float32) * sc, 'maa_w2': jax.random.normal(ks[4], (5, DM, E), jnp.float32) * sc, 'maa_stack': jax.random.normal(ks[5], (1, 5, E), jnp.float32) * 0.1, 'time_decay': jax.random.normal(ks[6], (E,), jnp.float32) * 0.5, 'td_w1': jax.random.normal(ks[7], (E, DD), jnp.float32) * sc, 'td_w2': jax.random.normal(ks[8], (DD, E), jnp.float32) * sc, 'u': jax.random.normal(ks[9], (H, S, 1), jnp.float32) * 0.1, 'Wr': jax.random.normal(ks[10], (E, E), jnp.float32) * sc, 'Wk': jax.random.normal(ks[11], (E, E), jnp.float32) * sc, 'Wv': jax.random.normal(ks[12], (E, E), jnp.float32) * sc, 'Wg': jax.random.normal(ks[13], (E, E), jnp.float32) * sc, 'Wo': jax.random.normal(ks[14], (E, E), jnp.float32) * sc, 'gn_w': jnp.ones((E,), jnp.float32), 'gn_b': jnp.zeros((E,), jnp.float32), 'ffn_maa_k': jax.random.normal(ks[15], (E,), jnp.float32) * 0.1, 'ffn_maa_r': jax.random.normal(ks[16], (E,), jnp.float32) * 0.1, 'Wfk': jax.random.normal(ks[17], (E, E), jnp.float32) * sc, 'Wfr': jax.random.normal(ks[18], (E, E), jnp.float32) * sc, 'Wfv': jax.random.normal(ks[19], (E, E), jnp.float32) * sc}
        return d
    _L2_xattn_all = _L2_xattn_setup()
    _L2_xattn_in = {k: v for k, v in _L2_xattn_all.items() if k in ('ln1_w', 'ln1_b', 'ln2_w', 'ln2_b', 'maa_x', 'maa_w1', 'maa_w2', 'maa_stack', 'time_decay', 'td_w1', 'td_w2', 'u', 'Wr', 'Wk', 'Wv', 'Wg', 'Wo', 'gn_w', 'gn_b', 'ffn_maa_k', 'ffn_maa_r', 'Wfk', 'Wfr', 'Wfv')}
    del _L2_xattn_all

    def _L3_xattn_setup():
        import jax, jax.numpy as jnp
        import numpy as np
        D = 512
        H = 16
        HD = D // H
        INNER = 4 * D
        EPS = 1e-05

        def layer_norm(x, w, b):
            mu = jnp.mean(x, axis=-1, keepdims=True)
            var = jnp.mean(jnp.square(x - mu), axis=-1, keepdims=True)
            return (x - mu) * jax.lax.rsqrt(var + EPS) * w + b
        key = jax.random.key(seed)
        ks = jax.random.split(key, 12)
        B, LQ, LK = (4, 256, 512)
        std = 0.02
        inp = {'hidden_states': jax.random.normal(ks[0], (B, LQ, D), jnp.float32), 'encoder_hidden_states': jax.random.normal(ks[1], (B, LK, D), jnp.float32), 'encoder_attention_mask': jnp.ones((B, LK), dtype=bool), 'ln1_w': jnp.ones((D,), jnp.float32), 'ln1_b': jnp.zeros((D,), jnp.float32), 'q_w': jax.random.normal(ks[2], (D, D), jnp.float32) * std, 'q_b': jnp.zeros((D,), jnp.float32), 'k_w': jax.random.normal(ks[3], (D, D), jnp.float32) * std, 'k_b': jnp.zeros((D,), jnp.float32), 'v_w': jax.random.normal(ks[4], (D, D), jnp.float32) * std, 'v_b': jnp.zeros((D,), jnp.float32), 'cproj_w': jax.random.normal(ks[5], (D, D), jnp.float32) * std, 'cproj_b': jnp.zeros((D,), jnp.float32), 'ln2_w': jnp.ones((D,), jnp.float32), 'ln2_b': jnp.zeros((D,), jnp.float32), 'fc_w': jax.random.normal(ks[6], (D, INNER), jnp.float32) * std, 'fc_b': jnp.zeros((INNER,), jnp.float32), 'proj_w': jax.random.normal(ks[7], (INNER, D), jnp.float32) * std, 'proj_b': jnp.zeros((D,), jnp.float32)}
        return inp
    _L3_xattn_all = _L3_xattn_setup()
    _L3_xattn_in = {k: v for k, v in _L3_xattn_all.items() if k in ('ln1_w', 'ln1_b', 'q_w', 'q_b', 'k_w', 'k_b', 'v_w', 'v_b', 'cproj_w', 'cproj_b', 'ln2_w', 'ln2_b', 'fc_w', 'fc_b', 'proj_w', 'proj_b')}
    del _L3_xattn_all
    return {'x': x, 'ctx_2048': ctx_2048, 'mask_Bx1xSxS2_ff0': mask_Bx1xSxS2_ff0, 'mask_BxS2_bf1': mask_BxS2_bf1, 'L0_xattn_Wq': _L0_xattn_in['Wq'], 'L0_xattn_bq': _L0_xattn_in['bq'], 'L0_xattn_Wk': _L0_xattn_in['Wk'], 'L0_xattn_bk': _L0_xattn_in['bk'], 'L0_xattn_Wv': _L0_xattn_in['Wv'], 'L0_xattn_bv': _L0_xattn_in['bv'], 'L0_xattn_Wo': _L0_xattn_in['Wo'], 'L0_xattn_bo': _L0_xattn_in['bo'], 'L0_xattn_gamma': _L0_xattn_in['gamma'], 'L0_xattn_beta': _L0_xattn_in['beta'], 'L1_xattn_Wg': _L1_xattn_in['Wg'], 'L1_xattn_bg': _L1_xattn_in['bg'], 'L1_xattn_Wtheta': _L1_xattn_in['Wtheta'], 'L1_xattn_btheta': _L1_xattn_in['btheta'], 'L1_xattn_Wphi': _L1_xattn_in['Wphi'], 'L1_xattn_bphi': _L1_xattn_in['bphi'], 'L1_xattn_Wz': _L1_xattn_in['Wz'], 'L1_xattn_bz': _L1_xattn_in['bz'], 'L1_xattn_gamma': _L1_xattn_in['gamma'], 'L1_xattn_beta': _L1_xattn_in['beta'], 'L2_xattn_ln1_w': _L2_xattn_in['ln1_w'], 'L2_xattn_ln1_b': _L2_xattn_in['ln1_b'], 'L2_xattn_ln2_w': _L2_xattn_in['ln2_w'], 'L2_xattn_ln2_b': _L2_xattn_in['ln2_b'], 'L2_xattn_maa_x': _L2_xattn_in['maa_x'], 'L2_xattn_maa_w1': _L2_xattn_in['maa_w1'], 'L2_xattn_maa_w2': _L2_xattn_in['maa_w2'], 'L2_xattn_maa_stack': _L2_xattn_in['maa_stack'], 'L2_xattn_time_decay': _L2_xattn_in['time_decay'], 'L2_xattn_td_w1': _L2_xattn_in['td_w1'], 'L2_xattn_td_w2': _L2_xattn_in['td_w2'], 'L2_xattn_u': _L2_xattn_in['u'], 'L2_xattn_Wr': _L2_xattn_in['Wr'], 'L2_xattn_Wk': _L2_xattn_in['Wk'], 'L2_xattn_Wv': _L2_xattn_in['Wv'], 'L2_xattn_Wg': _L2_xattn_in['Wg'], 'L2_xattn_Wo': _L2_xattn_in['Wo'], 'L2_xattn_gn_w': _L2_xattn_in['gn_w'], 'L2_xattn_gn_b': _L2_xattn_in['gn_b'], 'L2_xattn_ffn_maa_k': _L2_xattn_in['ffn_maa_k'], 'L2_xattn_ffn_maa_r': _L2_xattn_in['ffn_maa_r'], 'L2_xattn_Wfk': _L2_xattn_in['Wfk'], 'L2_xattn_Wfr': _L2_xattn_in['Wfr'], 'L2_xattn_Wfv': _L2_xattn_in['Wfv'], 'L3_xattn_ln1_w': _L3_xattn_in['ln1_w'], 'L3_xattn_ln1_b': _L3_xattn_in['ln1_b'], 'L3_xattn_q_w': _L3_xattn_in['q_w'], 'L3_xattn_q_b': _L3_xattn_in['q_b'], 'L3_xattn_k_w': _L3_xattn_in['k_w'], 'L3_xattn_k_b': _L3_xattn_in['k_b'], 'L3_xattn_v_w': _L3_xattn_in['v_w'], 'L3_xattn_v_b': _L3_xattn_in['v_b'], 'L3_xattn_cproj_w': _L3_xattn_in['cproj_w'], 'L3_xattn_cproj_b': _L3_xattn_in['cproj_b'], 'L3_xattn_ln2_w': _L3_xattn_in['ln2_w'], 'L3_xattn_ln2_b': _L3_xattn_in['ln2_b'], 'L3_xattn_fc_w': _L3_xattn_in['fc_w'], 'L3_xattn_fc_b': _L3_xattn_in['fc_b'], 'L3_xattn_proj_w': _L3_xattn_in['proj_w'], 'L3_xattn_proj_b': _L3_xattn_in['proj_b']}

def reference(x, ctx_2048, mask_Bx1xSxS2_ff0, mask_BxS2_bf1, L0_xattn_Wq, L0_xattn_bq, L0_xattn_Wk, L0_xattn_bk, L0_xattn_Wv, L0_xattn_bv, L0_xattn_Wo, L0_xattn_bo, L0_xattn_gamma, L0_xattn_beta, L1_xattn_Wg, L1_xattn_bg, L1_xattn_Wtheta, L1_xattn_btheta, L1_xattn_Wphi, L1_xattn_bphi, L1_xattn_Wz, L1_xattn_bz, L1_xattn_gamma, L1_xattn_beta, L2_xattn_ln1_w, L2_xattn_ln1_b, L2_xattn_ln2_w, L2_xattn_ln2_b, L2_xattn_maa_x, L2_xattn_maa_w1, L2_xattn_maa_w2, L2_xattn_maa_stack, L2_xattn_time_decay, L2_xattn_td_w1, L2_xattn_td_w2, L2_xattn_u, L2_xattn_Wr, L2_xattn_Wk, L2_xattn_Wv, L2_xattn_Wg, L2_xattn_Wo, L2_xattn_gn_w, L2_xattn_gn_b, L2_xattn_ffn_maa_k, L2_xattn_ffn_maa_r, L2_xattn_Wfk, L2_xattn_Wfr, L2_xattn_Wfv, L3_xattn_ln1_w, L3_xattn_ln1_b, L3_xattn_q_w, L3_xattn_q_b, L3_xattn_k_w, L3_xattn_k_b, L3_xattn_v_w, L3_xattn_v_b, L3_xattn_cproj_w, L3_xattn_cproj_b, L3_xattn_ln2_w, L3_xattn_ln2_b, L3_xattn_fc_w, L3_xattn_fc_b, L3_xattn_proj_w, L3_xattn_proj_b):
    import jax
    import jax.numpy as jnp

    def _L0_xattn_ref(hidden_state, encoder_hidden_state, encoder_attention_mask, Wq, bq, Wk, bk, Wv, bv, Wo, bo, gamma, beta):
        import jax, jax.numpy as jnp
        import numpy as np
        H = 512
        NH = 32
        KVH = 8
        HD = H // NH
        GROUPS = NH // KVH
        EPS = 1e-06
        B, L, S = (4, 256, 256)

        def _gqa_forward(hidden_state, encoder_hidden_state, encoder_attention_mask, Wq, bq, Wk, bk, Wv, bv, Wo, bo, gamma, beta):
            b, l, _ = hidden_state.shape
            s = encoder_hidden_state.shape[1]
            q = hidden_state @ Wq + bq
            k = encoder_hidden_state @ Wk + bk
            v = encoder_hidden_state @ Wv + bv
            q = q.reshape(b, l, KVH, GROUPS, HD).transpose(0, 2, 3, 1, 4)
            k = k.reshape(b, s, KVH, HD).transpose(0, 2, 1, 3)
            v = v.reshape(b, s, KVH, HD).transpose(0, 2, 1, 3)
            scale = 1.0 / jnp.sqrt(jnp.asarray(HD, q.dtype))
            scores = jnp.einsum('bkgld,bksd->bkgls', q, k) * scale
            scores = scores + encoder_attention_mask[:, :, None, :, :]
            attn = jax.nn.softmax(scores, axis=-1)
            out = jnp.einsum('bkgls,bksd->bkgld', attn, v)
            out = out.transpose(0, 3, 1, 2, 4).reshape(b, l, H)
            out = out @ Wo + bo
            x = out + hidden_state
            mu = jnp.mean(x, axis=-1, keepdims=True)
            var = jnp.var(x, axis=-1, keepdims=True)
            return (x - mu) * jax.lax.rsqrt(var + EPS) * gamma + beta
        return _gqa_forward(hidden_state, encoder_hidden_state, encoder_attention_mask, Wq, bq, Wk, bk, Wv, bv, Wo, bo, gamma, beta)

    def _L1_xattn_ref(x_this, x_other, Wg, bg, Wtheta, btheta, Wphi, bphi, Wz, bz, gamma, beta):
        import jax, jax.numpy as jnp
        import numpy as np
        B, C, CI, T = (8, 128, 64, 512)
        EPS = 1e-05
        g_x = jnp.einsum('oc,bct->bto', Wg, x_this) + bg
        theta = jnp.einsum('oc,bct->bot', Wtheta, x_this) + btheta[None, :, None]
        phi = jnp.einsum('oc,bct->bot', Wphi, x_other) + bphi[None, :, None]
        f = jnp.einsum('bci,bcj->bij', phi, theta)
        f_div_C = jax.nn.softmax(f, axis=-1)
        y = jnp.einsum('bij,bjo->bio', f_div_C, g_x)
        w_y = jnp.einsum('oc,btc->bot', Wz, y) + bz[None, :, None]
        mean = jnp.mean(w_y, axis=(0, 2), keepdims=True)
        var = jnp.var(w_y, axis=(0, 2), keepdims=True)
        w_y = gamma[None, :, None] * (w_y - mean) * jax.lax.rsqrt(var + EPS) + beta[None, :, None]
        return w_y + x_this

    def _L2_xattn_ref(x, state, ln1_w, ln1_b, ln2_w, ln2_b, maa_x, maa_w1, maa_w2, maa_stack, time_decay, td_w1, td_w2, u, Wr, Wk, Wv, Wg, Wo, gn_w, gn_b, ffn_maa_k, ffn_maa_r, Wfk, Wfr, Wfv):
        import jax, jax.numpy as jnp
        import numpy as np
        E, H, L, B = (512, 32, 256, 4)
        S = E // H
        DM, DD = (32, 64)

        def _ln(x, w, b, eps=1e-05):
            m = x.mean(-1, keepdims=True)
            v = ((x - m) ** 2).mean(-1, keepdims=True)
            return (x - m) / jnp.sqrt(v + eps) * w + b

        def _block(x, state, ln1_w, ln1_b, ln2_w, ln2_b, maa_x, maa_w1, maa_w2, maa_stack, time_decay, td_w1, td_w2, u, Wr, Wk, Wv, Wg, Wo, gn_w, gn_b, ffn_maa_k, ffn_maa_r, Wfk, Wfr, Wfv):
            b, l, e = x.shape
            h = u.shape[0]
            s_ = e // h
            xa = _ln(x, ln1_w, ln1_b)
            sx = jnp.concatenate([state[:, 1:2] - xa[:, :1], xa[:, :-1] - xa[:, 1:]], axis=1)
            xxx = jnp.tanh((xa + sx * maa_x) @ maa_w1).reshape(b, l, 5, DM)
            xxx = jnp.einsum('blfd,fde->blfe', xxx, maa_w2)
            xm = xa[:, :, None] + sx[:, :, None] * (maa_stack + xxx)
            xk, xw, xv, xr, xg = (xm[:, :, j] for j in range(5))
            w = jnp.exp(-jnp.exp(time_decay + jnp.tanh(xw @ td_w1) @ td_w2)).reshape(b, l, h, s_)
            r = (xr @ Wr.T).reshape(b, l, h, s_)
            k = (xk @ Wk.T).reshape(b, l, h, s_)
            v = (xv @ Wv.T).reshape(b, l, h, s_)
            g = jax.nn.silu(xg @ Wg.T)
            s0 = state[:, 2:2 + s_].reshape(b, h, s_, s_)

            def step(s, rkvw):
                r_t, k_t, v_t, w_t = rkvw
                a = k_t[..., :, None] * v_t[..., None, :]
                out = jnp.einsum('bhi,bhij->bhj', r_t, u * a + s)
                s = a + w_t[..., :, None] * s
                return (s, out)
            rkvw = tuple((jnp.moveaxis(t, 1, 0) for t in (r, k, v, w)))
            _, out = jax.lax.scan(step, s0, rkvw)
            out = jnp.moveaxis(out, 0, 1).reshape(b, l, e)
            og = out.reshape(b, l, h, s_)
            m = og.mean(-1, keepdims=True)
            va = ((og - m) ** 2).mean(-1, keepdims=True)
            og = ((og - m) / jnp.sqrt(va + 1e-05)).reshape(b, l, e) * gn_w + gn_b
            x1 = x + og * g @ Wo.T
            xc = _ln(x1, ln2_w, ln2_b)
            sx2 = jnp.concatenate([state[:, 0:1] - xc[:, :1], xc[:, :-1] - xc[:, 1:]], axis=1)
            xk2 = xc + sx2 * ffn_maa_k
            xr2 = xc + sx2 * ffn_maa_r
            rr = jax.nn.sigmoid(xr2 @ Wfr.T)
            kk = jnp.square(jax.nn.relu(xk2 @ Wfk.T))
            return x1 + rr * (kk @ Wfv.T)
        return _block(x, state, ln1_w, ln1_b, ln2_w, ln2_b, maa_x, maa_w1, maa_w2, maa_stack, time_decay, td_w1, td_w2, u, Wr, Wk, Wv, Wg, Wo, gn_w, gn_b, ffn_maa_k, ffn_maa_r, Wfk, Wfr, Wfv)

    def _L3_xattn_ref(hidden_states, encoder_hidden_states, encoder_attention_mask, ln1_w, ln1_b, q_w, q_b, k_w, k_b, v_w, v_b, cproj_w, cproj_b, ln2_w, ln2_b, fc_w, fc_b, proj_w, proj_b):
        import jax, jax.numpy as jnp
        import numpy as np
        D = 512
        H = 16
        HD = D // H
        INNER = 4 * D
        EPS = 1e-05

        def layer_norm(x, w, b):
            mu = jnp.mean(x, axis=-1, keepdims=True)
            var = jnp.mean(jnp.square(x - mu), axis=-1, keepdims=True)
            return (x - mu) * jax.lax.rsqrt(var + EPS) * w + b
        B, LQ, _ = hidden_states.shape
        LK = encoder_hidden_states.shape[1]
        residual = hidden_states
        x = layer_norm(hidden_states, ln1_w, ln1_b)
        q = (x @ q_w + q_b).reshape(B, LQ, H, HD).transpose(0, 2, 1, 3)
        k = (encoder_hidden_states @ k_w + k_b).reshape(B, LK, H, HD).transpose(0, 2, 1, 3)
        v = (encoder_hidden_states @ v_w + v_b).reshape(B, LK, H, HD).transpose(0, 2, 1, 3)
        scale = 1.0 / np.sqrt(HD).astype(np.float32)
        scores = jnp.einsum('bhqd,bhkd->bhqk', q, k) * scale
        mask = encoder_attention_mask[:, None, None, :]
        mask_value = jnp.finfo(scores.dtype).min
        scores = jnp.where(mask, scores, mask_value)
        attn = jax.nn.softmax(scores, axis=-1)
        out = jnp.einsum('bhqk,bhkd->bhqd', attn, v)
        out = out.transpose(0, 2, 1, 3).reshape(B, LQ, D)
        out = out @ cproj_w + cproj_b
        hidden = out + residual
        residual = hidden
        y = layer_norm(hidden, ln2_w, ln2_b)
        y = jax.nn.gelu(y @ fc_w + fc_b, approximate=True)
        y = y @ proj_w + proj_b
        return residual + y
    x = _L0_xattn_ref(x, ctx_2048, mask_Bx1xSxS2_ff0, L0_xattn_Wq, L0_xattn_bq, L0_xattn_Wk, L0_xattn_bk, L0_xattn_Wv, L0_xattn_bv, L0_xattn_Wo, L0_xattn_bo, L0_xattn_gamma, L0_xattn_beta)
    x = _L1_xattn_ref(x, ctx_2048, L1_xattn_Wg, L1_xattn_bg, L1_xattn_Wtheta, L1_xattn_btheta, L1_xattn_Wphi, L1_xattn_bphi, L1_xattn_Wz, L1_xattn_bz, L1_xattn_gamma, L1_xattn_beta)
    x = _L2_xattn_ref(x, ctx_2048, L2_xattn_ln1_w, L2_xattn_ln1_b, L2_xattn_ln2_w, L2_xattn_ln2_b, L2_xattn_maa_x, L2_xattn_maa_w1, L2_xattn_maa_w2, L2_xattn_maa_stack, L2_xattn_time_decay, L2_xattn_td_w1, L2_xattn_td_w2, L2_xattn_u, L2_xattn_Wr, L2_xattn_Wk, L2_xattn_Wv, L2_xattn_Wg, L2_xattn_Wo, L2_xattn_gn_w, L2_xattn_gn_b, L2_xattn_ffn_maa_k, L2_xattn_ffn_maa_r, L2_xattn_Wfk, L2_xattn_Wfr, L2_xattn_Wfv)
    x = _L3_xattn_ref(x, ctx_2048, mask_BxS2_bf1, L3_xattn_ln1_w, L3_xattn_ln1_b, L3_xattn_q_w, L3_xattn_q_b, L3_xattn_k_w, L3_xattn_k_b, L3_xattn_v_w, L3_xattn_v_b, L3_xattn_cproj_w, L3_xattn_cproj_b, L3_xattn_ln2_w, L3_xattn_ln2_b, L3_xattn_fc_w, L3_xattn_fc_b, L3_xattn_proj_w, L3_xattn_proj_b)
    return x

_drawn_inputs = setup_inputs


def setup_inputs(seed=0):
    import zlib

    import numpy as np

    out = dict(_drawn_inputs(seed))
    spreads = {'L0_xattn_bq': (0.0, 0.8),
     'L0_xattn_bk': (0.0, 2.0),
     'L0_xattn_bv': (0.0, 0.1),
     'L0_xattn_bo': (0.0, 0.1),
     'L0_xattn_gamma': (1.0, 0.2),
     'L0_xattn_beta': (0.0, 0.1),
     'L1_xattn_bg': (0.0, 2.0),
     'L1_xattn_btheta': (0.0, 2.0),
     'L1_xattn_bphi': (0.0, 0.1),
     'L1_xattn_bz': (0.0, 2.0),
     'L2_xattn_ln1_w': (1.0, 0.2),
     'L2_xattn_ln1_b': (0.0, 0.5),
     'L2_xattn_ln2_w': (1.0, 0.6),
     'L2_xattn_ln2_b': (0.0, 0.8),
     'L2_xattn_gn_w': (1.0, 0.6),
     'L2_xattn_gn_b': (0.0, 0.8),
     'L3_xattn_ln1_w': (1.0, 0.6),
     'L3_xattn_ln1_b': (0.0, 0.8),
     'L3_xattn_q_b': (0.0, 0.8),
     'L3_xattn_k_b': (0.0, 2.0),
     'L3_xattn_v_b': (0.0, 0.303),
     'L3_xattn_cproj_b': (0.0, 0.1),
     'L3_xattn_ln2_w': (1.0, 0.542),
     'L3_xattn_ln2_b': (0.0, 0.575),
     'L3_xattn_fc_b': (0.0, 0.271),
     'L3_xattn_proj_b': (0.0, 0.1)}
    factors = {'L0_xattn_Wq': 3.794,
     'L0_xattn_Wk': 3.82,
     'L2_xattn_maa_x': 8.0,
     'L2_xattn_maa_w1': 5.133,
     'L2_xattn_maa_w2': 5.14,
     'L2_xattn_td_w1': 8.0,
     'L2_xattn_td_w2': 8.0,
     'L2_xattn_u': 5.228,
     'L2_xattn_ffn_maa_k': 8.0,
     'L2_xattn_ffn_maa_r': 8.0,
     'L2_xattn_Wfr': 6.682,
     'L3_xattn_q_w': 8.0,
     'L3_xattn_k_w': 8.0}
    for name, (base, spread) in spreads.items():
        noise = np.random.default_rng([zlib.crc32(name.encode()), seed]).standard_normal(out[name].shape)
        drawn = base * np.exp(spread * noise) if base else spread * noise
        out[name] = jnp.asarray(drawn.astype(out[name].dtype))
    for name, factor in factors.items():
        out[name] = (out[name] * factor).astype(out[name].dtype)
    return out
```

```python
from contextlib import ExitStack

import numpy as np

import concourse.bass as bass
from concourse import mybir

F32 = mybir.dt.float32
U8 = mybir.dt.uint8
ALU = mybir.AluOpType
ACT = mybir.ActivationFunctionType
AX = mybir.AxisListType

B, T, D = 32, 128, 512
P = 128
KC = D // P
G = 4
NG = B // G
TOK = G * T
RING = 4
FMAX = 3.4028234663852886e38

VECS = ["L0_xattn_bq", "L2_xattn_ln1_w", "L2_xattn_ln1_b", "L2_xattn_ln2_w", "L2_xattn_ln2_b", "L2_xattn_maa_x",
        "L2_xattn_time_decay", "L2_xattn_u", "L2_xattn_gn_w", "L2_xattn_gn_b", "L2_xattn_ffn_maa_k",
        "L2_xattn_ffn_maa_r", "L3_xattn_ln1_w", "L3_xattn_ln1_b", "L3_xattn_q_b", "L3_xattn_k_b",
        "L3_xattn_ln2_w", "L3_xattn_ln2_b", "L3_xattn_fc_b", "L2_xattn_maa_stack"]
ROWS_A = ["L0_xattn_bo", "L0_xattn_gamma", "L0_xattn_beta", "L0_xattn_bv", "L1_xattn_bg"]
ROWS_C = ["L3_xattn_v_b", "L3_xattn_cproj_b", "L3_xattn_proj_b"]


class Signal:

    def __init__(self, sem, per):
        self.sem, self.per, self.seen = sem, per, 0

    def up(self, n=1):
        self.seen += n
        return self.sem, n

    def __call__(self, turn, k):
        return self.sem, turn * self.per + (self.per + k)

    def last(self, turn):
        return self(turn, self.seen)

    def before(self, turn, k=None):
        return self.sem, turn * self.per + (self.per if k is None else k)


class Ring:

    def __init__(self, items, filled, emptied):
        assert len(items) % RING == 0, len(items)
        self.at = {name: n for n, (name, _) in enumerate(items)}
        self.who = [who for _, who in items]
        self.filled, self.emptied = filled, emptied
        self.nth = [self.who[:n + 1].count(w) for n, w in enumerate(self.who)]

    def bank(self, *name):
        return self.at[name] % RING

    def ready(self, turn, name, moved=()):
        n = self.at[name] - RING
        last = {self.who[n]: self.nth[n] if n >= 0 else self.nth[n] - self.emptied[self.who[n]].per}
        for other in moved:
            n = self.at[other]
            last[self.who[n]] = max(last.get(self.who[n], 0), self.nth[n])
        return [self.emptied[w](turn, k) for w, k in last.items()]

    def full(self, turn, *name):
        return self.filled(turn, self.at[name] + 1)

    def full_before(self, turn, *name):
        return self.filled.before(turn, self.at[name] + 1)

    def out(self, turn, *name):
        n = self.at[name]
        return self.emptied[self.who[n]](turn, self.nth[n])


def vec_column(name):
    at = VECS.index(name)
    wide = VECS.index("L3_xattn_fc_b")
    return KC * at if at <= wide else KC * wide + 4 * D // P


def phase_a(nc, dram, stats):
    NH, KVH, HD = 32, 8, 16
    RH = NH // 2
    HV = HD + 1
    NR = 2 * G
    CI = 64
    items = []
    for c in range(KC):
        items += [(("xT", c), "act"), (("cT", c), "dve")]
    items += [(("q", c), "act") for c in range(KC)] + [(("k", c), "dve") for c in range(KC)]
    items += [(("v", g), "dve") for g in range(G)]
    for n in range(NR):
        items += [(("pT", n, b), "act" if b % 2 else "dve") for b in range(4)] + [(("pv", n), "dve")]
        if n >= 2 and n % 2 == 0:
            items += [(("aT", n // 2 - 1), "act"), (("o", n // 2 - 1), "dve")]
    items += [(("aT", G - 1), "act"), (("o", G - 1), "dve")]
    for g in range(G):
        items += [(("phi", g), "act"), (("th", g), "act"), (("gx", g), "dve")]
    for g in range(G):
        items += [(("fT", g, j), "act" if j % 2 else "dve") for j in range(4)] + [(("y", g), "act"), (("wy", g), "act")]

    with ExitStack() as ctx:
        def sb(name, shape, dt=F32):
            return ctx.enter_context(nc.sbuf_tensor("a_" + name, shape, dt))

        def sig(name, per):
            return Signal(ctx.enter_context(nc.semaphore("a_" + name)), per)

        wq, wo = sb("wq", [P, KC, D]), sb("wo", [P, KC, D])
        wk, wv = sb("wk", [P, KC, 128]), sb("wv", [P, KC, 128])
        wkr = sb("wkr", [P, KC, D])
        wgT, wthT, wphT = sb("wgT", [P, CI]), sb("wthT", [P, CI]), sb("wphT", [P, CI])
        wzT = sb("wzT", [CI, P])
        vec = sb("vec", [P, KC])
        bk = sb("bk", [P, KC])
        ci = sb("ci", [CI, 2])
        bz = sb("bz", [P, 1])
        rows = sb("rows", [P, 3 * D + 128 + CI])
        parity, ident = sb("parity", [P, 2]), sb("ident", [P, P])
        bo, gamma, beta = rows[:, 0:D], rows[:, D:2 * D], rows[:, 2 * D:3 * D]
        bv, bg = rows[:, 3 * D:3 * D + 128], rows[:, 3 * D + 128:]
        half = sb("half", [P, 1])

        x, c_tm, mask = sb("x", [P, G, D]), sb("c", [P, G, D]), sb("mask", [P, G, T])
        xT, cT, qT = sb("xT", [P, KC, TOK]), sb("cT", [P, KC, TOK]), sb("qT", [P, KC, TOK])
        kexp = sb("kexp", [P, KC, 2, TOK])
        v_ext = sb("v_ext", [P, G, KVH, HV])
        S = sb("S", [P, 2, RH, T])
        probsT = sb("probsT", [P, 2, RH, T])
        smax, rden = sb("smax", [P, 2, RH]), sb("rden", [P, 2, RH])
        att, attT = sb("att", [P, 2, D]), sb("attT", [P, KC, TOK])
        xbo, x1 = sb("xbo", [P, G, D]), sb("x1", [P, G, D])
        bn, mv = sb("bn", [P, 6]), sb("mv", [P, 2])
        veps, rstd = sb("veps", [P, 1]), sb("rstd", [P, 1])
        phi, theta = sb("phi", [CI, G, D]), sb("theta", [CI, G, D])
        gx = sb("gx", [P, G, KC, CI])
        nmax, fsum = sb("nmax", [P, 2, KC]), sb("fsum", [P, 2, KC])
        yT, wy = sb("yT", [CI, 2, D]), sb("wy", [P, 2, D])
        f_sb = S[:, :, :, :].rearrange("p a (i k) t -> p a i (k t)", i=KC)
        fT = probsT[:, :, :, :].rearrange("p a (i k) t -> p a i (k t)", i=KC)
        pS = ctx.enter_context(nc.psum_tensor("a_pS", [P, 4, 512], F32))
        pR = ctx.enter_context(nc.psum_tensor("a_pR", [P, RING, 512], F32))

        loaded_w = sig("loaded_w", 0)
        x_loaded, c_loaded, mask_loaded = sig("x_loaded", 16), sig("c_loaded", 16), sig("mask_loaded", 16)
        x1_stored, wy_stored = sig("x1_stored", 16 * G), [sig("wy_stored%d" % i, 16 * G // 2) for i in range(2)]
        filled = sig("filled", len(items))
        emptied = {w: sig("emptied_" + w, [i[1] for i in items].count(w)) for w in ("act", "dve")}
        ring = Ring(items, filled, emptied)
        ones_set, wk_wide = sig("ones_set", 0), sig("wk_wide", 0)
        scored, masked = sig("scored", NR + G), sig("masked", NR)
        max_found, centred, exp_done = sig("max_found", NR), sig("centred", NR), sig("exp_done", NR)
        xbo_ready, var_ready, rstd_ready = sig("xbo_ready", 1), sig("var_ready", G), sig("rstd_ready", G)
        whitened, x1_ready = sig("whitened", G), sig("x1_ready", G)
        f_max, f_exp, f_scaled, y_stats = sig("f_max", G), sig("f_exp", G), sig("f_scaled", G), sig("y_stats", G)
        held = sig("held", 0)
        dve_step, pool_step = sig("dve_step", 24), sig("pool_step", G)
        signals = [s for s in locals().values() if isinstance(s, Signal)] + list(emptied.values()) + wy_stored
        x_v, c_v = dram["x"].rearrange("b t d -> t b d"), dram["ctx_2048"].rearrange("b t d -> t b d")
        m_v = dram["mask_Bx1xSxS2_ff0"].rearrange("b o l s -> l (b o) s")
        block = ctx.enter_context(nc.Block())

        @block.sync
        def _(sp):
            for s in signals:
                if s.per:
                    sp.sem_inc(s.sem, s.per)
            w3 = [(wq, "L0_xattn_Wq"), (wk, "L0_xattn_Wk"), (wv, "L0_xattn_Wv"), (wo, "L0_xattn_Wo")]
            for tile, name in w3:
                sp.dma_start(tile[:, :, :], dram[name].rearrange("(k p) n -> p k n", p=P)).then_inc(*loaded_w.up(16))
            for tile, name in [(wgT, "L1_WgT"), (wthT, "L1_WthetaT"), (wphT, "L1_WphiT"), (wzT, "L1_WzT"), (bk, "bk_wide"),
                               (ci, "L1_ci"), (bz, "L1_bz"), (rows, "rows_a"), (parity, "parity"), (ident, "ident")]:
                sp.dma_start(tile[:, :], dram[name]).then_inc(*loaded_w.up(16))
            sp.dma_start(vec[:, :], dram["vecs"][:, 0:KC]).then_inc(*loaded_w.up(16))
            with sp.Fori(0, NG) as turn:
    
                sp.wait_ge(*xbo_ready.before(turn))
                sp.sem_inc(held.sem, 1)
                sp.dma_start(x[:, :, :], x_v[:, bass.ds(turn * G, G), :]).then_inc(*x_loaded.up(16))
                sp.wait_ge(*ring.full_before(turn, "phi", G - 1))
                sp.sem_inc(held.sem, 1)
                sp.dma_start(c_tm[:, :, :], c_v[:, bass.ds(turn * G, G), :]).then_inc(*c_loaded.up(16))
                sp.wait_ge(*masked.before(turn))
                sp.sem_inc(held.sem, 1)
                sp.dma_start(mask[:, :, :], m_v[:, bass.ds(turn * G, G), :]).then_inc(*mask_loaded.up(16))
                for g in range(G):
                    sp.wait_ge(*x1_ready(turn, g + 1))
                    sp.sem_inc(held.sem, 1)
                    sp.dma_start(dram["x1"][bass.ds(turn * G + g, 1), :, :].rearrange("b t d -> t (b d)"),
                                 x1[:, g, :]).then_inc(*x1_stored.up(16))
                for g in range(G):
                    sp.wait_ge(*ring.out(turn, "wy", g))
                    sp.sem_inc(held.sem, 1)
                    sp.dma_start(dram["wy"][bass.ds(turn * G + g, 1), :, :].rearrange("b t d -> t (b d)"),
                                 wy[:, g % 2, :]).then_inc(*wy_stored[g % 2].up(16))
            sp.wait_ge(*x1_stored(NG - 1, 16 * G))
            for half_stored in wy_stored:
                sp.wait_ge(*half_stored(NG - 1, 16 * G // 2))

        def fill(pe, turn, *name, moved=()):
            for wait in ring.ready(turn, name, moved):
                pe.wait_ge(*wait)
            return pR[:, ring.bank(*name), :]

        def post_attention_pe(pe, turn, g):
            bank = fill(pe, turn, "aT", g, moved=[("pv", 2 * g + 1)])
            for c in range(KC):
                mm = nc.tensor.transpose(bank[:, c * P:c * P + P], att[:, g % 2, c * P:c * P + P], ident[:, :])
            mm.then_inc(*filled.up())
            bank = fill(pe, turn, "o", g, moved=[("aT", g)])
            for c in range(KC):
                mm = nc.tensor.matmul(bank[:, :], attT[:, c, g * T:g * T + T], wo[:, c, :], start=(c == 0), stop=(c == KC - 1))
            mm.then_inc(*filled.up())

        @block.tensor
        def _(pe):
            pe.wait_ge(loaded_w.sem, loaded_w.seen)
            pe.wait_ge(wk_wide.sem, KC)

            def scores(turn, n):
                g, half_ = n // 2, n % 2
                if n:
                    pe.wait_ge(*masked(turn, n))
                else:
                    pe.wait_ge(*f_exp.before(turn))
                for cc in range(2):
                    c = 2 * half_ + cc
                    for r in range(4):
                        rows_ = slice(32 * r, 32 * r + 32)
                        mm = nc.tensor.matmul(pS[:, r, cc * 256:cc * 256 + 256].rearrange("p (a t) -> p a t", a=2), qT[rows_, c, g * T:g * T + T],
                                              kexp[rows_, c, :, g * T:g * T + T], start=True, stop=True)
                mm.then_inc(*scored.up())

            with pe.Fori(0, NG) as turn:
                for c in range(KC):
                    for name, src, ld in (("xT", x, x_loaded), ("cT", c_tm, c_loaded)):
                        bank = fill(pe, turn, name, c)
                        pe.wait_ge(*ld(turn, 16))
                        for g in range(G):
                            mm = nc.tensor.transpose(bank[:, g * T:g * T + T], src[:, g, c * P:c * P + P], ident[:, :])
                        mm.then_inc(*filled.up())
                for name, w, src, ready in (("q", wq, xT, "xT"), ("k", wkr, cT, "cT")):
                    for m in range(KC):
                        bank = fill(pe, turn, name, m, moved=[(ready, KC - 1)])
                        for c in range(KC):
                            mm = nc.tensor.matmul(bank[:, :], w[:, c, m * P:m * P + P], src[:, c, :],
                                                  start=(c == 0), stop=(c == KC - 1))
                        mm.then_inc(*filled.up())
                for g in range(G):
                    bank = fill(pe, turn, "v", g)
                    for c in range(KC):
                        mm = nc.tensor.matmul(bank[:, 0:P], cT[:, c, g * T:g * T + T], wv[:, c, :],
                                              start=(c == 0), stop=(c == KC - 1))
                    mm.then_inc(*filled.up())
                pe.wait_ge(*ring.out(turn, "q", KC - 1))
                pe.wait_ge(*ring.out(turn, "v", G - 1))
                scores(turn, 0)
                for n in range(NR):
                    g = n // 2
                    if n + 1 < NR:
                        scores(turn, n + 1)
                    pe.wait_ge(*exp_done(turn, n + 1))
                    for b in range(4):
                        bank = fill(pe, turn, "pT", n, b)
                        for i in range(4):
                            mm = nc.tensor.transpose(bank[:, i * T:i * T + T], S[:, n % 2, 4 * b + i, :], ident[:, :])
                        mm.then_inc(*filled.up())
                    bank = fill(pe, turn, "pv", n, moved=[("pT", n, b) for b in range(4)])
                    for b in range(4):
                        for cc in range(2):
                            for par in range(2):
                                h = cc * 8 + 2 * b + par
                                kv = (n % 2 * RH + h) // (NH // KVH)
                                mm = nc.tensor.matmul(bank[:, h * HV:h * HV + HV], probsT[:, n % 2, 4 * b + 2 * cc + par, :],
                                                      v_ext[:, g, kv, :], start=True, stop=True)
                    mm.then_inc(*filled.up())
                    if n >= 2 and n % 2 == 0:
                        post_attention_pe(pe, turn, n // 2 - 1)
                post_attention_pe(pe, turn, G - 1)

                for g in range(G):
                    bank = fill(pe, turn, "phi", g)
                    nc.tensor.matmul(bank[0:CI, :], wphT[:, :], c_tm[:, g, :], start=True, stop=True).then_inc(*filled.up())
                    bank = fill(pe, turn, "th", g)
                    pe.wait_ge(*x1_ready(turn, g + 1))
                    nc.tensor.matmul(bank[0:CI, :], wthT[:, :], x1[:, g, :], start=True, stop=True).then_inc(*filled.up())
                    bank = fill(pe, turn, "gx", g)
                    for j in range(KC):
                        mm = nc.tensor.matmul(bank[:, j * CI:j * CI + CI], x1[:, g, j * P:j * P + P], wgT[:, :],
                                              start=True, stop=True)
                    mm.then_inc(*filled.up())

                def affinity(g):
                    if g:
                        pe.wait_ge(*f_exp(turn, g))
                    else:
                        pe.wait_ge(*masked(turn, NR))
                    pe.wait_ge(*ring.out(turn, "th", g))
                    for i in range(KC):
                        mm = nc.tensor.matmul(pS[:, i, :], phi[:, g, i * P:i * P + P], theta[:, g, :], start=True, stop=True)
                    mm.then_inc(*scored.up())

                affinity(0)
                for g in range(G):
                    if g + 1 < G:
                        affinity(g + 1)
                    pe.wait_ge(*f_scaled(turn, g + 1))
                    for j in range(KC):
                        bank = fill(pe, turn, "fT", g, j)
                        for i in range(KC):
                            mm = nc.tensor.transpose(bank[:, i * P:i * P + P], f_sb[:, g % 2, i, j * P:j * P + P], ident[:, :])
                        mm.then_inc(*filled.up())
                    bank = fill(pe, turn, "y", g, moved=[("gx", g)] + [("fT", g, j) for j in range(KC)])
                    for j in range(KC):
                        mm = nc.tensor.matmul(bank[0:CI, :], gx[:, g, j, :], fT[:, g % 2, j, :], start=(j == 0), stop=(j == KC - 1))
                    mm.then_inc(*filled.up())
                    bank = fill(pe, turn, "wy", g, moved=[("y", g)])
                    nc.tensor.matmul(bank[:, :], wzT[:, :], yT[:, g % 2, :], start=True, stop=True).then_inc(*filled.up())

        @block.scalar
        def _(act):
            act.wait_ge(loaded_w.sem, loaded_w.seen)

            def take(turn, *name):
                act.wait_ge(*ring.full(turn, *name))
                return pR[:, ring.bank(*name), :]

            def exp_round(turn, n):
                act.wait_ge(*centred(turn, n + 1))
                nc.scalar.activation(S[:, n % 2, :, :], S[:, n % 2, :, :], ACT.Exp).then_inc(*exp_done.up())

            def turn_att(turn, g):
                bank = take(turn, "aT", g)
                nc.scalar.activation(attT[:, :, g * T:g * T + T], bank[:, :].rearrange("p (k t) -> p k t", k=KC), ACT.Copy)\
                    .then_inc(*emptied["act"].up())

            with act.Fori(0, NG) as turn:
                for c in range(KC):
                    bank = take(turn, "xT", c)
                    nc.scalar.activation(xT[:, c, :], bank, ACT.Copy).then_inc(*emptied["act"].up())
                act.wait_ge(*scored.before(turn, NR))
                for c in range(KC):
                    bank = take(turn, "q", c)
                    nc.scalar.activation(qT[:, c, :], bank, ACT.Identity, bias=vec[:, c:c + 1]).then_inc(*emptied["act"].up())
                exp_round(turn, 0)
                for n in range(NR):
                    if n + 1 < NR:
                        exp_round(turn, n + 1)
                    for b in (1, 3):
                        bank = take(turn, "pT", n, b)
                        nc.scalar.activation(probsT[:, n % 2, 4 * b:4 * b + 4, :], bank.rearrange("p (h t) -> p h t", h=4), ACT.Copy)\
                            .then_inc(*emptied["act"].up())
                    if n >= 2 and n % 2 == 0:
                        turn_att(turn, n // 2 - 1)
                turn_att(turn, G - 1)
                act.wait_ge(*scored.before(turn, NR + G))
                for g in range(G):
                    bank = take(turn, "phi", g)
                    nc.scalar.activation(phi[:, g, :], bank[0:CI, :], ACT.Identity, bias=ci[:, 0:1]).then_inc(*emptied["act"].up())
                    bank = take(turn, "th", g)
                    nc.scalar.activation(theta[:, g, :], bank[0:CI, :], ACT.Identity, bias=ci[:, 1:2]).then_inc(*emptied["act"].up())

                def exp_f(g):
                    act.wait_ge(*f_max(turn, g + 1))
                    if g >= 2:
                        act.wait_ge(*ring.full(turn, "fT", g - 2, KC - 1))
                    else:
                        act.wait_ge(*ring.full(turn, "pT", NR - 1, 3))
                    for i in range(KC):
                        ins = nc.scalar.activation(f_sb[:, g % 2, i, :], pS[:, i, :], ACT.Exp, bias=nmax[:, g % 2, i:i + 1],
                                                   accum_out=fsum[:, g % 2, i:i + 1])
                    ins.then_inc(*f_exp.up())

                exp_f(0)
                for g in range(G):
                    if g + 1 < G:
                        exp_f(g + 1)
                    for j in (1, 3):
                        bank = take(turn, "fT", g, j)
                        nc.scalar.activation(fT[:, g % 2, j, :], bank, ACT.Copy).then_inc(*emptied["act"].up())
                    bank = take(turn, "y", g)
                    nc.scalar.activation(yT[:, g % 2, :], bank[0:CI, :], ACT.Copy).then_inc(*emptied["act"].up())
                    bank = take(turn, "wy", g)
                    if g >= 2:
                        act.wait_ge(*wy_stored[g % 2](turn, 16))
                        act.wait_ge(*y_stats(turn, g - 1))
                    else:
                        act.wait_ge(*wy_stored[g % 2].before(turn))
                        act.wait_ge(*y_stats.before(turn))
                    nc.scalar.activation(wy[:, g % 2, :], bank, ACT.Identity, bias=bz[:, 0:1]).then_inc(*emptied["act"].up())

        @block.vector
        def _(dve):
            dve.wait_ge(loaded_w.sem, loaded_w.seen)
            nc.vector.memset(v_ext[:, :, :, HD:HV], 1.0).then_inc(*ones_set.up())
            nc.vector.memset(half[:, :], -0.5).then_inc(*ones_set.up())
            for c in range(KC):
                src = wk[:, c, :].rearrange("p (v d) -> p v d", v=KVH).unsqueeze(2).to_broadcast([P, KVH, NH // KVH, HD])
                nc.vector.tensor_copy(wkr[:, c, :].rearrange("p (v g d) -> p v g d", v=KVH, d=HD), src).then_inc(*wk_wide.up())

            def take(turn, *name):
                dve.wait_ge(*ring.full(turn, *name))
                return pR[:, ring.bank(*name), :]

            def softmax_max(turn, n):
                dve.wait_ge(*scored(turn, n + 1))
                if n >= 2:
                    dve.wait_ge(*ring.full(turn, "pT", n - 2, 3))
                else:
                    dve.wait_ge(*ring.full_before(turn, "fT", G - 1, KC - 1))
                nc.vector.scalar_tensor_tensor(out=S[:, n % 2, :, :], in0=pS[:, :, :].rearrange("p r (h t) -> p (r h) t", t=T),
                                               scalar=float(HD) ** -0.5, in1=mask[:, n // 2:n // 2 + 1, :].to_broadcast([P, RH, T]),
                                               op0=ALU.mult, op1=ALU.add).then_inc(*masked.up())
                dve.wait_ge(*masked(turn, n + 1))
                if n >= 2:
                    dve.wait_ge(*centred(turn, n - 1))
                nc.vector.tensor_reduce(smax[:, n % 2, :], S[:, n % 2, :, :], AX.X, ALU.max).then_inc(*max_found.up())

            def normalise(turn, n):
                bank = take(turn, "pv", n)[:, 0:RH * HV].rearrange("p (h e) -> p h e", e=HV)
                nc.vector.reciprocal(rden[:, n % 2, :].unsqueeze(2), bank[:, :, HD:HV]).then_inc(*dve_step.up())
                dve.wait_ge(*dve_step.last(turn))
                nc.vector.tensor_tensor(att[:, n // 2 % 2, n % 2 * 256:n % 2 * 256 + 256].rearrange("p (h d) -> p h d", d=HD),
                                        bank[:, :, 0:HD], rden[:, n % 2, :].unsqueeze(2).to_broadcast([P, RH, HD]), ALU.mult)\
                    .then_inc(*emptied["dve"].up())

            def norm_out(turn, g):
                if g == 0:
                    dve.wait_ge(*xbo_ready(turn, 1))
                bank = take(turn, "o", g)
                nc.vector.tensor_tensor(xbo[:, g, :], bank, xbo[:, g, :], ALU.add).then_inc(*emptied["dve"].up())
                dve.wait_ge(*ring.out(turn, "o", g))
                nc.vector.bn_stats(bn[:, :], xbo[:, g, :]).then_inc(*dve_step.up())
                dve.wait_ge(*dve_step.last(turn))
                dve.sem_inc(held.sem, 1)
                nc.vector.bn_aggr(mv[:, :], bn[:, :]).then_inc(*dve_step.up())
                dve.wait_ge(*dve_step.last(turn))
                nc.vector.tensor_scalar(veps[:, :], mv[:, 1:2], 1e-6, None, ALU.add).then_inc(*var_ready.up())
                dve.wait_ge(*rstd_ready(turn, g + 1))
                nc.vector.tensor_scalar(xbo[:, g, :], xbo[:, g, :], mv[:, 0:1], rstd[:, 0:1], ALU.subtract, ALU.mult)\
                    .then_inc(*whitened.up())

            dve.wait_ge(ones_set.sem, 2)
            with dve.Fori(0, NG) as turn:
                for c in range(KC):
                    bank = take(turn, "cT", c)
                    nc.vector.tensor_copy(cT[:, c, :], bank).then_inc(*emptied["dve"].up())
                dve.wait_ge(*scored.before(turn, NR))
                for c in range(KC):
                    bank = take(turn, "k", c)
                    nc.vector.tensor_scalar(kexp[:, c, 0, :], bank, bk[:, c:c + 1], parity[:, 0:1], ALU.add, ALU.mult)\
                        .then_inc(*dve_step.up())
                    nc.vector.tensor_scalar(kexp[:, c, 1, :], bank, bk[:, c:c + 1], parity[:, 1:2], ALU.add, ALU.mult)\
                        .then_inc(*emptied["dve"].up())
                for g in range(G):
                    bank = take(turn, "v", g)
                    nc.vector.tensor_tensor(v_ext[:, g, :, 0:HD], bank[:, 0:P].rearrange("p (v d) -> p v d", d=HD),
                                            bv.rearrange("p (v d) -> p v d", d=HD), ALU.add).then_inc(*emptied["dve"].up())
                dve.wait_ge(*mask_loaded(turn, 16))
                softmax_max(turn, 0)
                for n in range(NR):
                    if n + 1 < NR:
                        softmax_max(turn, n + 1)
                    for b in (0, 2):
                        bank = take(turn, "pT", n, b)
                        nc.vector.tensor_copy(probsT[:, n % 2, 4 * b:4 * b + 4, :], bank.rearrange("p (h t) -> p h t", h=4))\
                            .then_inc(*emptied["dve"].up())
                    normalise(turn, n)
                    if n >= 2 and n % 2 == 0:
                        norm_out(turn, n // 2 - 1)
                norm_out(turn, G - 1)
                for g in range(G):
                    bank = take(turn, "gx", g)
                    nc.vector.tensor_tensor(gx[:, g, :, :], bank[:, 0:KC * CI].rearrange("p (j o) -> p j o", o=CI),
                                            bg.unsqueeze(1).to_broadcast([P, KC, CI]), ALU.add).then_inc(*emptied["dve"].up())

                def affinity_max(g):
                    dve.wait_ge(*scored(turn, NR + g + 1))
                    nc.vector.tensor_reduce(nmax[:, g % 2, :], pS[:, :, :], AX.X, ALU.max, negate=True).then_inc(*f_max.up())

                affinity_max(0)
                for g in range(G):
                    if g + 1 < G:
                        affinity_max(g + 1)
                    dve.wait_ge(*f_exp(turn, g + 1))
                    nc.vector.reciprocal(rden[:, g % 2, 0:KC], fsum[:, g % 2, :]).then_inc(*dve_step.up())
                    dve.wait_ge(*dve_step.last(turn))
                    for i in range(KC):
                        ins = nc.vector.tensor_scalar(f_sb[:, g % 2, i, :], f_sb[:, g % 2, i, :], rden[:, g % 2, i:i + 1], None, ALU.mult)
                    ins.then_inc(*f_scaled.up())
                    for j in (0, 2):
                        bank = take(turn, "fT", g, j)
                        nc.vector.tensor_copy(fT[:, g % 2, j, :], bank).then_inc(*emptied["dve"].up())
                    dve.wait_ge(*ring.out(turn, "wy", g))
                    nc.vector.bn_stats(stats[:, bass.ds(turn * (G * 6) + g * 6, 6)], wy[:, g % 2, :]).then_inc(*y_stats.up())

        @block.gpsimd
        def _(pool):
            pool.wait_ge(loaded_w.sem, loaded_w.seen)
            pool.wait_ge(ones_set.sem, 2)
            with pool.Fori(0, NG) as turn:
                pool.wait_ge(*ring.full(turn, "xT", KC - 1))
                pool.wait_ge(*x1_ready.before(turn))
                nc.gpsimd.tensor_tensor(xbo[:, :, :], x[:, :, :], bo.unsqueeze(1).to_broadcast([P, G, D]), ALU.add).then_inc(*xbo_ready.up())

                def centre(n):
                    pool.wait_ge(*max_found(turn, n + 1))
                    nc.gpsimd.tensor_tensor(S[:, n % 2, :, :], S[:, n % 2, :, :],
                                            smax[:, n % 2, :].unsqueeze(2).to_broadcast([P, RH, T]), ALU.subtract).then_inc(*centred.up())

                def finish(g):
                    pool.wait_ge(*var_ready(turn, g + 1))
                    nc.gpsimd.tensor_tensor(rstd[:, :], veps[:, :], half[:, :], ALU.pow).then_inc(*rstd_ready.up())
                    if g == 0:
                        pool.wait_ge(*x1_stored.before(turn))
                        pool.wait_ge(*ring.full_before(turn, "gx", G - 1))
                    pool.wait_ge(*whitened(turn, g + 1))
                    nc.gpsimd.tensor_tensor(xbo[:, g, :], xbo[:, g, :], gamma, ALU.mult).then_inc(*pool_step.up())
                    pool.wait_ge(*pool_step.last(turn))
                    nc.gpsimd.tensor_tensor(x1[:, g, :], xbo[:, g, :], beta, ALU.add).then_inc(*x1_ready.up())

                centre(0)
                for n in range(NR):
                    if n + 1 < NR:
                        centre(n + 1)
                    if n >= 2 and n % 2 == 0:
                        finish(n // 2 - 1)
                finish(G - 1)

        wrong = {s.sem.name: (s.per, s.seen) for s in signals if s.per and s.per != s.seen}
        assert not wrong, wrong



def phase_b(nc, dram, norm):
    NH, HD = 32, 16
    HC = P // HD
    DM, DD = 32, 64
    LORA = ["k", "w", "v", "r", "g"]
    items = [(("n1", c), "act") for c in range(KC)] + [(("h0",), "act"), (("h1",), "act")]
    items += [(("m", 0, c), "dve") for c in range(KC)]
    for j, name in enumerate(LORA):
        if j + 1 < len(LORA):
            items += [(("m", j + 1, c), "dve") for c in range(KC)]
        if name == "w":
            items += [(("td1",), "act")]
        items += [((name, c), "dve" if name == "g" else "act") for c in range(KC)]
        if name == "v":
            items += [(("vt", g), "act") for g in range(G)]
    items += [(("vb", n), "dve") for n in range(KC * HD)]
    items += [(("u",), "dve")]
    items += [(("gn", c), "act") for c in range(KC)] + [(("o", g), "dve") for g in range(G)]
    items += [(("n2", c), "act") for c in range(KC)]
    items += [(("fk", c), "act") for c in range(KC)] + [(("fr", g), "act") for g in range(G)]
    items += [(("fv", g), "dve") for g in range(G)]

    with ExitStack() as ctx:
        def sb(name, shape, dt=F32):
            return ctx.enter_context(nc.sbuf_tensor("b_" + name, shape, dt))

        def sig(name, per):
            return Signal(ctx.enter_context(nc.semaphore("b_" + name)), per)

        W = {n: sb("w" + n, [P, KC, D]) for n in ("Wk", "Wv", "Wr", "Wg", "Wo", "Wfk", "Wfr", "Wfv")}
        w1, w2a, w2b = sb("w1", [P, KC, 5 * DM]), sb("w2a", [P, D]), sb("w2b", [DM, D])
        td1, td2 = sb("td1", [P, KC, DD]), sb("td2", [DD, D])
        vec = sb("vec", [P, dram["vecs"].shape[1]])
        ident, pick, heads = sb("ident", [P, P]), sb("pick", [P, HD, P]), sb("heads", [P, HC])
        half = sb("half", [P, G * NH])

        def col(name, c, j=0):
            at = vec_column(name) + KC * j + c
            return vec[:, at:at + 1]

        x1g, x2, xn = sb("x1g", [P, G, D]), sb("x2", [P, G, D]), sb("xn", [P, G, D])
        wyg = xn
        xT, sx = sb("xT", [P, KC, G, T + 1]), sb("sx", [P, KC, TOK])
        xm = [sb("xm0", [P, KC, TOK]), sb("xm1", [P, KC, TOK])]
        kT, wT, vT, rT, gT = (sb(n, [P, KC, TOK]) for n in ("kT", "wT", "vT", "rT", "gT"))
        v_tm = sb("v_tm", [P, G, D])
        hid, hid4 = sb("hid", [P, TOK]), sb("hid4", [DM, TOK])
        prev, s0 = sb("prev", [P, G, 2, KC]), sb("s0", [P, KC, G, HD])
        a_kv, S, rs = sb("a_kv", [P, 2, TOK]), sb("S", [P, 2, G, T + 1]), sb("rs", [P, 2, TOK])
        bn, mv = sb("bn", [P, G, 6]), sb("mv", [P, G, 2])
        veps, rstd = sb("veps", [P, G]), sb("rstd", [P, G])
        gsum, gvar, grstd = sb("gsum", [P, G, NH]), sb("gvar", [P, G, NH]), sb("grstd", [P, G, NH])
        pO = ctx.enter_context(nc.psum_tensor("b_pO", [P, G, 512], F32))
        pR = ctx.enter_context(nc.psum_tensor("b_pR", [P, RING, 512], F32))
        th = a_kv[0:DD, 0, :]
        u0 = xm[1]
        ruk = xm[0]

        loaded_w = sig("loaded_w", 0)
        consts, held = sig("consts", 0), sig("held", 0)
        y_loaded, ctx_loaded, stored = sig("y_loaded", 32), sig("ctx_loaded", 32), sig("stored", 16 * G)
        filled = sig("filled", len(items))
        emptied = {w: sig("emptied_" + w, [i[1] for i in items].count(w)) for w in ("act", "dve")}
        ring = Ring(items, filled, emptied)
        wy_normed, x2_ready = sig("wy_normed", G), sig("x2_ready", G)
        var_ready, rstd_ready, xn_ready = sig("var_ready", 2), sig("rstd_ready", 2), sig("xn_ready", 2 * G)
        first_set, sx_ready, u0_ready = sig("first_set", 2), sig("sx_ready", 2), sig("u0_ready", 1)
        xm_ready = sig("xm_ready", 5 * KC)
        tanh_g, s_first, scanned = sig("tanh_g", KC), sig("s_first", KC * HD), sig("scanned", KC * HD)
        rs_ready, summed, ruk_ready = sig("rs_ready", KC * HD), sig("summed", KC * HD), sig("ruk_ready", 1)
        out_ready = sig("out_ready", G)
        gn_centred, gn_squared, gn_var, gn_rstd, gn_ready = (sig(n, 1) for n in ("gn_c", "gn_s", "gn_v", "gn_r", "gn_o"))
        z_ready = sig("z_ready", KC)
        mix_ready, squared, x4_ready = sig("mix_ready", 2), sig("squared", KC), sig("x4_ready", G)
        dve_step, act_step = sig("dve_step", 21), sig("act_step", KC)
        signals = [s for s in locals().values() if isinstance(s, Signal)] + list(emptied.values())
        x1_v, wy_v = dram["x1"].rearrange("b t d -> t b d"), dram["wy"].rearrange("b t d -> t b d")
        block = ctx.enter_context(nc.Block())

        @block.sync
        def _(sp):
            for s in signals:
                if s.per:
                    sp.sem_inc(s.sem, s.per)
            for tile, name in [(vec, "vecs"), (ident, "ident"), (heads, "heads"), (td2, "L2_xattn_td_w2")]:
                sp.dma_start(tile[:, :], dram[name]).then_inc(*loaded_w.up(16))
            sp.dma_start(pick[:, :, :], dram["pick"].rearrange("p (j q) -> p j q", j=HD)).then_inc(*loaded_w.up(16))
            w2 = dram["L2_xattn_maa_w2"].rearrange("f d e -> (f d) e")
            sp.dma_start(w2a[:, :], w2[0:4 * DM, :]).then_inc(*loaded_w.up(16))
            sp.dma_start(w2b[:, :], w2[4 * DM:5 * DM, :]).then_inc(*loaded_w.up(16))
            for tile, name in [(w1, "L2_xattn_maa_w1"), (td1, "L2_xattn_td_w1")] + [(W[n], "L2_%sT" % n) for n in W]:
                sp.dma_start(tile[:, :, :], dram[name].rearrange("(k p) n -> p k n", p=P)).then_inc(*loaded_w.up(16))
            with sp.Fori(0, NG) as turn:
                sp.wait_ge(*x2_ready.before(turn))
                sp.sem_inc(held.sem, 1)
                sp.dma_start(x1g[:, :, :], x1_v[:, bass.ds(turn * G, G), :]).then_inc(*y_loaded.up(16))
                sp.wait_ge(*ring.full_before(turn, "n2", KC - 1))
                sp.sem_inc(held.sem, 1)
                sp.dma_start(wyg[:, :, :], wy_v[:, bass.ds(turn * G, G), :]).then_inc(*y_loaded.up(16))
                sp.wait_ge(*first_set.before(turn))
                sp.sem_inc(held.sem, 1)
                sp.dma_start(prev[:, :, :, :], dram["state_rows"][:, bass.ds(turn * G, G), :, :]).then_inc(*ctx_loaded.up(16))
                sp.dma_start(s0[:, :, :, :], dram["state_heads"][:, bass.ds(turn * KC, KC), :, :]).then_inc(*ctx_loaded.up(16))
                for g in range(G):
                    sp.wait_ge(*x4_ready(turn, g + 1))
                    sp.sem_inc(held.sem, 1)
                    sp.dma_start(dram["x4"][bass.ds(turn * G + g, 1), :, :].rearrange("b t d -> t (b d)"),
                                 x2[:, g, :]).then_inc(*stored.up(16))
            sp.wait_ge(*stored(NG - 1, 16 * G))

        @block.tensor
        def _(pe):
            pe.wait_ge(loaded_w.sem, loaded_w.seen)

            def fill(turn, *name, moved=()):
                for wait in ring.ready(turn, name, moved):
                    pe.wait_ge(*wait)
                return pR[:, ring.bank(*name), :]

            def turn_norm(turn, which):
                pe.wait_ge(*xn_ready(turn, G * (which + 1)))
                for c in range(KC):
                    bank = fill(turn, "n%d" % (which + 1), c)
                    for g in range(G):
                        mm = nc.tensor.transpose(bank[:, g * T:g * T + T], xn[:, g, c * P:c * P + P], ident[:, :])
                    mm.then_inc(*filled.up())

            def linear(turn, name, w, src):
                for m in range(KC):
                    bank = fill(turn, name, m)
                    for c in range(KC):
                        mm = nc.tensor.matmul(bank, w[:, c, m * P:m * P + P], src[:, c, :], start=(c == 0), stop=(c == KC - 1))
                    mm.then_inc(*filled.up())

            def linear_tokens(turn, name, w, src):
                for g in range(G):
                    bank = fill(turn, name, g)
                    for c in range(KC):
                        mm = nc.tensor.matmul(bank, src[:, c, g * T:g * T + T], w[:, c, :], start=(c == 0), stop=(c == KC - 1))
                    mm.then_inc(*filled.up())

            def lora(turn, j):
                for c in range(KC):
                    bank = fill(turn, "m", j, c, moved=[("h1",)])
                    if j < 4:
                        mm = nc.tensor.matmul(bank, w2a[j * DM:j * DM + DM, c * P:c * P + P], hid[j * DM:j * DM + DM, :], start=True, stop=True)
                    else:
                        mm = nc.tensor.matmul(bank, w2b[:, c * P:c * P + P], hid4[:, :], start=True, stop=True)
                    mm.then_inc(*filled.up())

            def broadcast_v(turn, n):
                c, j = divmod(n, HD)
                bank = fill(turn, "vb", n, moved=[("v", KC - 1)])
                nc.tensor.matmul(bank, pick[:, j, :], vT[:, c, :], start=True, stop=True).then_inc(*filled.up())

            with pe.Fori(0, NG) as turn:
                turn_norm(turn, 0)
                pe.wait_ge(*u0_ready(turn, 1))
                for name, lo, size in (("h0", 0, 4 * DM), ("h1", 4 * DM, DM)):
                    bank = fill(turn, name)
                    for c in range(KC):
                        mm = nc.tensor.matmul(bank[0:size, :], w1[:, c, lo:lo + size], u0[:, c, :], start=(c == 0), stop=(c == KC - 1))
                    mm.then_inc(*filled.up())
                lora(turn, 0)
                for j, name in enumerate(LORA):
                    if j + 1 < len(LORA):
                        lora(turn, j + 1)
                    pe.wait_ge(*xm_ready(turn, KC * (j + 1)))
                    src = xm[j % 2]
                    if name == "w":
                        bank = fill(turn, "td1")
                        for c in range(KC):
                            mm = nc.tensor.matmul(bank[0:DD, :], td1[:, c, :], src[:, c, :], start=(c == 0), stop=(c == KC - 1))
                        mm.then_inc(*filled.up())
                        for c in range(KC):
                            bank = fill(turn, "w", c, moved=[("td1",)])
                            nc.tensor.matmul(bank, td2[:, c * P:c * P + P], th, start=True, stop=True).then_inc(*filled.up())
                        continue
                    linear(turn, name, W["W" + name], src)
                    if name == "v":
                        linear_tokens(turn, "vt", W["Wv"], src)
                pe.wait_ge(*out_ready.before(turn))
                broadcast_v(turn, 0)
                broadcast_v(turn, 1)
                for n in range(KC * HD):
                    if n + 2 < KC * HD:
                        broadcast_v(turn, n + 2)
                    pe.wait_ge(*rs_ready(turn, n + 1))
                    for g in range(G):
                        mm = nc.tensor.matmul(pO[:, g, n * HC:n * HC + HC], rs[:, n % 2, g * T:g * T + T], heads[:, :], start=True, stop=True)
                    mm.then_inc(*summed.up())
                bank = fill(turn, "u")
                pe.wait_ge(*ruk_ready(turn, 1))
                for g in range(G):
                    for c in range(KC):
                        at = g * NH + c * HC
                        mm = nc.tensor.matmul(bank[:, at:at + HC], ruk[:, c, g * T:g * T + T], heads[:, :], start=True, stop=True)
                mm.then_inc(*filled.up())
                pe.wait_ge(*gn_ready(turn, 1))
                for c in range(KC):
                    bank = fill(turn, "gn", c)
                    for g in range(G):
                        mm = nc.tensor.transpose(bank[:, g * T:g * T + T], xn[:, g, c * P:c * P + P], ident[:, :])
                    mm.then_inc(*filled.up())
                pe.wait_ge(*z_ready(turn, KC))
                linear_tokens(turn, "o", W["Wo"], xm[1])
                turn_norm(turn, 1)
                pe.wait_ge(*mix_ready(turn, 1))
                linear(turn, "fk", W["Wfk"], xm[0])
                pe.wait_ge(*mix_ready(turn, 2))
                linear_tokens(turn, "fr", W["Wfr"], xm[1])
                pe.wait_ge(*squared(turn, KC))
                linear_tokens(turn, "fv", W["Wfv"], kT)

        @block.scalar
        def _(act):
            act.wait_ge(loaded_w.sem, loaded_w.seen)

            def take(turn, *name):
                act.wait_ge(*ring.full(turn, *name))
                return pR[:, ring.bank(*name), :]

            def affine_norm(turn, which):
                for c in range(KC):
                    bank = take(turn, "n%d" % (which + 1), c)
                    ln = "L2_xattn_ln%d" % (which + 1)
                    nc.scalar.activation(xT[:, c, :, 1:T + 1], bank.rearrange("p (g t) -> p g t", g=G), ACT.Identity,
                                         bias=col(ln + "_b", c), scale=col(ln + "_w", c)).then_inc(*emptied["act"].up())

            def drain(turn, dst, *name, func=ACT.Copy, **kw):
                bank = take(turn, *name)
                nc.scalar.activation(dst, bank[0:dst.shape[0], :], func, **kw).then_inc(*emptied["act"].up())

            def first_columns(turn, which):
                nc.scalar.activation(xT[:, :, :, 0:1], prev[:, :, 1 - which, :].rearrange("p g k -> p k g").unsqueeze(3), ACT.Copy)\
                    .then_inc(*first_set.up())

            with act.Fori(0, NG) as turn:
                act.wait_ge(*y_loaded(turn, 32))
                for g in range(G):
                    nc.scalar.activation(wyg[:, g, :], wyg[:, g, :], ACT.Identity, bias=norm[:, 1:2], scale=norm[:, 0:1])\
                        .then_inc(*wy_normed.up())
                act.wait_ge(*mix_ready.before(turn))
                act.wait_ge(*ctx_loaded(turn, ctx_loaded.per))
                first_columns(turn, 0)
                affine_norm(turn, 0)
                drain(turn, hid[:, :], "h0", func=ACT.Tanh)
                drain(turn, hid4[:, :], "h1", func=ACT.Tanh)
                for c in range(KC):
                    drain(turn, kT[:, c, :], "k", c)
                drain(turn, th, "td1", func=ACT.Tanh)
                for c in range(KC):
                    bank = take(turn, "w", c)
                    nc.scalar.activation(wT[:, c, :], bank, ACT.Exp, bias=col("L2_xattn_time_decay", c)).then_inc(*emptied["act"].up())
                    act.wait_ge(*ring.out(turn, "w", c))
                    nc.scalar.activation(wT[:, c, :], wT[:, c, :], ACT.Exp, scale=-1.0).then_inc(*act_step.up())
                for c in range(KC):
                    drain(turn, vT[:, c, :], "v", c)
                act.wait_ge(*x4_ready.before(turn))
                for g in range(G):
                    drain(turn, v_tm[:, g, :], "vt", g)
                for c in range(KC):
                    drain(turn, rT[:, c, :], "r", c)
                for c in range(KC):
                    bank = take(turn, "g", c)
                    nc.scalar.activation(gT[:, c, :], bank, ACT.Tanh, scale=0.5).then_inc(*tanh_g.up())
                for n in range(KC * HD):
                    c, j = divmod(n, HD)
                    act.wait_ge(*(rs_ready(turn, n - 1) if n >= 2 else rs_ready.before(turn)))
                    nc.scalar.activation(S[:, n % 2, :, 0:1], s0[:, c, :, j:j + 1], ACT.Copy).then_inc(*s_first.up())
                for c in range(KC):
                    drain(turn, xm[1][:, c, :], "gn", c, func=ACT.Identity, bias=col("L2_xattn_gn_b", c), scale=col("L2_xattn_gn_w", c))
                act.wait_ge(*xm_ready(turn, 5 * KC))
                first_columns(turn, 1)
                affine_norm(turn, 1)
                for c in range(KC):
                    drain(turn, kT[:, c, :], "fk", c, func=ACT.Relu)
                act.wait_ge(*out_ready(turn, G))
                for g in range(G):
                    drain(turn, v_tm[:, g, :], "fr", g, func=ACT.Tanh, scale=0.5)

        @block.vector
        def _(dve):
            dve.wait_ge(loaded_w.sem, loaded_w.seen)
            nc.vector.memset(half[:, :], -0.5).then_inc(*consts.up())

            def take(turn, *name):
                dve.wait_ge(*ring.full(turn, *name))
                return pR[:, ring.bank(*name), :]

            def whiten(turn, which, ready):
                for g in range(G):
                    dve.wait_ge(*ready(turn, g + 1))
                    nc.vector.bn_stats(bn[:, g, :], x2[:, g, :]).then_inc(*dve_step.up())
                    dve.wait_ge(*dve_step.last(turn))
                    dve.sem_inc(held.sem, 1)
                    nc.vector.bn_aggr(mv[:, g, :], bn[:, g, :]).then_inc(*dve_step.up())
                dve.wait_ge(*dve_step.last(turn))
                nc.vector.tensor_scalar(veps[:, :].unsqueeze(2), mv[:, :, 1:2], 1e-5, None, ALU.add).then_inc(*var_ready.up())
                dve.wait_ge(*rstd_ready(turn, which + 1))
                for g in range(G):
                    nc.vector.tensor_scalar(xn[:, g, :], x2[:, g, :], mv[:, g, 0:1], rstd[:, g:g + 1], ALU.subtract, ALU.mult)\
                        .then_inc(*xn_ready.up())

            def shift(turn, which):
                for c in range(KC):
                    dve.wait_ge(*ring.out(turn, "n%d" % (which + 1), c))
                    ins = nc.vector.tensor_tensor(sx[:, c, :].rearrange("p (g t) -> p g t", g=G), xT[:, c, :, 0:T], xT[:, c, :, 1:T + 1],
                                                  ALU.subtract)
                ins.then_inc(*sx_ready.up())
                dve.wait_ge(*sx_ready(turn, which + 1))

            def mix(dst, name):
                for c in range(KC):
                    ins = nc.vector.scalar_tensor_tensor(out=dst[:, c, :].rearrange("p (g t) -> p g t", g=G),
                                                         in0=sx[:, c, :].rearrange("p (g t) -> p g t", g=G), scalar=col(name, c),
                                                         in1=xT[:, c, :, 1:T + 1], op0=ALU.mult, op1=ALU.add)
                return ins

            def lora(turn, j):
                for c in range(KC):
                    bank = take(turn, "m", j, c)
                    nc.vector.scalar_tensor_tensor(out=xm[j % 2][:, c, :], in0=bank, scalar=col("L2_xattn_maa_stack", c, j),
                                                   in1=sx[:, c, :], op0=ALU.add, op1=ALU.mult).then_inc(*emptied["dve"].up())

            dve.wait_ge(consts.sem, 1)
            with dve.Fori(0, NG) as turn:
                dve.wait_ge(*ring.full_before(turn, "n2", KC - 1))
                whiten(turn, 0, x2_ready)
                dve.wait_ge(*first_set(turn, 1))
                shift(turn, 0)
                dve.wait_ge(*ring.full_before(turn, "fr", G - 1))
                mix(u0, "L2_xattn_maa_x").then_inc(*u0_ready.up())
                for j in range(len(LORA)):
                    lora(turn, j)
                for c in range(KC):
                    bank = take(turn, "g", c)
                    dve.wait_ge(*tanh_g(turn, c + 1))
                    nc.vector.scalar_tensor_tensor(out=gT[:, c, :], in0=gT[:, c, :], scalar=1.0, in1=bank, op0=ALU.add, op1=ALU.mult)\
                        .then_inc(*emptied["dve"].up())
                dve.wait_ge(*ring.out(turn, "r", KC - 1))
                for c in range(KC):
                    ins = nc.vector.scalar_tensor_tensor(out=ruk[:, c, :], in0=rT[:, c, :], scalar=col("L2_xattn_u", c), in1=kT[:, c, :],
                                                         op0=ALU.mult, op1=ALU.mult)
                ins.then_inc(*ruk_ready.up())
                dve.wait_ge(*ctx_loaded(turn, ctx_loaded.per))
                dve.wait_ge(*act_step(turn, KC))
                for n in range(KC * HD):
                    c, j = divmod(n, HD)
                    bank = take(turn, "vb", n)
                    dve.wait_ge(*(scanned(turn, n - 1) if n >= 2 else scanned.before(turn)))
                    nc.vector.tensor_tensor(a_kv[:, n % 2, :], kT[:, c, :], bank, ALU.mult).then_inc(*emptied["dve"].up())
                    dve.wait_ge(*ring.out(turn, "vb", n))
                    if n >= 2:
                        dve.wait_ge(*rs_ready(turn, n - 1))
                    else:
                        dve.wait_ge(*rs_ready.before(turn))
                    for g in range(G):
                        ins = nc.vector.tensor_tensor_scan(S[:, n % 2, g, 1:T + 1], wT[:, c, g * T:g * T + T], a_kv[:, n % 2, g * T:g * T + T],
                                                           s0[:, c, g, j:j + 1], ALU.mult, ALU.add)
                    ins.then_inc(*scanned.up())
                u = take(turn, "u")
                dve.wait_ge(*summed(turn, KC * HD))
                dve.wait_ge(*ring.out(turn, "vt", G - 1))
                o = xn[:, :, :].rearrange("p g (h j) -> p (g h) j", j=HD)
                for g in range(G):
                    nc.vector.tensor_tensor(xn[:, g, :].rearrange("p (h j) -> p h j", j=HD),
                                            v_tm[:, g, :].rearrange("p (h j) -> p h j", j=HD),
                                            u[:, g * NH:g * NH + NH].unsqueeze(2).to_broadcast([P, NH, HD]), ALU.mult)\
                        .then_inc(*(emptied["dve"].up() if g == G - 1 else dve_step.up()))
                dve.wait_ge(*ring.out(turn, "u"))
                dve.wait_ge(*dve_step.last(turn))
                for g in range(G):
                    nc.vector.tensor_tensor(xn[:, g, :].rearrange("p (c h j) -> p c h j", c=KC, j=HD),
                                            xn[:, g, :].rearrange("p (c h j) -> p c h j", c=KC, j=HD),
                                            pO[:, g, :].rearrange("p (c j h) -> p c h j", c=KC, j=HD), ALU.add).then_inc(*out_ready.up())
                dve.wait_ge(*out_ready(turn, G))
                nc.vector.tensor_reduce(gsum[:, :, :].rearrange("p g h -> p (g h)"), o, AX.X, ALU.add).then_inc(*dve_step.up())
                dve.wait_ge(*dve_step.last(turn))
                mean = gsum[:, :, :].rearrange("p g h -> p (g h)")
                nc.vector.scalar_tensor_tensor(out=o, in0=mean.unsqueeze(2).to_broadcast([P, G * NH, HD]), scalar=-1.0 / HD, in1=o,
                                               op0=ALU.mult, op1=ALU.add).then_inc(*gn_centred.up())
                dve.wait_ge(*gn_squared(turn, 1))
                sq = sx[:, :, :].rearrange("p k (h j) -> p (k h) j", j=HD)
                nc.vector.tensor_reduce(gvar[:, :, :].rearrange("p g h -> p (g h)"), sq, AX.X, ALU.add).then_inc(*dve_step.up())
                dve.wait_ge(*dve_step.last(turn))
                nc.vector.tensor_scalar(gvar[:, :, :], gvar[:, :, :], 1.0 / HD, 1e-5, ALU.mult, ALU.add).then_inc(*gn_var.up())
                dve.wait_ge(*gn_rstd(turn, 1))
                nc.vector.tensor_tensor(o, o, grstd[:, :, :].rearrange("p g h -> p (g h)").unsqueeze(2).to_broadcast([P, G * NH, HD]),
                                        ALU.mult).then_inc(*gn_ready.up())
                for c in range(KC):
                    dve.wait_ge(*ring.out(turn, "gn", c))
                    nc.vector.scalar_tensor_tensor(out=xm[1][:, c, :], in0=xm[1][:, c, :], scalar=0.5, in1=gT[:, c, :],
                                                   op0=ALU.mult, op1=ALU.mult).then_inc(*z_ready.up())
                for g in range(G):
                    bank = take(turn, "o", g)
                    nc.vector.tensor_tensor(x2[:, g, :], x2[:, g, :], bank, ALU.add)\
                        .then_inc(*emptied["dve"].up())
                whiten(turn, 1, lambda t, k: ring.out(t, "o", k - 1))
                dve.wait_ge(*first_set(turn, 2))
                shift(turn, 1)
                mix(xm[0], "L2_xattn_ffn_maa_k").then_inc(*mix_ready.up())
                mix(xm[1], "L2_xattn_ffn_maa_r").then_inc(*mix_ready.up())
                for g in range(G):
                    bank = take(turn, "fv", g)
                    dve.wait_ge(*ring.out(turn, "fr", g))
                    nc.vector.scalar_tensor_tensor(out=v_tm[:, g, :], in0=v_tm[:, g, :], scalar=1.0, in1=bank, op0=ALU.add, op1=ALU.mult)\
                        .then_inc(*emptied["dve"].up())
                    dve.wait_ge(*ring.out(turn, "fv", g))
                    nc.vector.scalar_tensor_tensor(out=x2[:, g, :], in0=v_tm[:, g, :], scalar=0.5, in1=x2[:, g, :], op0=ALU.mult, op1=ALU.add)\
                        .then_inc(*x4_ready.up())

        @block.gpsimd
        def _(pool):
            pool.wait_ge(consts.sem, 1)

            def deviation(turn, which):
                pool.wait_ge(*var_ready(turn, which + 1))
                nc.gpsimd.tensor_tensor(rstd[:, :], veps[:, :], half[:, 0:G], ALU.pow).then_inc(*rstd_ready.up())

            with pool.Fori(0, NG) as turn:
                pool.wait_ge(*stored.before(turn))
                for g in range(G):
                    pool.wait_ge(*wy_normed(turn, g + 1))
                    nc.gpsimd.tensor_tensor(x2[:, g, :], wyg[:, g, :], x1g[:, g, :], ALU.add).then_inc(*x2_ready.up())
                deviation(turn, 0)
                for j in range(len(LORA)):
                    for c in range(KC):
                        pool.wait_ge(*ring.out(turn, "m", j, c))
                        nc.gpsimd.tensor_tensor(xm[j % 2][:, c, :].rearrange("p (g t) -> p g t", g=G),
                                                xm[j % 2][:, c, :].rearrange("p (g t) -> p g t", g=G), xT[:, c, :, 1:T + 1], ALU.add)\
                            .then_inc(*xm_ready.up())
                pool.wait_ge(*ring.out(turn, "r", KC - 1))
                for n in range(KC * HD):
                    c, j = divmod(n, HD)
                    pool.wait_ge(*s_first(turn, n + 1))
                    pool.wait_ge(*scanned(turn, n + 1))
                    if n >= 2:
                        pool.wait_ge(*summed(turn, n - 1))
                    else:
                        pool.wait_ge(*summed.before(turn))
                    nc.gpsimd.tensor_tensor(rs[:, n % 2, :].rearrange("p (g t) -> p g t", g=G), S[:, n % 2, :, 0:T],
                                            rT[:, c, :].rearrange("p (g t) -> p g t", g=G), ALU.mult).then_inc(*rs_ready.up())
                pool.wait_ge(*gn_centred(turn, 1))
                nc.gpsimd.tensor_tensor(sx[:, :, :].rearrange("p k n -> p (k n)"), xn[:, :, :].rearrange("p g d -> p (g d)"),
                                        xn[:, :, :].rearrange("p g d -> p (g d)"), ALU.mult).then_inc(*gn_squared.up())
                pool.wait_ge(*gn_var(turn, 1))
                nc.gpsimd.tensor_tensor(grstd[:, :, :].rearrange("p g h -> p (g h)"), gvar[:, :, :].rearrange("p g h -> p (g h)"),
                                        half[:, :], ALU.pow).then_inc(*gn_rstd.up())
                deviation(turn, 1)
                for c in range(KC):
                    pool.wait_ge(*ring.out(turn, "fk", c))
                    nc.gpsimd.tensor_tensor(kT[:, c, :], kT[:, c, :], kT[:, c, :], ALU.mult).then_inc(*squared.up())

        wrong = {s.sem.name: (s.per, s.seen) for s in signals if s.per and s.per != s.seen}
        assert not wrong, wrong


def phase_c(nc, dram):
    NH, HD = 16, 32
    HV = HD + 1
    PH = NH // 2
    FC = 4 * D // P
    items = [(("cT", c), "dve") for c in range(KC)] + [(("k", c), "act") for c in range(KC)] + [(("v", g), "dve") for g in range(G)]
    items += [(("n1", c), "act") for c in range(KC)] + [(("q", c), "act") for c in range(KC)]
    for g in range(G):
        items += [(("pT", g, b), "act" if b % 2 else "dve") for b in range(4)] + [(("pv", g, h), "dve") for h in range(2)]
        if g:
            items += [(("aT", g - 1), "act"), (("o", g - 1), "dve")]
    items += [(("aT", G - 1), "act"), (("o", G - 1), "dve")]
    items += [(("n2", c), "act") for c in range(KC)] + [(("fc", m), "act") for m in range(FC)] + [(("pr", g), "dve") for g in range(G)]

    with ExitStack() as ctx:
        def sb(name, shape, dt=F32):
            return ctx.enter_context(nc.sbuf_tensor("c_" + name, shape, dt))

        def sig(name, per):
            return Signal(ctx.enter_context(nc.semaphore("c_" + name)), per)

        W = {n: sb(n, [P, KC, D]) for n in ("q_w", "k_w", "v_w", "cproj_w")}
        fc_w, proj_w = sb("fc_w", [P, KC, 4 * D]), sb("proj_w", [P, FC, D])
        vec = sb("vec", [P, dram["vecs"].shape[1]])
        rows, ident = sb("rows", [P, 3 * D]), sb("ident", [P, P])
        v_b, cproj_b, proj_b = (rows[:, i * D:i * D + D] for i in range(3))
        half = sb("half", [P, G])
        x, c_tm, xn = sb("x", [P, G, D]), sb("c", [P, G, D]), sb("xn", [P, G, D])
        xT, cT, qT, kT = (sb(n, [P, KC, TOK]) for n in ("xT", "cT", "qT", "kT"))
        attT = cT
        v_ext = sb("v_ext", [P, G, NH, HV])
        wide = sb("wide", [P, 4, NH * T])
        S = wide[:, 0:2, :].rearrange("p a (h t) -> p a h t", t=T)
        probsT = wide[:, 2:4, :].rearrange("p a (h t) -> p a h t", t=T)
        fcT = wide[:, :, :].rearrange("p a (m n) -> p (a m) n", n=TOK)
        mask_u8, limit = sb("mask_u8", [P, G, T], U8), sb("limit", [P, G, T])
        smax, rden = sb("smax", [P, 2, NH]), sb("rden", [P, 2, PH])
        att = sb("att", [P, 2, D])
        bn, mv = sb("bn", [P, G, 6]), sb("mv", [P, G, 2])
        veps, rstd = sb("veps", [P, G]), sb("rstd", [P, G])
        pS = ctx.enter_context(nc.psum_tensor("c_pS", [P, 4, 512], F32))
        pR = ctx.enter_context(nc.psum_tensor("c_pR", [P, RING, 512], F32))

        loaded_w, consts, held = sig("loaded_w", 0), sig("consts", 0), sig("held", 0)
        x_loaded, c_loaded, mask_loaded, stored = sig("x_loaded", 16), sig("c_loaded", 16), sig("mask_loaded", 16), sig("stored", 16 * G)
        filled = sig("filled", len(items))
        emptied = {w: sig("emptied_" + w, [i[1] for i in items].count(w)) for w in ("act", "dve")}
        ring = Ring(items, filled, emptied)
        limit_sign, limit_ready = sig("limit_sign", 1), sig("limit_ready", 1)
        scored, masked, max_found, centred, exp_done = (sig(n, G) for n in ("scored", "masked", "max_found", "centred", "exp_done"))
        var_ready, rstd_ready, xn_ready = sig("var_ready", 2), sig("rstd_ready", 2), sig("xn_ready", 2 * G)
        xb_ready, hb_ready, out_ready = sig("xb_ready", 1), sig("hb_ready", 1), sig("out_ready", G)
        dve_step = sig("dve_step", 24)
        signals = [s for s in locals().values() if isinstance(s, Signal)] + list(emptied.values())
        x_v, c_v = dram["x4"].rearrange("b t d -> t b d"), dram["ctx_2048"].rearrange("b t d -> t b d")
        block = ctx.enter_context(nc.Block())

        def col(name, c):
            at = vec_column(name) + c
            return vec[:, at:at + 1]

        @block.sync
        def _(sp):
            for s in signals:
                if s.per:
                    sp.sem_inc(s.sem, s.per)
            for tile, name in [(vec, "vecs"), (ident, "ident"), (rows, "rows_c")]:
                sp.dma_start(tile[:, :], dram[name]).then_inc(*loaded_w.up(16))
            for tile, name in [(W[n], n) for n in W] + [(fc_w, "fc_w"), (proj_w, "proj_w")]:
                sp.dma_start(tile[:, :, :], dram["L3_xattn_" + name].rearrange("(k p) n -> p k n", p=P)).then_inc(*loaded_w.up(16))
            with sp.Fori(0, NG) as turn:
                sp.wait_ge(*stored.before(turn))
                sp.sem_inc(held.sem, 1)
                sp.dma_start(x[:, :, :], x_v[:, bass.ds(turn * G, G), :]).then_inc(*x_loaded.up(16))
                sp.wait_ge(*ring.full_before(turn, "cT", KC - 1))
                sp.sem_inc(held.sem, 1)
                sp.dma_start(c_tm[:, :, :], c_v[:, bass.ds(turn * G, G), :]).then_inc(*c_loaded.up(16))
                sp.wait_ge(*limit_sign.before(turn))
                sp.sem_inc(held.sem, 1)
                sp.dma_start(mask_u8[:, :, :], dram["mask_rows"][:, bass.ds(turn * G, G), :]).then_inc(*mask_loaded.up(16))
                for g in range(G):
                    sp.wait_ge(*out_ready(turn, g + 1))
                    sp.sem_inc(held.sem, 1)
                    sp.dma_start(dram["out"][bass.ds(turn * G + g, 1), :, :].rearrange("b t d -> t (b d)"),
                                 x[:, g, :]).then_inc(*stored.up(16))
            sp.wait_ge(*stored(NG - 1, 16 * G))

        @block.tensor
        def _(pe):
            pe.wait_ge(loaded_w.sem, loaded_w.seen)

            def fill(turn, *name, moved=()):
                for wait in ring.ready(turn, name, moved):
                    pe.wait_ge(*wait)
                return pR[:, ring.bank(*name), :]

            def turned(turn, name, src):
                for c in range(KC):
                    bank = fill(turn, name, c)
                    for g in range(G):
                        mm = nc.tensor.transpose(bank[:, g * T:g * T + T], src[:, g, c * P:c * P + P], ident[:, :])
                    mm.then_inc(*filled.up())

            def linear(turn, name, w, src, chunks, turned):
                for m in range(chunks):
                    bank = fill(turn, name, m, moved=[(turned, KC - 1)])
                    for c in range(KC):
                        mm = nc.tensor.matmul(bank, w[:, c, m * P:m * P + P], src[:, c, :], start=(c == 0), stop=(c == KC - 1))
                    mm.then_inc(*filled.up())

            def scores(turn, g):
                if g:
                    pe.wait_ge(*masked(turn, g))
                else:
                    pe.wait_ge(*masked.before(turn))
                for c in range(KC):
                    for r in range(4):
                        at = slice(HD * r, HD * r + HD)
                        mm = nc.tensor.matmul(pS[:, r, c * T:c * T + T], qT[at, c, g * T:g * T + T], kT[at, c, g * T:g * T + T],
                                              start=True, stop=True)
                mm.then_inc(*scored.up())

            def project(turn, g):
                bank = fill(turn, "aT", g, moved=[("pv", g, 1)])
                for c in range(KC):
                    mm = nc.tensor.transpose(bank[:, c * P:c * P + P], att[:, g % 2, c * P:c * P + P], ident[:, :])
                mm.then_inc(*filled.up())
                bank = fill(turn, "o", g, moved=[("aT", g)])
                for c in range(KC):
                    mm = nc.tensor.matmul(bank, attT[:, c, g * T:g * T + T], W["cproj_w"][:, c, :], start=(c == 0), stop=(c == KC - 1))
                mm.then_inc(*filled.up())

            with pe.Fori(0, NG) as turn:
                pe.wait_ge(*c_loaded(turn, 16))
                turned(turn, "cT", c_tm)
                linear(turn, "k", W["k_w"], cT, KC, "cT")
                for g in range(G):
                    bank = fill(turn, "v", g)
                    for c in range(KC):
                        mm = nc.tensor.matmul(bank, cT[:, c, g * T:g * T + T], W["v_w"][:, c, :], start=(c == 0), stop=(c == KC - 1))
                    mm.then_inc(*filled.up())
                pe.wait_ge(*xn_ready(turn, G))
                turned(turn, "n1", xn)
                linear(turn, "q", W["q_w"], xT, KC, "n1")
                pe.wait_ge(*ring.out(turn, "q", KC - 1))
                scores(turn, 0)
                for g in range(G):
                    if g + 1 < G:
                        scores(turn, g + 1)
                    pe.wait_ge(*exp_done(turn, g + 1))
                    for b in range(4):
                        bank = fill(turn, "pT", g, b)
                        for i in range(4):
                            mm = nc.tensor.transpose(bank[:, i * T:i * T + T], S[:, g % 2, 4 * b + i, :], ident[:, :])
                        mm.then_inc(*filled.up())
                    for h2 in range(2):
                        bank = fill(turn, "pv", g, h2, moved=[("v", G - 1)] + [("pT", g, b) for b in range(4)])
                        for i in range(PH):
                            h = PH * h2 + i
                            mm = nc.tensor.matmul(bank[:, i * HV:i * HV + HV], probsT[:, g % 2, h % 4 * 4 + h // 4, :], v_ext[:, g, h, :],
                                                  start=True, stop=True)
                        mm.then_inc(*filled.up())
                    if g:
                        project(turn, g - 1)
                project(turn, G - 1)
                pe.wait_ge(*xn_ready(turn, 2 * G))
                turned(turn, "n2", xn)
                linear(turn, "fc", fc_w, xT, FC, "n2")
                for g in range(G):
                    bank = fill(turn, "pr", g, moved=[("fc", FC - 1)])
                    for m in range(FC):
                        mm = nc.tensor.matmul(bank, fcT[:, m, g * T:g * T + T], proj_w[:, m, :], start=(m == 0), stop=(m == FC - 1))
                    mm.then_inc(*filled.up())

        @block.scalar
        def _(act):
            act.wait_ge(loaded_w.sem, loaded_w.seen)

            def drain(turn, dst, *name, func=ACT.Copy, **kw):
                act.wait_ge(*ring.full(turn, *name))
                nc.scalar.activation(dst, pR[:, ring.bank(*name), :], func, **kw).then_inc(*emptied["act"].up())

            def exp_round(turn, g):
                act.wait_ge(*centred(turn, g + 1))
                nc.scalar.activation(S[:, g % 2, :, :], S[:, g % 2, :, :], ACT.Exp).then_inc(*exp_done.up())

            def turn_att(turn, g):
                act.wait_ge(*ring.full(turn, "aT", g))
                nc.scalar.activation(attT[:, :, g * T:g * T + T], pR[:, ring.bank("aT", g), :].rearrange("p (k t) -> p k t", k=KC), ACT.Copy)\
                    .then_inc(*emptied["act"].up())

            with act.Fori(0, NG) as turn:
                act.wait_ge(*scored.before(turn))
                for c in range(KC):
                    drain(turn, kT[:, c, :], "k", c, func=ACT.Identity, bias=col("L3_xattn_k_b", c))
                for c in range(KC):
                    drain(turn, xT[:, c, :], "n1", c, func=ACT.Identity, bias=col("L3_xattn_ln1_b", c), scale=col("L3_xattn_ln1_w", c))
                for c in range(KC):
                    drain(turn, qT[:, c, :], "q", c, func=ACT.Identity, bias=col("L3_xattn_q_b", c))
                exp_round(turn, 0)
                for g in range(G):
                    if g + 1 < G:
                        exp_round(turn, g + 1)
                    for b in (1, 3):
                        drain(turn, wide[:, 2 + g % 2, b * 512:b * 512 + 512], "pT", g, b)
                    if g:
                        turn_att(turn, g - 1)
                turn_att(turn, G - 1)
                for c in range(KC):
                    drain(turn, xT[:, c, :], "n2", c, func=ACT.Identity, bias=col("L3_xattn_ln2_b", c), scale=col("L3_xattn_ln2_w", c))
                for m in range(FC):
                    drain(turn, fcT[:, m, :], "fc", m, func=ACT.Gelu_apprx_tanh, bias=col("L3_xattn_fc_b", m))

        @block.vector
        def _(dve):
            dve.wait_ge(loaded_w.sem, loaded_w.seen)
            nc.vector.memset(half[:, :], -0.5).then_inc(*consts.up())
            nc.vector.memset(v_ext[:, :, :, HD:HV], 1.0).then_inc(*consts.up())

            def take(turn, *name):
                dve.wait_ge(*ring.full(turn, *name))
                return pR[:, ring.bank(*name), :]

            def whiten(turn, which):
                for g in range(G):
                    nc.vector.bn_stats(bn[:, g, :], x[:, g, :]).then_inc(*dve_step.up())
                    dve.wait_ge(*dve_step.last(turn))
                    dve.sem_inc(held.sem, 1)
                    nc.vector.bn_aggr(mv[:, g, :], bn[:, g, :]).then_inc(*dve_step.up())
                dve.wait_ge(*dve_step.last(turn))
                nc.vector.tensor_scalar(veps[:, :].unsqueeze(2), mv[:, :, 1:2], 1e-5, None, ALU.add).then_inc(*var_ready.up())
                dve.wait_ge(*rstd_ready(turn, which + 1))
                for g in range(G):
                    nc.vector.tensor_scalar(xn[:, g, :], x[:, g, :], mv[:, g, 0:1], rstd[:, g:g + 1], ALU.subtract, ALU.mult)\
                        .then_inc(*xn_ready.up())

            def softmax_max(turn, g):
                dve.wait_ge(*scored(turn, g + 1))
                dve.wait_ge(*(ring.full(turn, "pT", g - 2, 3) if g >= 2 else ring.full_before(turn, "pr", G - 1)))
                nc.vector.scalar_tensor_tensor(out=S[:, g % 2, :, :], in0=pS[:, :, :].rearrange("p r (h t) -> p (r h) t", t=T),
                                               scalar=float(np.float32(1) / np.sqrt(HD).astype(np.float32)),
                                               in1=limit[:, g:g + 1, :].to_broadcast([P, NH, T]), op0=ALU.mult, op1=ALU.min)\
                    .then_inc(*masked.up())
                dve.wait_ge(*masked(turn, g + 1))
                if g >= 2:
                    dve.wait_ge(*centred(turn, g - 1))
                nc.vector.tensor_reduce(smax[:, g % 2, :], S[:, g % 2, :, :], AX.X, ALU.max).then_inc(*max_found.up())

            def normalise(turn, g, h2):
                bank = take(turn, "pv", g, h2)[:, 0:PH * HV].rearrange("p (h e) -> p h e", e=HV)
                nc.vector.reciprocal(rden[:, h2, :].unsqueeze(2), bank[:, :, HD:HV]).then_inc(*dve_step.up())
                dve.wait_ge(*dve_step.last(turn))
                nc.vector.tensor_tensor(att[:, g % 2, h2 * 256:h2 * 256 + 256].rearrange("p (h d) -> p h d", d=HD), bank[:, :, 0:HD],
                                        rden[:, h2, :].unsqueeze(2).to_broadcast([P, PH, HD]), ALU.mult).then_inc(*emptied["dve"].up())

            def residual(turn, g):
                bank = take(turn, "o", g)
                if g == 0:
                    dve.wait_ge(*xb_ready(turn, 1))
                nc.vector.tensor_tensor(x[:, g, :], x[:, g, :], bank, ALU.add).then_inc(*emptied["dve"].up())

            dve.wait_ge(consts.sem, 2)
            with dve.Fori(0, NG) as turn:
                for c in range(KC):
                    bank = take(turn, "cT", c)
                    nc.vector.tensor_copy(cT[:, c, :], bank).then_inc(*emptied["dve"].up())
                dve.wait_ge(*x_loaded(turn, 16))
                dve.wait_ge(*ring.full_before(turn, "n2", KC - 1))
                whiten(turn, 0)
                for g in range(G):
                    bank = take(turn, "v", g)
                    nc.vector.tensor_tensor(v_ext[:, g, :, 0:HD], bank.rearrange("p (h d) -> p h d", d=HD),
                                            v_b.rearrange("p (h d) -> p h d", d=HD), ALU.add).then_inc(*emptied["dve"].up())
                dve.wait_ge(*mask_loaded(turn, 16))
                nc.vector.tensor_scalar(limit[:, :, :], mask_u8[:, :, :], 2.0, -1.0, ALU.mult, ALU.add).then_inc(*limit_sign.up())
                dve.wait_ge(*limit_sign(turn, 1))
                nc.vector.tensor_scalar(limit[:, :, :], limit[:, :, :], FMAX, None, ALU.mult).then_inc(*limit_ready.up())
                dve.wait_ge(*limit_ready(turn, 1))
                softmax_max(turn, 0)
                for g in range(G):
                    if g + 1 < G:
                        softmax_max(turn, g + 1)
                    for b in (0, 2):
                        bank = take(turn, "pT", g, b)
                        nc.vector.tensor_copy(wide[:, 2 + g % 2, b * 512:b * 512 + 512], bank).then_inc(*emptied["dve"].up())
                    normalise(turn, g, 0)
                    normalise(turn, g, 1)
                    if g:
                        residual(turn, g - 1)
                residual(turn, G - 1)
                dve.wait_ge(*ring.out(turn, "o", G - 1))
                whiten(turn, 1)
                dve.wait_ge(*hb_ready(turn, 1))
                for g in range(G):
                    bank = take(turn, "pr", g)
                    nc.vector.tensor_tensor(x[:, g, :], x[:, g, :], bank, ALU.add).then_inc(*emptied["dve"].up())
                    out_ready_after = ring.out(turn, "pr", g)
                    dve.wait_ge(*out_ready_after)
                    nc.vector.memset(bn[:, 0, 0:1], 0.0).then_inc(*out_ready.up())

        @block.gpsimd
        def _(pool):
            pool.wait_ge(loaded_w.sem, loaded_w.seen)
            pool.wait_ge(consts.sem, 2)
            with pool.Fori(0, NG) as turn:
                pool.wait_ge(*var_ready(turn, 1))
                nc.gpsimd.tensor_tensor(rstd[:, :], veps[:, :], half[:, :], ALU.pow).then_inc(*rstd_ready.up())
                pool.wait_ge(*xn_ready(turn, G))
                nc.gpsimd.tensor_tensor(x[:, :, :], x[:, :, :], cproj_b.unsqueeze(1).to_broadcast([P, G, D]), ALU.add).then_inc(*xb_ready.up())
                for g in range(G):
                    pool.wait_ge(*max_found(turn, g + 1))
                    nc.gpsimd.tensor_tensor(S[:, g % 2, :, :], S[:, g % 2, :, :], smax[:, g % 2, :].unsqueeze(2).to_broadcast([P, NH, T]),
                                            ALU.subtract).then_inc(*centred.up())
                pool.wait_ge(*var_ready(turn, 2))
                nc.gpsimd.tensor_tensor(rstd[:, :], veps[:, :], half[:, :], ALU.pow).then_inc(*rstd_ready.up())
                pool.wait_ge(*xn_ready(turn, 2 * G))
                nc.gpsimd.tensor_tensor(x[:, :, :], x[:, :, :], proj_b.unsqueeze(1).to_broadcast([P, G, D]), ALU.add).then_inc(*hb_ready.up())

        wrong = {s.sem.name: (s.per, s.seen) for s in signals if s.per and s.per != s.seen}
        assert not wrong, wrong


def phase_norm(nc, dram, stats, norm):
    with ExitStack() as ctx:
        par, mv = ctx.enter_context(nc.sbuf_tensor("n_par", [P, 2], F32)), ctx.enter_context(nc.sbuf_tensor("n_mv", [P, 2], F32))
        half, rstd = ctx.enter_context(nc.sbuf_tensor("n_half", [P, 1], F32)), ctx.enter_context(nc.sbuf_tensor("n_rstd", [P, 1], F32))
        loaded, var_ready, rstd_ready, step = (ctx.enter_context(nc.semaphore("n_" + n)) for n in ("loaded", "var", "rstd", "step"))
        block = ctx.enter_context(nc.Block())

        @block.sync
        def _(sp):
            sp.dma_start(par[:, :], dram["L1_affine"]).then_inc(loaded, 16)

        @block.gpsimd
        def _(pool):
            pool.wait_ge(var_ready, 2)
            nc.gpsimd.tensor_tensor(rstd[:, :], mv[:, 1:2], half[:, :], ALU.pow).then_inc(rstd_ready, 1)

        @block.vector
        def _(dve):
            nc.vector.memset(half[:, :], -0.5).then_inc(var_ready, 1)
            nc.vector.bn_aggr(mv[:, :], stats[:, :]).then_inc(step, 1)
            dve.wait_ge(step, 1)
            nc.vector.tensor_scalar(mv[:, 1:2], mv[:, 1:2], 1e-5, None, ALU.add).then_inc(var_ready, 1)
            dve.wait_ge(loaded, 16)
            dve.wait_ge(rstd_ready, 1)
            nc.vector.tensor_tensor(norm[:, 0:1], rstd[:, :], par[:, 0:1], ALU.mult).then_inc(step, 1)
            dve.wait_ge(step, 2)
            nc.vector.tensor_tensor(mv[:, 0:1], mv[:, 0:1], norm[:, 0:1], ALU.mult).then_inc(step, 1)
            dve.wait_ge(step, 3)
            nc.vector.tensor_tensor(norm[:, 1:2], par[:, 1:2], mv[:, 0:1], ALU.subtract).then_inc(step, 1)
            dve.wait_ge(step, 4)


def program(nc, dram):
    with ExitStack() as ctx:
        stats = ctx.enter_context(nc.sbuf_tensor("stats", [P, B * 6], F32))
        norm = ctx.enter_context(nc.sbuf_tensor("norm", [P, 2], F32))
        phase_a(nc, dram, stats)
        phase_norm(nc, dram, stats, norm)
        phase_b(nc, dram, norm)
        phase_c(nc, dram)


def _layout(inputs):
    a = {n: np.asarray(v) for n, v in inputs.items()}
    out = {n: a[n] for n in ("x", "ctx_2048", "mask_Bx1xSxS2_ff0", "L0_xattn_Wq", "L0_xattn_Wk", "L0_xattn_Wv", "L0_xattn_Wo",
                             "L2_xattn_maa_w1", "L2_xattn_maa_w2", "L2_xattn_td_w1", "L2_xattn_td_w2",
                             "L3_xattn_q_w", "L3_xattn_k_w", "L3_xattn_v_w", "L3_xattn_cproj_w", "L3_xattn_fc_w", "L3_xattn_proj_w")}
    for n in ("Wg", "Wtheta", "Wphi", "Wz"):
        out["L1_" + n + "T"] = a["L1_xattn_" + n].T
    for n in ("Wk", "Wv", "Wr", "Wg", "Wo", "Wfk", "Wfr", "Wfv"):
        out["L2_" + n + "T"] = a["L2_xattn_" + n].T
    out["vecs"] = np.concatenate([a[n].reshape(-1, P).T for n in VECS], axis=1)
    out["bk_wide"] = np.broadcast_to(a["L0_xattn_bk"].reshape(8, 1, 16), (8, 4, 16)).reshape(KC, P).T
    out["rows_a"] = np.concatenate([np.broadcast_to(a[n][None, :], (P, a[n].size)) for n in ROWS_A], axis=1)
    out["rows_c"] = np.concatenate([np.broadcast_to(a[n][None, :], (P, a[n].size)) for n in ROWS_C], axis=1)
    out["L1_ci"] = np.stack([a["L1_xattn_bphi"], a["L1_xattn_btheta"]], axis=1)
    out["L1_bz"] = a["L1_xattn_bz"].reshape(P, 1)
    out["L1_affine"] = np.stack([a["L1_xattn_gamma"], a["L1_xattn_beta"]], axis=1)
    out["mask_rows"] = np.broadcast_to(np.ascontiguousarray(a["mask_BxS2_bf1"]).view(np.uint8)[None], (P, B, T))
    state = a["ctx_2048"]
    out["state_rows"] = state[:, 0:2].reshape(B, 2, KC, P).transpose(3, 0, 1, 2)
    out["state_heads"] = state[:, 2:18].reshape(NG, G, KC, P, 16).transpose(3, 0, 2, 1, 4).reshape(P, NG * KC, G, 16)
    out["ident"] = np.eye(P, dtype=np.float32)
    p = np.arange(P)
    out["parity"] = (p[:, None] // 16 % 2 == np.arange(2)[None, :]).astype(np.float32)
    out["heads"] = (p[:, None] // 16 == np.arange(P // 16)[None, :]).astype(np.float32)
    out["pick"] = ((p[:, None, None] // 16 == p[None, None, :] // 16)
                   & (p[:, None, None] % 16 == np.arange(16)[None, :, None])).astype(np.float32).reshape(P, -1)
    return {n: np.ascontiguousarray(v) for n, v in out.items()}


def kernel(**inputs):
    import concourse.bacc as bacc
    from concourse.bass_utils import run_bass_kernel_spmd as run

    arrays = _layout(inputs)
    nc = bacc.Bacc("TRN2", target_bir_lowering=False, num_devices=1)
    dram = {n: nc.dram_tensor(n, v.shape, mybir.dt.from_np(v.dtype), kind="ExternalInput").ap() for n, v in arrays.items()}
    for n in ("x1", "wy", "x4"):
        dram[n] = nc.dram_tensor("mid_" + n, (B, T, D), F32, kind="Internal").ap()
    dram["out"] = nc.dram_tensor("out", (B, T, D), F32, kind="ExternalOutput").ap()
    program(nc, dram)
    return run(nc, [arrays], core_ids=[0]).results[0]["out"]
```

```python
from contextlib import ExitStack

import numpy as np

import concourse.bass as bass
from concourse import mybir

F32 = mybir.dt.float32
F32R = mybir.dt.float32r
U8 = mybir.dt.uint8
ALU = mybir.AluOpType
ACT = mybir.ActivationFunctionType
AX = mybir.AxisListType

B, T, D = 32, 128, 512
P = 128
KC = D // P
G = 4
NG = B // G
TOK = G * T
RING = 4
FMAX = 3.4028234663852886e38

VECS = ["L0_xattn_bq", "L2_xattn_ln1_w", "L2_xattn_ln1_b", "L2_xattn_ln2_w", "L2_xattn_ln2_b", "L2_xattn_maa_x",
        "L2_xattn_time_decay", "L2_xattn_u", "L2_xattn_gn_w", "L2_xattn_gn_b", "L2_xattn_ffn_maa_k",
        "L2_xattn_ffn_maa_r", "L3_xattn_ln1_w", "L3_xattn_ln1_b", "L3_xattn_q_b", "L3_xattn_k_b",
        "L3_xattn_ln2_w", "L3_xattn_ln2_b", "L3_xattn_fc_b", "L2_xattn_maa_stack"]
ROWS_A = ["L0_xattn_bo", "L0_xattn_gamma", "L0_xattn_beta", "L0_xattn_bv", "L1_xattn_bg"]
ROWS_C = ["L3_xattn_v_b", "L3_xattn_cproj_b", "L3_xattn_proj_b"]


class Turn:

    def __init__(self, reg, mult=1, add=0):
        self.reg, self.mult, self.add = reg, mult, add

    def __add__(self, n):
        return Turn(self.reg, self.mult, self.add + n)

    def times(self, n, more=0):
        return self.add * n + more if self.reg is None else self.reg * (self.mult * n) + (self.add * n + more)

    def exists(self):
        return self.reg is not None or self.add >= 0


class Signal:

    def __init__(self, sem, per):
        self.sem, self.per, self.seen = sem, per, 0

    def up(self, n=1):
        self.seen += n
        return self.sem, n

    def __call__(self, turn, k):
        turn = turn if isinstance(turn, Turn) else Turn(turn)
        return self.sem, turn.times(self.per, self.per + k)

    def all(self, turn):
        return self(turn, self.per)

    def last(self, turn):
        return self(turn, (self.seen - 1) % self.per + 1)

    def before(self, turn, k=None):
        turn = turn if isinstance(turn, Turn) else Turn(turn)
        return self(turn + -1, self.per if k is None else k)


class Ring:

    def __init__(self, items, filled, emptied, banks=RING):
        assert len(items) % banks == 0, len(items)
        self.at = {name: n for n, (name, _) in enumerate(items)}
        self.who = [who for _, who in items]
        self.filled, self.emptied, self.banks = filled, emptied, banks
        self.nth = [self.who[:n + 1].count(w) for n, w in enumerate(self.who)]

    def bank(self, *name):
        return self.at[name] % self.banks

    def ready(self, turn, name, moved=()):
        n = self.at[name] - self.banks
        last = {self.who[n]: self.nth[n] if n >= 0 else self.nth[n] - self.emptied[self.who[n]].per}
        for other in moved:
            n = self.at[other]
            last[self.who[n]] = max(last.get(self.who[n], -10**9), self.nth[n])
        return [self.emptied[w](turn, k) for w, k in last.items()]

    def full(self, turn, *name):
        return self.filled(turn, self.at[name] + 1)

    def full_before(self, turn, *name):
        return self.filled.before(turn, self.at[name] + 1)

    def out(self, turn, *name):
        n = self.at[name]
        return self.emptied[self.who[n]](turn, self.nth[n])


def vec_column(name):
    at = VECS.index(name)
    wide = VECS.index("L3_xattn_fc_b")
    return KC * at if at <= wide else KC * wide + 4 * D // P


def phase_a(nc, dram, stats):
    NH, KVH, HD = 32, 8, 16
    RH = NH // 2
    HV = HD + 1
    NR = 2 * G
    AHEAD = 3
    CI = 64
    items = []
    for c in range(KC):
        items += [(("xT", c), "act"), (("cT", c), "dve")]
    items += [(("q", c), "act") for c in range(KC)] + [(("k", c), "dve") for c in range(KC)]
    items += [(("v", g), "dve") for g in range(G)]
    for n in range(NR):
        items += [(("pT", n, b), "act" if b % 2 else "dve") for b in range(4)] + [(("pv", n), "dve")]
        if n >= 2 and n % 2 == 0:
            items += [(("aT", n // 2 - 1), "act"), (("o", n // 2 - 1), "dve")]
    items += [(("aT", G - 1), "act"), (("o", G - 1), "dve")]
    for g in range(G):
        items += [(("phi", g), "act"), (("th", g), "act"), (("gx", g), "dve")]
    for g in range(G):
        items += [(("fT", g, j), "act" if j % 2 else "dve") for j in range(4)] + [(("y", g), "act"), (("wy", g), "act")]

    with ExitStack() as ctx:
        def sb(name, shape, dt=F32):
            return ctx.enter_context(nc.sbuf_tensor("a_" + name, shape, dt))

        def sig(name, per):
            return Signal(ctx.enter_context(nc.semaphore("a_" + name)), per)

        wq, wo = sb("wq", [P, KC, D]), sb("wo", [P, KC, D])
        wk, wv = sb("wk", [P, KC, 128]), sb("wv", [P, KC, 128])
        wkr = sb("wkr", [P, KC, D])
        wgT, wthT, wphT = sb("wgT", [P, CI]), sb("wthT", [P, CI]), sb("wphT", [P, CI])
        wzT = sb("wzT", [CI, P])
        vec = sb("vec", [P, KC])
        bk = sb("bk", [P, KC])
        ci = sb("ci", [CI, 2])
        bz = sb("bz", [P, 1])
        rows = sb("rows", [P, 3 * D + 128 + CI])
        parity, ident = sb("parity", [P, 2]), sb("ident", [P, P])
        bo, gamma, beta = rows[:, 0:D], rows[:, D:2 * D], rows[:, 2 * D:3 * D]
        bv, bg = rows[:, 3 * D:3 * D + 128], rows[:, 3 * D + 128:]
        half = sb("half", [P, 1])

        x, c_tm, mask = sb("x", [P, G, D]), sb("c", [P, G, D]), sb("mask", [P, G, T])
        xT, cT, qT = sb("xT", [P, KC, TOK]), sb("cT", [P, KC, TOK]), sb("qT", [P, KC, TOK])
        kexp = sb("kexp", [P, KC, 2, TOK])
        v_ext = sb("v_ext", [P, G, KVH, HV])
        S = sb("S", [P, AHEAD, RH, T])
        probsT = sb("probsT", [P, 2, RH, T])
        smax, rden = sb("smax", [P, 2, RH]), sb("rden", [P, 2, RH])
        att, attT = sb("att", [P, 2, D]), sb("attT", [P, KC, TOK])
        xbo, x1 = sb("xbo", [P, G, D]), sb("x1", [P, G, D])
        bn, mv = sb("bn", [P, 6]), sb("mv", [P, 2])
        veps, rstd = sb("veps", [P, 1]), sb("rstd", [P, 1])
        phi, theta = sb("phi", [CI, G, D]), sb("theta", [CI, G, D])
        gx = sb("gx", [P, G, KC, CI])
        nmax, fsum = sb("nmax", [P, 2, KC]), sb("fsum", [P, 2, KC])
        yT, wy = sb("yT", [CI, 2, D]), sb("wy", [P, 2, D])
        f_sb = S[:, 0:2, :, :].rearrange("p a (i k) t -> p a i (k t)", i=KC)
        fT = probsT[:, :, :, :].rearrange("p a (i k) t -> p a i (k t)", i=KC)
        pS = ctx.enter_context(nc.psum_tensor("a_pS", [P, 4, 512], F32))
        pR = ctx.enter_context(nc.psum_tensor("a_pR", [P, RING, 512], F32))

        loaded_w, loaded_rest = sig("loaded_w", 0), sig("loaded_rest", 0)
        x_loaded, c_loaded, mask_loaded = sig("x_loaded", 16), sig("c_loaded", 16), sig("mask_loaded", 16)
        x1_stored, wy_stored = sig("x1_stored", 16 * G), [sig("wy_stored%d" % i, 16 * G // 2) for i in range(2)]
        filled = sig("filled", len(items))
        emptied = {w: sig("emptied_" + w, [i[1] for i in items].count(w)) for w in ("act", "dve")}
        ring = Ring(items, filled, emptied)
        ones_set, wk_wide = sig("ones_set", 0), sig("wk_wide", 0)
        scored, masked = sig("scored", NR + G), sig("masked", NR)
        max_found, centred, exp_done = sig("max_found", NR), sig("centred", NR), sig("exp_done", NR)
        xbo_ready, var_ready, rstd_ready = sig("xbo_ready", 1), sig("var_ready", G), sig("rstd_ready", G)
        whitened, x1_ready = sig("whitened", G), sig("x1_ready", G)
        f_max, f_exp, f_scaled, y_stats = sig("f_max", G), sig("f_exp", G), sig("f_scaled", G), sig("y_stats", G)
        held = sig("held", 0)
        dve_step, pool_step = sig("dve_step", 24), sig("pool_step", G)
        signals = [s for s in locals().values() if isinstance(s, Signal)] + list(emptied.values()) + wy_stored
        x_v, c_v = dram["x"].rearrange("b t d -> t b d"), dram["ctx_2048"].rearrange("b t d -> t b d")
        m_v = dram["mask_Bx1xSxS2_ff0"].rearrange("b o l s -> l (b o) s")
        block = ctx.enter_context(nc.Block())

        @block.sync
        def _(sp):
            for s in signals:
                if s.per:
                    sp.sem_inc(s.sem, s.per)

            def load(turn, tile, src, signal, free):
                if free:
                    sp.wait_ge(*free)
                    sp.sem_inc(held.sem, 1)
                sp.dma_start(tile[:, :, :], src[:, bass.ds(turn.times(G), G), :]).then_inc(*signal.up(16))

            def store_x1(turn):
                for g in range(G):
                    sp.wait_ge(*x1_ready(turn, g + 1))
                    sp.sem_inc(held.sem, 1)
                    sp.dma_start(dram["x1"][bass.ds(turn.times(G, g), 1), :, :].rearrange("b t d -> t (b d)"),
                                 x1[:, g, :]).then_inc(*x1_stored.up(16))

            def store_wy(turn):
                for g in range(G):
                    sp.wait_ge(*ring.out(turn, "wy", g))
                    sp.sem_inc(held.sem, 1)
                    sp.dma_start(dram["wy"][bass.ds(turn.times(G, g), 1), :, :].rearrange("b t d -> t (b d)"),
                                 wy[:, g % 2, :]).then_inc(*wy_stored[g % 2].up(16))

            sp.dma_start(ident[:, :], dram["ident"]).then_inc(*loaded_w.up(16))
            sp.dma_start(wk[:, :, :], dram["L0_xattn_Wk"].rearrange("(k p) n -> p k n", p=P)).then_inc(*loaded_w.up(16))
            load(Turn(None), x, x_v, x_loaded, None)
            load(Turn(None), c_tm, c_v, c_loaded, None)
            for tile, name in [(wq, "L0_xattn_Wq"), (wv, "L0_xattn_Wv"), (wo, "L0_xattn_Wo")]:
                sp.dma_start(tile[:, :, :], dram[name].rearrange("(k p) n -> p k n", p=P)).then_inc(*loaded_rest.up(16))
            for tile, name in [(bk, "bk_wide"), (parity, "parity"), (rows, "rows_a"), (wgT, "L1_WgT"), (wthT, "L1_WthetaT"),
                               (wphT, "L1_WphiT"), (wzT, "L1_WzT"), (ci, "L1_ci"), (bz, "L1_bz")]:
                sp.dma_start(tile[:, :], dram[name]).then_inc(*loaded_rest.up(16))
            sp.dma_start(vec[:, :], dram["vecs"][:, 0:KC]).then_inc(*loaded_rest.up(16))
            load(Turn(None), mask, m_v, mask_loaded, None)
            with sp.Fori(0, NG - 1) as reg:
                turn = Turn(reg)
                load(turn + 1, x, x_v, x_loaded, xbo_ready.all(turn))
                store_x1(turn)
                load(turn + 1, c_tm, c_v, c_loaded, ring.full(turn, "phi", G - 1))
                load(turn + 1, mask, m_v, mask_loaded, masked.all(turn))
                store_wy(turn)
            store_x1(Turn(None, add=NG - 1))
            store_wy(Turn(None, add=NG - 1))
            sp.wait_ge(*x1_stored(NG - 1, 16 * G))
            for half_stored in wy_stored:
                sp.wait_ge(*half_stored(NG - 1, 16 * G // 2))

        def fill(pe, turn, *name, moved=()):
            for wait in ring.ready(turn, name, moved):
                pe.wait_ge(*wait)
            return pR[:, ring.bank(*name), :]

        def post_attention_pe(pe, turn, g):
            bank = fill(pe, turn, "aT", g, moved=[("pv", 2 * g + 1)])
            for c in range(KC):
                mm = nc.tensor.transpose(bank[:, c * P:c * P + P], att[:, g % 2, c * P:c * P + P], ident[:, :])
            mm.then_inc(*filled.up())
            bank = fill(pe, turn, "o", g, moved=[("aT", g)])
            for c in range(KC):
                mm = nc.tensor.matmul(bank[:, :], attT[:, c, g * T:g * T + T], wo[:, c, :], start=(c == 0), stop=(c == KC - 1))
            mm.then_inc(*filled.up())

        @block.tensor
        def _(pe):
            pe.wait_ge(loaded_w.sem, loaded_w.seen)

            def scores(turn, n):
                g, half_ = n // 2, n % 2
                if n:
                    pe.wait_ge(*masked(turn, n))
                else:
                    pe.wait_ge(*f_exp.before(turn))
                for cc in range(2):
                    c = 2 * half_ + cc
                    for r in range(4):
                        rows_ = slice(32 * r, 32 * r + 32)
                        mm = nc.tensor.matmul(pS[:, r, cc * 256:cc * 256 + 256].rearrange("p (a t) -> p a t", a=2), qT[rows_, c, g * T:g * T + T],
                                              kexp[rows_, c, :, g * T:g * T + T], start=True, stop=True)
                mm.then_inc(*scored.up())

            with pe.Fori(0, NG) as turn:
                for c in range(KC):
                    for name, src, ld in (("xT", x, x_loaded), ("cT", c_tm, c_loaded)):
                        bank = fill(pe, turn, name, c)
                        pe.wait_ge(*ld(turn, 16))
                        for g in range(G):
                            mm = nc.tensor.transpose(bank[:, g * T:g * T + T], src[:, g, c * P:c * P + P], ident[:, :])
                        mm.then_inc(*filled.up())
                pe.wait_ge(loaded_rest.sem, loaded_rest.seen)
                pe.wait_ge(wk_wide.sem, KC)
                for name, w, src, ready in (("q", wq, xT, "xT"), ("k", wkr, cT, "cT")):
                    for m in range(KC):
                        bank = fill(pe, turn, name, m, moved=[(ready, KC - 1)])
                        for c in range(KC):
                            mm = nc.tensor.matmul(bank[:, :], w[:, c, m * P:m * P + P], src[:, c, :],
                                                  start=(c == 0), stop=(c == KC - 1))
                        mm.then_inc(*filled.up())
                for g in range(G):
                    bank = fill(pe, turn, "v", g)
                    for c in range(KC):
                        mm = nc.tensor.matmul(bank[:, 0:P], cT[:, c, g * T:g * T + T], wv[:, c, :],
                                              start=(c == 0), stop=(c == KC - 1))
                    mm.then_inc(*filled.up())
                pe.wait_ge(*ring.out(turn, "q", KC - 1))
                pe.wait_ge(*ring.out(turn, "v", G - 1))
                scores(turn, 0)
                scores(turn, 1)
                for n in range(NR):
                    g = n // 2
                    pe.wait_ge(*exp_done(turn, n + 1))
                    for b in range(4):
                        bank = fill(pe, turn, "pT", n, b)
                        for i in range(4):
                            mm = nc.tensor.transpose(bank[:, i * T:i * T + T], S[:, n % AHEAD, 4 * b + i, :], ident[:, :])
                        mm.then_inc(*filled.up())
                    if n + 2 < NR:
                        scores(turn, n + 2)
                    bank = fill(pe, turn, "pv", n, moved=[("pT", n, b) for b in range(4)])
                    for b in range(4):
                        for cc in range(2):
                            for par in range(2):
                                h = cc * 8 + 2 * b + par
                                kv = (n % 2 * RH + h) // (NH // KVH)
                                mm = nc.tensor.matmul(bank[:, h * HV:h * HV + HV], probsT[:, n % 2, 4 * b + 2 * cc + par, :],
                                                      v_ext[:, g, kv, :], start=True, stop=True)
                    mm.then_inc(*filled.up())
                    if n >= 2 and n % 2 == 0:
                        post_attention_pe(pe, turn, n // 2 - 1)
                post_attention_pe(pe, turn, G - 1)

                for g in range(G):
                    bank = fill(pe, turn, "phi", g)
                    nc.tensor.matmul(bank[0:CI, :], wphT[:, :], c_tm[:, g, :], start=True, stop=True).then_inc(*filled.up())
                    bank = fill(pe, turn, "th", g)
                    pe.wait_ge(*x1_ready(turn, g + 1))
                    nc.tensor.matmul(bank[0:CI, :], wthT[:, :], x1[:, g, :], start=True, stop=True).then_inc(*filled.up())
                    bank = fill(pe, turn, "gx", g)
                    for j in range(KC):
                        mm = nc.tensor.matmul(bank[:, j * CI:j * CI + CI], x1[:, g, j * P:j * P + P], wgT[:, :],
                                              start=True, stop=True)
                    mm.then_inc(*filled.up())

                def affinity(g):
                    if g:
                        pe.wait_ge(*f_exp(turn, g))
                    else:
                        pe.wait_ge(*masked(turn, NR))
                    pe.wait_ge(*ring.out(turn, "th", g))
                    for i in range(KC):
                        mm = nc.tensor.matmul(pS[:, i, :], phi[:, g, i * P:i * P + P], theta[:, g, :], start=True, stop=True)
                    mm.then_inc(*scored.up())

                affinity(0)
                for g in range(G):
                    if g + 1 < G:
                        affinity(g + 1)
                    pe.wait_ge(*f_scaled(turn, g + 1))
                    for j in range(KC):
                        bank = fill(pe, turn, "fT", g, j)
                        for i in range(KC):
                            mm = nc.tensor.transpose(bank[:, i * P:i * P + P], f_sb[:, g % 2, i, j * P:j * P + P], ident[:, :])
                        mm.then_inc(*filled.up())
                    bank = fill(pe, turn, "y", g, moved=[("gx", g)] + [("fT", g, j) for j in range(KC)])
                    for j in range(KC):
                        mm = nc.tensor.matmul(bank[0:CI, :], gx[:, g, j, :], fT[:, g % 2, j, :], start=(j == 0), stop=(j == KC - 1))
                    mm.then_inc(*filled.up())
                    bank = fill(pe, turn, "wy", g, moved=[("y", g)])
                    nc.tensor.matmul(bank[:, :], wzT[:, :], yT[:, g % 2, :], start=True, stop=True).then_inc(*filled.up())

        @block.scalar
        def _(act):

            def take(turn, *name):
                act.wait_ge(*ring.full(turn, *name))
                return pR[:, ring.bank(*name), :]

            def exp_round(turn, n):
                act.wait_ge(*centred(turn, n + 1))
                nc.scalar.activation(S[:, n % AHEAD, :, :], S[:, n % AHEAD, :, :], ACT.Exp).then_inc(*exp_done.up())

            def turn_att(turn, g):
                bank = take(turn, "aT", g)
                nc.scalar.activation(attT[:, :, g * T:g * T + T], bank[:, :].rearrange("p (k t) -> p k t", k=KC), ACT.Copy)\
                    .then_inc(*emptied["act"].up())

            with act.Fori(0, NG) as turn:
                for c in range(KC):
                    bank = take(turn, "xT", c)
                    nc.scalar.activation(xT[:, c, :], bank, ACT.Copy).then_inc(*emptied["act"].up())
                act.wait_ge(loaded_rest.sem, loaded_rest.seen)
                act.wait_ge(*scored.before(turn, NR))
                for c in range(KC):
                    bank = take(turn, "q", c)
                    nc.scalar.activation(qT[:, c, :], bank, ACT.Identity, bias=vec[:, c:c + 1]).then_inc(*emptied["act"].up())
                exp_round(turn, 0)
                for n in range(NR):
                    for b in (1, 3):
                        bank = take(turn, "pT", n, b)
                        nc.scalar.activation(probsT[:, n % 2, 4 * b:4 * b + 4, :], bank.rearrange("p (h t) -> p h t", h=4), ACT.Copy)\
                            .then_inc(*emptied["act"].up())
                    if n + 1 < NR:
                        exp_round(turn, n + 1)
                    if n >= 2 and n % 2 == 0:
                        turn_att(turn, n // 2 - 1)
                turn_att(turn, G - 1)
                act.wait_ge(*scored.before(turn, NR + G))
                for g in range(G):
                    bank = take(turn, "phi", g)
                    nc.scalar.activation(phi[:, g, :], bank[0:CI, :], ACT.Identity, bias=ci[:, 0:1]).then_inc(*emptied["act"].up())
                    bank = take(turn, "th", g)
                    nc.scalar.activation(theta[:, g, :], bank[0:CI, :], ACT.Identity, bias=ci[:, 1:2]).then_inc(*emptied["act"].up())

                def exp_f(g):
                    act.wait_ge(*f_max(turn, g + 1))
                    if g >= 2:
                        act.wait_ge(*ring.full(turn, "fT", g - 2, KC - 1))
                    else:
                        act.wait_ge(*ring.full(turn, "pT", NR - 1, 3))
                    for i in range(KC):
                        ins = nc.scalar.activation(f_sb[:, g % 2, i, :], pS[:, i, :], ACT.Exp, bias=nmax[:, g % 2, i:i + 1],
                                                   accum_out=fsum[:, g % 2, i:i + 1])
                    ins.then_inc(*f_exp.up())

                exp_f(0)
                for g in range(G):
                    for j in (1, 3):
                        bank = take(turn, "fT", g, j)
                        nc.scalar.activation(fT[:, g % 2, j, :], bank, ACT.Copy).then_inc(*emptied["act"].up())
                    if g + 1 < G:
                        exp_f(g + 1)
                    bank = take(turn, "y", g)
                    nc.scalar.activation(yT[:, g % 2, :], bank[0:CI, :], ACT.Copy).then_inc(*emptied["act"].up())
                    bank = take(turn, "wy", g)
                    if g >= 2:
                        act.wait_ge(*wy_stored[g % 2](turn, 16))
                        act.wait_ge(*y_stats(turn, g - 1))
                    else:
                        act.wait_ge(*wy_stored[g % 2].before(turn))
                        act.wait_ge(*y_stats.before(turn))
                    nc.scalar.activation(wy[:, g % 2, :], bank, ACT.Identity, bias=bz[:, 0:1]).then_inc(*emptied["act"].up())

        @block.vector
        def _(dve):
            dve.wait_ge(loaded_w.sem, loaded_w.seen)
            nc.vector.memset(v_ext[:, :, :, HD:HV], 1.0).then_inc(*ones_set.up())
            nc.vector.memset(half[:, :], -0.5).then_inc(*ones_set.up())
            for c in range(KC):
                src = wk[:, c, :].rearrange("p (v d) -> p v d", v=KVH).unsqueeze(2).to_broadcast([P, KVH, NH // KVH, HD])
                nc.vector.tensor_copy(wkr[:, c, :].rearrange("p (v g d) -> p v g d", v=KVH, d=HD), src).then_inc(*wk_wide.up())

            def take(turn, *name):
                dve.wait_ge(*ring.full(turn, *name))
                return pR[:, ring.bank(*name), :]

            def softmax_max(turn, n):
                dve.wait_ge(*scored(turn, n + 1))
                if n >= AHEAD:
                    dve.wait_ge(*ring.full(turn, "pT", n - AHEAD, 3))
                else:
                    dve.wait_ge(*ring.full_before(turn, "fT", G - 1, KC - 1))
                nc.vector.scalar_tensor_tensor(out=S[:, n % AHEAD, :, :], in0=pS[:, :, :].rearrange("p r (h t) -> p (r h) t", t=T),
                                               scalar=float(HD) ** -0.5, in1=mask[:, n // 2:n // 2 + 1, :].to_broadcast([P, RH, T]),
                                               op0=ALU.mult, op1=ALU.add).then_inc(*masked.up())
                dve.wait_ge(*masked(turn, n + 1))
                if n >= 2:
                    dve.wait_ge(*centred(turn, n - 1))
                nc.vector.tensor_reduce(smax[:, n % 2, :], S[:, n % AHEAD, :, :], AX.X, ALU.max).then_inc(*max_found.up())

            def normalise(turn, n):
                bank = take(turn, "pv", n)[:, 0:RH * HV].rearrange("p (h e) -> p h e", e=HV)
                nc.vector.reciprocal(rden[:, n % 2, :].unsqueeze(2), bank[:, :, HD:HV]).then_inc(*dve_step.up())
                dve.wait_ge(*dve_step.last(turn))
                nc.vector.tensor_tensor(att[:, n // 2 % 2, n % 2 * 256:n % 2 * 256 + 256].rearrange("p (h d) -> p h d", d=HD),
                                        bank[:, :, 0:HD], rden[:, n % 2, :].unsqueeze(2).to_broadcast([P, RH, HD]), ALU.mult)\
                    .then_inc(*emptied["dve"].up())

            def norm_out(turn, g):
                if g == 0:
                    dve.wait_ge(*xbo_ready(turn, 1))
                bank = take(turn, "o", g)
                nc.vector.tensor_tensor(xbo[:, g, :], bank, xbo[:, g, :], ALU.add).then_inc(*emptied["dve"].up())
                dve.wait_ge(*ring.out(turn, "o", g))
                nc.vector.bn_stats(bn[:, :], xbo[:, g, :]).then_inc(*dve_step.up())
                dve.wait_ge(*dve_step.last(turn))
                dve.sem_inc(held.sem, 1)
                nc.vector.bn_aggr(mv[:, :], bn[:, :]).then_inc(*dve_step.up())
                dve.wait_ge(*dve_step.last(turn))
                nc.vector.tensor_scalar(veps[:, :], mv[:, 1:2], 1e-6, None, ALU.add).then_inc(*var_ready.up())
                dve.wait_ge(*rstd_ready(turn, g + 1))
                nc.vector.tensor_scalar(xbo[:, g, :], xbo[:, g, :], mv[:, 0:1], rstd[:, 0:1], ALU.subtract, ALU.mult)\
                    .then_inc(*whitened.up())

            dve.wait_ge(ones_set.sem, 2)
            with dve.Fori(0, NG) as turn:
                for c in range(KC):
                    bank = take(turn, "cT", c)
                    nc.vector.tensor_copy(cT[:, c, :], bank).then_inc(*emptied["dve"].up())
                dve.wait_ge(loaded_rest.sem, loaded_rest.seen)
                dve.wait_ge(*scored.before(turn, NR))
                for c in range(KC):
                    bank = take(turn, "k", c)
                    nc.vector.tensor_scalar(kexp[:, c, 0, :], bank, bk[:, c:c + 1], parity[:, 0:1], ALU.add, ALU.mult)\
                        .then_inc(*dve_step.up())
                    nc.vector.tensor_scalar(kexp[:, c, 1, :], bank, bk[:, c:c + 1], parity[:, 1:2], ALU.add, ALU.mult)\
                        .then_inc(*emptied["dve"].up())
                for g in range(G):
                    bank = take(turn, "v", g)
                    nc.vector.tensor_tensor(v_ext[:, g, :, 0:HD], bank[:, 0:P].rearrange("p (v d) -> p v d", d=HD),
                                            bv.rearrange("p (v d) -> p v d", d=HD), ALU.add).then_inc(*emptied["dve"].up())
                dve.wait_ge(*mask_loaded(turn, 16))
                softmax_max(turn, 0)
                softmax_max(turn, 1)
                for n in range(NR):
                    for b in (0, 2):
                        bank = take(turn, "pT", n, b)
                        nc.vector.tensor_copy(probsT[:, n % 2, 4 * b:4 * b + 4, :], bank.rearrange("p (h t) -> p h t", h=4))\
                            .then_inc(*emptied["dve"].up())
                    if n + 2 < NR:
                        softmax_max(turn, n + 2)
                    normalise(turn, n)
                    if n >= 2 and n % 2 == 0:
                        norm_out(turn, n // 2 - 1)
                norm_out(turn, G - 1)
                for g in range(G):
                    bank = take(turn, "gx", g)
                    nc.vector.tensor_tensor(gx[:, g, :, :], bank[:, 0:KC * CI].rearrange("p (j o) -> p j o", o=CI),
                                            bg.unsqueeze(1).to_broadcast([P, KC, CI]), ALU.add).then_inc(*emptied["dve"].up())

                def affinity_max(g):
                    dve.wait_ge(*scored(turn, NR + g + 1))
                    nc.vector.tensor_reduce(nmax[:, g % 2, :], pS[:, :, :], AX.X, ALU.max, negate=True).then_inc(*f_max.up())

                affinity_max(0)
                for g in range(G):
                    dve.wait_ge(*f_exp(turn, g + 1))
                    nc.vector.reciprocal(rden[:, g % 2, 0:KC], fsum[:, g % 2, :]).then_inc(*dve_step.up())
                    dve.wait_ge(*dve_step.last(turn))
                    for i in range(KC):
                        ins = nc.vector.tensor_scalar(f_sb[:, g % 2, i, :], f_sb[:, g % 2, i, :], rden[:, g % 2, i:i + 1], None, ALU.mult)
                    ins.then_inc(*f_scaled.up())
                    if g + 1 < G:
                        affinity_max(g + 1)
                    for j in (0, 2):
                        bank = take(turn, "fT", g, j)
                        nc.vector.tensor_copy(fT[:, g % 2, j, :], bank).then_inc(*emptied["dve"].up())
                    dve.wait_ge(*ring.out(turn, "wy", g))
                    nc.vector.bn_stats(stats[:, bass.ds(turn * (G * 6) + g * 6, 6)], wy[:, g % 2, :]).then_inc(*y_stats.up())

        @block.gpsimd
        def _(pool):
            pool.wait_ge(loaded_rest.sem, loaded_rest.seen)
            pool.wait_ge(ones_set.sem, 2)
            with pool.Fori(0, NG) as turn:
                pool.wait_ge(*ring.full(turn, "xT", KC - 1))
                pool.wait_ge(*x1_ready.before(turn))
                nc.gpsimd.tensor_tensor(xbo[:, :, :], x[:, :, :], bo.unsqueeze(1).to_broadcast([P, G, D]), ALU.add).then_inc(*xbo_ready.up())

                def centre(n):
                    pool.wait_ge(*max_found(turn, n + 1))
                    nc.gpsimd.tensor_tensor(S[:, n % AHEAD, :, :], S[:, n % AHEAD, :, :],
                                            smax[:, n % 2, :].unsqueeze(2).to_broadcast([P, RH, T]), ALU.subtract).then_inc(*centred.up())

                def finish(g):
                    pool.wait_ge(*var_ready(turn, g + 1))
                    nc.gpsimd.tensor_tensor(rstd[:, :], veps[:, :], half[:, :], ALU.pow).then_inc(*rstd_ready.up())
                    if g == 0:
                        pool.wait_ge(*x1_stored.before(turn))
                        pool.wait_ge(*ring.full_before(turn, "gx", G - 1))
                    pool.wait_ge(*whitened(turn, g + 1))
                    nc.gpsimd.tensor_tensor(xbo[:, g, :], xbo[:, g, :], gamma, ALU.mult).then_inc(*pool_step.up())
                    pool.wait_ge(*pool_step.last(turn))
                    nc.gpsimd.tensor_tensor(x1[:, g, :], xbo[:, g, :], beta, ALU.add).then_inc(*x1_ready.up())

                centre(0)
                centre(1)
                for n in range(NR):
                    if n + 2 < NR:
                        centre(n + 2)
                    if n >= 2 and n % 2 == 0:
                        finish(n // 2 - 1)
                finish(G - 1)

        wrong = {s.sem.name: (s.per, s.seen) for s in signals if s.per and s.seen % s.per}
        assert not wrong, wrong



def phase_b(nc, dram, norm):
    G = 2
    N = B // G
    TOK = G * T
    NH, HD = 32, 16
    HC = P // HD
    JS = 2
    STEPS = KC * HD // JS
    DM, DD = 32, 64
    LORA = ["k", "w", "v", "r", "g"]
    PROJECT = {0: ["x2"], 1: ["stats"], 3: ["whiten"], 5: ["n1"], 6: ["shift"], 9: ["h"], 10: ["m0"], 11: ["m1"], 12: ["k0"], 13: ["k1"],
               14: ["m2"], 15: ["td"], 16: ["m3"], 17: ["w"], 18: ["v0"], 20: ["v1"], 22: ["vT"], 24: ["m4"], 26: ["r0"], 28: ["r1"],
               30: ["g0"], 31: ["save"]}
    LATE = {0: ["g1"], 1: ["u"]}
    FINISH = {0: ["gn_mean"], 1: ["gn_var"], 2: ["gn_div"], 4: ["gate"], 6: ["o0"], 7: ["o1"], 8: ["stats"], 10: ["whiten"], 12: ["n2"],
              13: ["shift"], 16: ["fk0"], 19: ["fk1"], 21: ["fr0"], 23: ["fr1"], 25: ["fv0"], 27: ["fv1"]}
    p_items = [(("n1", 0), "act"), (("n1", 1), "act"), (("h", 0), "act"), (("h", 1), "act")]
    for name in ("m0", "m1", "k", "m2", "td", "m3", "w", "v", "vT", "m4", "r", "g", "u"):
        who = "dve" if name[0] in "mg" or name == "vT" else "act"
        p_items += [((name, 0), who)] + ([((name, 1), who)] if name not in ("td", "u") else [])
    f_items = [((name, h), who) for name, who in (("gn", "act"), ("o", "dve"), ("n2", "act"), ("fk", "act"), ("fr", "act"), ("fv", "dve"))
               for h in range(2)]
    s_items = [(("v", n), "dve") for n in range(STEPS)]

    with ExitStack() as ctx:
        def sb(name, shape, dt=F32):
            return ctx.enter_context(nc.sbuf_tensor("b_" + name, shape, dt))

        def sig(name, per):
            return Signal(ctx.enter_context(nc.semaphore("b_" + name)), per)

        def pair(name, shape, dt=F32):
            return [sb(name + str(i), shape, dt) for i in range(2)]

        W = {n: sb("w" + n, [P, KC, D]) for n in ("Wk", "Wv", "Wr", "Wg", "Wo", "Wfk", "Wfr", "Wfv")}
        w1, w2a, w2b = sb("w1", [P, KC, 5 * DM]), sb("w2a", [P, D]), sb("w2b", [DM, D])
        td1, td2 = sb("td1", [P, KC, DD]), sb("td2", [DD, D])
        vec = sb("vec", [P, dram["vecs"].shape[1]])
        ident, heads, pick = sb("ident", [P, P]), sb("heads", [P, HC]), sb("pick", [P, HD, P], F32R)
        half = sb("half", [P, 1])
        state = sb("state", [P, B, 2, KC])

        def col(name, c, j=0):
            at = vec_column(name) + KC * j + c
            return vec[:, at:at + 1]

        x1g, wyg, x2 = sb("x1g", [P, G, D]), sb("wyg", [P, G, D]), pair("x2", [P, G, D])
        xn = [sb("xn0", [P, G, D]), sb("xn1", [P, G, D])]
        xT = [sb("xT0", [P, KC, G, T + 1]), sb("xT1", [P, KC, G, T + 1])]
        sx = [sb("sx0", [P, KC, TOK]), sb("sx1", [P, KC, TOK])]
        xm = [sb("xm0", [P, KC, TOK]), sb("xm1", [P, KC, TOK])]
        hid = sb("hid", [P, TOK])
        kT, wT, rT, gT = (pair(n, [P, KC, TOK]) for n in ("kT", "wT", "rT", "gT"))
        v_tm, v_hi, v_lo = pair("v_tm", [P, G, D]), pair("v_hi", [P, KC, TOK], F32R), pair("v_lo", [P, KC, TOK], F32R)
        usum, s0 = pair("usum", [P, G, NH]), pair("s0", [P, KC, G, HD])
        a_kv, S = sb("a_kv", [P, 2, JS, TOK]), sb("S", [P, 2, JS, G, T + 1])
        o, z = sb("o", [P, G, D]), sb("z", [P, KC, TOK])
        bn, mv = [sb("bn0", [P, G, 6]), sb("bn1", [P, G, 6])], [sb("mv0", [P, G, 2]), sb("mv1", [P, G, 2])]
        veps, rstd = [sb("veps0", [P, G]), sb("veps1", [P, G])], [sb("rstd0", [P, G]), sb("rstd1", [P, G])]
        gsum, grstd = sb("gsum", [P, G * NH]), sb("grstd", [P, G * NH])
        gvar = gsum
        flat = [t[:, :, :].rearrange("p g d -> p (g d)").rearrange("p (k n) -> p k n", k=KC) for t in xn]
        u0 = ruk = flat[0]
        hid4, th = x1g[0:DM, 0, 0:TOK], x1g[0:DD, 1, 0:TOK]
        rs = a_kv
        xr, xk = flat[1], z
        rt = sx[1][:, :, :].rearrange("p k n -> p (k n)").rearrange("p (g d) -> p g d", g=G)
        kk = xT[1][:, :, :, :].rearrange("p k g t -> p (k g t)")[:, 0:KC * TOK].rearrange("p (k n) -> p k n", k=KC)
        sq = z[:, :, :].rearrange("p k n -> p (k n)")
        gnewt = sq[:, 0:G * NH]
        pO = ctx.enter_context(nc.psum_tensor("b_pO", [P, G, 512], F32))
        pS, pP, pF = (ctx.enter_context(nc.psum_tensor("b_p" + n, [P, 2, 512], F32)) for n in "SPF")

        def ring_of(name, items):
            emptied = {w: sig(name + "_emptied_" + w, k) for w in ("act", "dve") for k in [[i[1] for i in items].count(w)] if k}
            return Ring(items, sig(name + "_filled", len(items)), emptied, banks=2)

        loaded_w, loaded_k, loaded_v, loaded_f, consts, held = (sig(n, 0) for n in ("loaded_w", "loaded_k", "loaded_v", "loaded_f", "consts", "held"))
        y_loaded, s0_loaded, stored = sig("y_loaded", 32), sig("s0_loaded", 16), sig("stored", 16 * G)
        P_, F_, S_ = ring_of("p", p_items), ring_of("f", f_items), ring_of("s", s_items)
        wy_normed, x2_ready, x2_saved = sig("wy_normed", G), sig("x2_ready", G), sig("x2_saved", 1)
        var_ready, rstd_ready, xn_ready, first_set, shifted = ([sig(n + str(i), k) for i in range(2)] for n, k in
                                                               (("var", 1), ("rstd", 1), ("xn", G), ("first", 1), ("shifted", 1)))
        u0_ready, xm_ready = sig("u0_ready", 1), sig("xm_ready", 2 * len(LORA))
        decay_ready, v_hi_ready, tanh_g, ruk_ready = sig("decay", 2), sig("v_hi_ready", 2), sig("tanh_g", 2), sig("ruk", 1)
        s_first, scanned, rs_ready, summed = (sig(n, STEPS) for n in ("s_first", "scanned", "rs_ready", "summed"))
        own_ready, out_ready = sig("own", 1), sig("out_ready", 1)
        gn_centred, gn_squared, gn_var, gn_root, gn_ready = (sig("gn" + n, 1) for n in ("c", "s", "v", "r", "o"))
        z_ready, xk_ready, xr_ready = sig("z_ready", 2), sig("xk_ready", 1), sig("xr_ready", 1)
        squared, x4_ready = sig("squared", 2), sig("x4_ready", G)
        gn_step, ln_step = sig("gn_step", 7), [sig("ln_step%d" % i, 2 * G) for i in range(2)]
        signals = [loaded_w, loaded_k, loaded_v, loaded_f, consts, held, y_loaded, s0_loaded, stored, wy_normed, x2_ready, x2_saved, u0_ready, xm_ready, decay_ready, v_hi_ready, tanh_g,
                   ruk_ready, s_first, scanned, rs_ready, summed, own_ready, out_ready, gn_centred, gn_squared, gn_var, gn_root, gn_ready,
                   z_ready, xk_ready, xr_ready, squared, x4_ready, gn_step] + ln_step + var_ready + rstd_ready + xn_ready + first_set + shifted
        for ring in (P_, F_, S_):
            signals += [ring.filled] + list(ring.emptied.values())
        x1_v, wy_v = dram["x1"].rearrange("b t d -> t b d"), dram["wy"].rearrange("b t d -> t b d")
        block = ctx.enter_context(nc.Block())

        def fill(pe, ring, psum, turn, *name, moved=()):
            for wait in ring.ready(turn, name, moved):
                pe.wait_ge(*wait)
            return psum[:, ring.bank(*name), :]

        def take(eng, ring, psum, turn, *name):
            eng.wait_ge(*ring.full(turn, *name))
            return psum[:, ring.bank(*name), :]

        def run(eng, scan, project, finish):
            def turn(i, par, last, next_):
                for n in range(STEPS):
                    scan(i, par, n)
                    for s in LATE.get(n, ()):
                        project(i, par, s)
                    for s in FINISH.get(n, ()) if last else ():
                        finish(i + -1, 1 - par, s)
                    for s in PROJECT.get(n, ()) if next_ else ():
                        project(i + 1, 1 - par, s)
                scan(i, par, STEPS)

            for steps in PROJECT.values():
                for s in steps:
                    project(Turn(None), 0, s)
            turn(Turn(None), 0, False, True)
            with eng.Fori(0, (N - 2) // 2) as reg:
                for u in range(2):
                    turn(Turn(reg, 2, 1 + u), (1 + u) % 2, True, True)
            turn(Turn(None, add=N - 1), (N - 1) % 2, True, False)
            for steps in FINISH.values():
                for s in steps:
                    finish(Turn(None, add=N - 1), (N - 1) % 2, s)

        @block.sync
        def _(sp):
            for s in signals:
                if s.per:
                    sp.sem_inc(s.sem, s.per)

            def wait(value):
                sp.wait_ge(*value)
                sp.sem_inc(held.sem, 1)

            def load(i):
                if (i + -1).exists():
                    wait(x2_saved.all(i + -1))
                sp.dma_start(x1g[:, :, :], x1_v[:, bass.ds(i.times(G), G), :]).then_inc(*y_loaded.up(16))
                sp.dma_start(wyg[:, :, :], wy_v[:, bass.ds(i.times(G), G), :]).then_inc(*y_loaded.up(16))

            def load_state(i, par):
                if (i + -2).exists():
                    wait(rs_ready.all(i + -2))
                sp.dma_start(s0[par][:, :, :, :], dram["state_heads"][:, bass.ds(i.times(KC), KC), :, :]).then_inc(*s0_loaded.up(16))

            def store(i, par):
                for g in range(G):
                    wait(x4_ready(i, g + 1))
                    sp.dma_start(dram["x4"][bass.ds(i.times(G, g), 1), :, :].rearrange("b t d -> t (b d)"), x2[par][:, g, :])\
                        .then_inc(*stored.up(16))

            for tile, name in [(vec, "vecs"), (ident, "ident"), (heads, "heads")]:
                sp.dma_start(tile[:, :], dram[name]).then_inc(*loaded_w.up(16))
            sp.dma_start(state[:, :, :, :], dram["state_rows"]).then_inc(*loaded_w.up(16))
            for h in range(2):
                sp.dma_start(xm[h][:, :, :].rearrange("p k n -> p (k n)"), dram["pick"][:, h * KC * TOK:(h + 1) * KC * TOK]).then_inc(*loaded_w.up(16))
            load(Turn(None))
            load_state(Turn(None), 0)
            load_state(Turn(None, add=1), 1)

            def load_weights(signal, tile, name):
                sp.dma_start(tile[:, :, :], dram[name].rearrange("(k p) n -> p k n", p=P)).then_inc(*signal.up(16))

            load_weights(loaded_k, w1, "L2_xattn_maa_w1")
            w2 = dram["L2_xattn_maa_w2"].rearrange("f d e -> (f d) e")
            for tile, src in [(w2a, w2[0:4 * DM, :]), (w2b, w2[4 * DM:5 * DM, :]), (td2, dram["L2_xattn_td_w2"])]:
                sp.dma_start(tile[:, :], src).then_inc(*loaded_k.up(16))
            load_weights(loaded_k, W["Wk"], "L2_WkT")
            load_weights(loaded_v, td1, "L2_xattn_td_w1")
            for signal, n in [(loaded_v, "Wv"), (loaded_v, "Wr"), (loaded_v, "Wg"), (loaded_f, "Wo"), (loaded_f, "Wfk"), (loaded_f, "Wfr"),
                              (loaded_f, "Wfv")]:
                load_weights(signal, W[n], "L2_%sT" % n)
            load(Turn(None, add=1))
            load(Turn(None, add=2))
            load_state(Turn(None, add=2), 0)
            with sp.Fori(0, (N - 4) // 2) as reg:
                for u in range(2):
                    i = Turn(reg, 2, 1 + u)
                    store(i + -1, u % 2)
                    load(i + 2)
                    load_state(i + 2, (1 + u) % 2)
            store(Turn(None, add=N - 4), 0)
            load(Turn(None, add=N - 1))
            load_state(Turn(None, add=N - 1), 1)
            for i in range(N - 3, N):
                store(Turn(None, add=i), i % 2)
            sp.wait_ge(*stored.all(Turn(None, add=N - 1)))

        @block.tensor
        def _(pe):
            pe.wait_ge(loaded_w.sem, loaded_w.seen)
            pe.wait_ge(consts.sem, 3)

            def two_chunks(ring, psum, i, name, h, w, src, moved=()):
                bank = fill(pe, ring, psum, i, name, h, moved=moved)
                for m in range(2):
                    at = (2 * h + m) * P
                    for c in range(KC):
                        mm = nc.tensor.matmul(bank[:, m * TOK:m * TOK + TOK], w[:, c, at:at + P], src[:, c, :],
                                              start=(c == 0), stop=(c == KC - 1))
                mm.then_inc(*ring.filled.up())

            def tokens(ring, psum, i, name, g, w, src):
                bank = fill(pe, ring, psum, i, name, g)
                for c in range(KC):
                    mm = nc.tensor.matmul(bank, src[:, c, g * T:g * T + T], w[:, c, :], start=(c == 0), stop=(c == KC - 1))
                mm.then_inc(*ring.filled.up())

            def turned(ring, psum, i, name, src):
                for h in range(2):
                    bank = fill(pe, ring, psum, i, name, h)
                    for m in range(2):
                        for g in range(G):
                            mm = nc.tensor.transpose(bank[:, (m * G + g) * T:(m * G + g + 1) * T],
                                                     src[:, g, (2 * h + m) * P:(2 * h + m + 1) * P], ident[:, :])
                    mm.then_inc(*ring.filled.up())

            def project(i, par, s):
                if s == "n1":
                    pe.wait_ge(*xn_ready[0].all(i))
                    turned(P_, pP, i, "n1", xn[0])
                elif s == "h":
                    pe.wait_ge(loaded_k.sem, loaded_k.seen)
                    pe.wait_ge(*u0_ready(i, 1))
                    for k, (lo, size) in enumerate(((0, 4 * DM), (4 * DM, DM))):
                        bank = fill(pe, P_, pP, i, "h", k)
                        for c in range(KC):
                            mm = nc.tensor.matmul(bank[0:size, 0:TOK], w1[:, c, lo:lo + size], u0[:, c, :], start=(c == 0), stop=(c == KC - 1))
                        mm.then_inc(*P_.filled.up())
                elif s[0] == "m":
                    j = int(s[1])
                    for h in range(2):
                        bank = fill(pe, P_, pP, i, s, h, moved=[("h", 1)])
                        for m in range(2):
                            at = (2 * h + m) * P
                            w, src = (w2a[j * DM:j * DM + DM, at:at + P], hid[j * DM:j * DM + DM, :]) if j < 4 else (w2b[:, at:at + P], hid4)
                            mm = nc.tensor.matmul(bank[:, m * TOK:m * TOK + TOK], w, src, start=True, stop=True)
                        mm.then_inc(*P_.filled.up())
                elif s[0] in "krg":
                    j = LORA.index(s[0])
                    pe.wait_ge(*xm_ready(i, 2 * j + 2))
                    two_chunks(P_, pP, i, s[0], int(s[1]), W["W" + s[0]], xm[j % 2])
                elif s == "vT":
                    pe.wait_ge(*P_.out(i, "v", 1))
                    turned(P_, pP, i, "vT", v_tm[par])
                elif s[0] == "v":
                    pe.wait_ge(*xm_ready(i, 6))
                    tokens(P_, pP, i, "v", int(s[1]), W["Wv"], xm[0])
                elif s == "td":
                    pe.wait_ge(loaded_v.sem, loaded_v.seen)
                    pe.wait_ge(*xm_ready(i, 4))
                    bank = fill(pe, P_, pP, i, "td", 0)
                    for c in range(KC):
                        mm = nc.tensor.matmul(bank[0:DD, 0:TOK], td1[:, c, :], xm[1][:, c, :], start=(c == 0), stop=(c == KC - 1))
                    mm.then_inc(*P_.filled.up())
                elif s == "w":
                    for h in range(2):
                        bank = fill(pe, P_, pP, i, "w", h, moved=[("td", 0)])
                        for m in range(2):
                            at = (2 * h + m) * P
                            mm = nc.tensor.matmul(bank[:, m * TOK:m * TOK + TOK], td2[:, at:at + P], th, start=True, stop=True)
                        mm.then_inc(*P_.filled.up())
                elif s == "u":
                    bank = fill(pe, P_, pP, i, "u", 0)
                    pe.wait_ge(*ruk_ready(i, 1))
                    for g in range(G):
                        for c in range(KC):
                            at = g * NH + c * HC
                            mm = nc.tensor.matmul(bank[:, at:at + HC], ruk[:, c, g * T:g * T + T], heads[:, :], start=True, stop=True)
                    mm.then_inc(*P_.filled.up())

            def spread(i, par, n):
                c, j = divmod(n * JS, HD)
                bank = fill(pe, S_, pS, i, "v", n)
                for m in range(JS):
                    nc.tensor.matmul(bank[:, m * TOK:m * TOK + TOK], pick[:, j + m, :], v_hi[par][:, c, :], start=True, stop=False)
                    mm = nc.tensor.matmul(bank[:, m * TOK:m * TOK + TOK], pick[:, j + m, :], v_lo[par][:, c, :], start=False, stop=True)
                mm.then_inc(*S_.filled.up())

            def scan(i, par, n):
                if n == 0:
                    pe.wait_ge(*P_.out(i, "vT", 1))
                    spread(i, par, 0)
                if n + 1 < STEPS:
                    spread(i, par, n + 1)
                if n == 0:
                    return
                if n == 1 and (i + -1).exists():
                    pe.wait_ge(*out_ready(i + -1, 1))
                pe.wait_ge(*rs_ready(i, n))
                for m in range(JS):
                    for g in range(G):
                        at = ((n - 1) * JS + m) * HC
                        mm = nc.tensor.matmul(pO[:, g, at:at + HC], rs[:, (n - 1) % 2, m, g * T:g * T + T], heads[:, :], start=True, stop=True)
                mm.then_inc(*summed.up())

            def finish(i, par, s):
                if s == "gate":
                    pe.wait_ge(loaded_f.sem, loaded_f.seen)
                    pe.wait_ge(*gn_ready(i, 1))
                    turned(F_, pF, i, "gn", o)
                elif s[0] == "o":
                    pe.wait_ge(*z_ready(i, 2))
                    tokens(F_, pF, i, "o", int(s[1]), W["Wo"], z)
                elif s == "n2":
                    pe.wait_ge(*xn_ready[1].all(i))
                    turned(F_, pF, i, "n2", xn[1])
                elif s[:2] == "fk":
                    pe.wait_ge(*xk_ready(i, 1))
                    two_chunks(F_, pF, i, "fk", int(s[2]), W["Wfk"], xk)
                elif s[:2] == "fr":
                    pe.wait_ge(*xr_ready(i, 1))
                    tokens(F_, pF, i, "fr", int(s[2]), W["Wfr"], xr)
                elif s[:2] == "fv":
                    pe.wait_ge(*squared(i, 2))
                    tokens(F_, pF, i, "fv", int(s[2]), W["Wfv"], kk)

            run(pe, scan, project, finish)

        @block.scalar
        def _(act):
            act.wait_ge(loaded_w.sem, loaded_w.seen)

            def affine_norm(ring, psum, i, k, free):
                ln = "L2_xattn_ln%d" % (k + 1)
                if (i + -1).exists():
                    act.wait_ge(*free.all(i + -1))
                nc.scalar.activation(xT[k][:, :, :, 0:1], state[:, bass.ds(i.times(G), G), 1 - k, :].rearrange("p g k -> p k g").unsqueeze(3), ACT.Copy)\
                    .then_inc(*first_set[k].up())
                for h in range(2):
                    bank = take(act, ring, psum, i, "n%d" % (k + 1), h)
                    for m in range(2):
                        c = 2 * h + m
                        ins = nc.scalar.activation(xT[k][:, c, :, 1:T + 1], bank[:, m * TOK:m * TOK + TOK].rearrange("p (g t) -> p g t", g=G),
                                                   ACT.Identity, bias=col(ln + "_b", c), scale=col(ln + "_w", c))
                    ins.then_inc(*ring.emptied["act"].up())

            def project(i, par, s):
                if s == "x2":
                    act.wait_ge(*y_loaded.all(i))
                    for g in range(G):
                        nc.scalar.activation(wyg[:, g, :], wyg[:, g, :], ACT.Identity, bias=norm[:, 1:2], scale=norm[:, 0:1]).then_inc(*wy_normed.up())
                elif s == "n1":
                    affine_norm(P_, pP, i, 0, xm_ready)
                elif s == "h":
                    for k, tile in enumerate((hid[:, :], hid4)):
                        bank = take(act, P_, pP, i, "h", k)
                        nc.scalar.activation(tile, bank[0:tile.shape[0], 0:TOK], ACT.Tanh).then_inc(*P_.emptied["act"].up())
                elif s[0] in "kr":
                    h = int(s[1])
                    bank = take(act, P_, pP, i, s[0], h)
                    if h == 0 and (i + -2).exists():
                        act.wait_ge(*rs_ready.all(i + -2))
                    dst = (kT if s[0] == "k" else rT)[par]
                    nc.scalar.activation(dst[:, 2 * h:2 * h + 2, :], bank.rearrange("p (m n) -> p m n", m=2), ACT.Copy)\
                        .then_inc(*P_.emptied["act"].up())
                elif s == "td":
                    bank = take(act, P_, pP, i, "td", 0)
                    nc.scalar.activation(th, bank[0:DD, 0:TOK], ACT.Tanh).then_inc(*P_.emptied["act"].up())
                elif s == "w":
                    for h in range(2):
                        bank = take(act, P_, pP, i, "w", h)
                        for m in range(2):
                            c = 2 * h + m
                            ins = nc.scalar.activation(wT[par][:, c, :], bank[:, m * TOK:m * TOK + TOK], ACT.Exp, bias=col("L2_xattn_time_decay", c))
                        ins.then_inc(*P_.emptied["act"].up())
                    act.wait_ge(*P_.out(i, "w", 1))
                    for h in range(2):
                        nc.scalar.activation(wT[par][:, 2 * h:2 * h + 2, :], wT[par][:, 2 * h:2 * h + 2, :], ACT.Exp, scale=-1.0).then_inc(*decay_ready.up())
                elif s == "vT":
                    for h in range(2):
                        bank = take(act, P_, pP, i, "vT", h)
                        nc.scalar.activation(v_hi[par][:, 2 * h:2 * h + 2, :], bank.rearrange("p (m n) -> p m n", m=2), ACT.Copy)\
                            .then_inc(*v_hi_ready.up())
                elif s[0] == "v":
                    g = int(s[1])
                    bank = take(act, P_, pP, i, "v", g)
                    if g == 0 and (i + -2).exists():
                        act.wait_ge(*out_ready.all(i + -2))
                    nc.scalar.activation(v_tm[par][:, g, :], bank, ACT.Copy).then_inc(*P_.emptied["act"].up())
                elif s[0] == "g":
                    h = int(s[1])
                    bank = take(act, P_, pP, i, "g", h)
                    if h == 0 and (i + -2).exists():
                        act.wait_ge(*z_ready.all(i + -2))
                    nc.scalar.activation(gT[par][:, 2 * h:2 * h + 2, :], bank.rearrange("p (m n) -> p m n", m=2), ACT.Tanh, scale=0.5)\
                        .then_inc(*tanh_g.up())
                elif s == "u":
                    bank = take(act, P_, pP, i, "u", 0)
                    nc.scalar.activation(usum[par][:, :, :], bank[:, 0:G * NH].rearrange("p (g h) -> p g h", g=G), ACT.Copy)\
                        .then_inc(*P_.emptied["act"].up())

                elif s == "save":
                    if (i + -2).exists():
                        act.wait_ge(*stored.all(i + -2))
                    act.wait_ge(*x2_ready.all(i))
                    nc.scalar.activation(x2[par][:, :, :], wyg[:, :, :], ACT.Copy).then_inc(*x2_saved.up())

            def scan(i, par, n):
                if n == STEPS:
                    return
                if n == 0:
                    act.wait_ge(*s0_loaded.all(i))
                c, j = divmod(n * JS, HD)
                if n >= 2 or (i + -1).exists():
                    act.wait_ge(*(rs_ready(i, n - 1) if n >= 2 else rs_ready(i + -1, STEPS - 1 + n)))
                nc.scalar.activation(S[:, n % 2, :, :, 0:1], s0[par][:, c, :, j:j + JS].rearrange("p g j -> p j g").unsqueeze(3), ACT.Copy).then_inc(*s_first.up())

            def finish(i, par, s):
                if s == "gn_mean":
                    act.wait_ge(*gn_centred(i, 1))
                    if (i + -1).exists():
                        act.wait_ge(*F_.full(i + -1, "fk", 1))
                    nc.scalar.activation(sq, o[:, :, :].rearrange("p g d -> p (g d)"), ACT.Square).then_inc(*gn_squared.up())
                elif s == "gn_var":
                    act.wait_ge(*gn_var(i, 1))
                    nc.scalar.activation(grstd[:, :], gvar[:, :], ACT.Sqrt).then_inc(*gn_root.up())
                elif s == "gate":
                    act.wait_ge(*gn_var(i, 1))
                    for h in range(2):
                        bank = take(act, F_, pF, i, "gn", h)
                        for m in range(2):
                            c = 2 * h + m
                            ins = nc.scalar.activation(z[:, c, :], bank[:, m * TOK:m * TOK + TOK], ACT.Identity,
                                                       bias=col("L2_xattn_gn_b", c), scale=col("L2_xattn_gn_w", c))
                        ins.then_inc(*F_.emptied["act"].up())
                elif s == "n2":
                    affine_norm(F_, pF, i, 1, x4_ready)
                elif s[:2] == "fk":
                    h = int(s[2])
                    bank = take(act, F_, pF, i, "fk", h)
                    if h == 0:
                        act.wait_ge(*xr_ready(i, 1))
                    nc.scalar.activation(kk[:, 2 * h:2 * h + 2, :], bank.rearrange("p (m n) -> p m n", m=2), ACT.Relu).then_inc(*F_.emptied["act"].up())
                    act.wait_ge(*F_.out(i, "fk", h))
                    nc.scalar.activation(kk[:, 2 * h:2 * h + 2, :], kk[:, 2 * h:2 * h + 2, :], ACT.Square).then_inc(*squared.up())
                elif s[:2] == "fr":
                    g = int(s[2])
                    bank = take(act, F_, pF, i, "fr", g)
                    nc.scalar.activation(rt[:, g, :], bank, ACT.Tanh, scale=0.5).then_inc(*F_.emptied["act"].up())

            run(act, scan, project, finish)

        @block.vector
        def _(dve):
            dve.wait_ge(loaded_w.sem, loaded_w.seen)
            nc.vector.memset(half[:, :], -0.5).then_inc(*consts.up())
            for h in range(2):
                nc.vector.tensor_copy(pick[:, h * HD // 2:(h + 1) * HD // 2, :], xm[h][:, :, :].rearrange("p k n -> p (k n)").rearrange("p (j q) -> p j q", q=P))\
                    .then_inc(*consts.up())
            dve.wait_ge(consts.sem, 3)

            def statistics(i, x, k):
                for g in range(G):
                    nc.vector.bn_stats(bn[k][:, g, :], x[:, g, :]).then_inc(*ln_step[k].up())
                dve.wait_ge(*ln_step[k].last(i))
                dve.sem_inc(held.sem, 1)
                for g in range(G):
                    nc.vector.bn_aggr(mv[k][:, g, :], bn[k][:, g, :]).then_inc(*ln_step[k].up())
                dve.wait_ge(*ln_step[k].last(i))
                nc.vector.tensor_scalar(veps[k][:, :].unsqueeze(2), mv[k][:, :, 1:2], 1e-5, None, ALU.add).then_inc(*var_ready[k].up())

            def whiten(i, x, k):
                dve.wait_ge(*rstd_ready[k](i, 1))
                for g in range(G):
                    nc.vector.tensor_scalar(xn[k][:, g, :], x[:, g, :], mv[k][:, g, 0:1], rstd[k][:, g:g + 1], ALU.subtract, ALU.mult)\
                        .then_inc(*xn_ready[k].up())

            def shift(ring, i, k):
                dve.wait_ge(*first_set[k](i, 1))
                dve.wait_ge(*ring.out(i, "n%d" % (k + 1), 1))
                nc.vector.tensor_tensor(sx[k][:, :, :].rearrange("p k (g t) -> p (k g) t", g=G), xT[k][:, :, :, 0:T].rearrange("p k g t -> p (k g) t"),
                                        xT[k][:, :, :, 1:T + 1].rearrange("p k g t -> p (k g) t"), ALU.subtract).then_inc(*shifted[k].up())
                dve.wait_ge(*shifted[k](i, 1))

            def mix(dst, name, k):
                for c in range(KC):
                    ins = nc.vector.scalar_tensor_tensor(out=dst[:, c, :].rearrange("p (g t) -> p g t", g=G),
                                                         in0=sx[k][:, c, :].rearrange("p (g t) -> p g t", g=G), scalar=col(name, c),
                                                         in1=xT[k][:, c, :, 1:T + 1], op0=ALU.mult, op1=ALU.add)
                return ins

            def project(i, par, s):
                if s == "stats":
                    dve.wait_ge(*x2_ready.all(i))
                    statistics(i, wyg, 0)
                elif s == "whiten":
                    if (i + -1).exists():
                        dve.wait_ge(*P_.full(i + -1, "u", 0))
                    whiten(i, wyg, 0)
                elif s == "shift":
                    if (i + -1).exists():
                        dve.wait_ge(*xm_ready.all(i + -1))
                    shift(P_, i, 0)
                    mix(u0, "L2_xattn_maa_x", 0).then_inc(*u0_ready.up())
                elif s[0] == "m":
                    j = int(s[1])
                    for h in range(2):
                        bank = take(dve, P_, pP, i, s, h)
                        for m in range(2):
                            c = 2 * h + m
                            ins = nc.vector.scalar_tensor_tensor(out=xm[j % 2][:, c, :], in0=bank[:, m * TOK:m * TOK + TOK],
                                                                 scalar=col("L2_xattn_maa_stack", c, j), in1=sx[0][:, c, :], op0=ALU.add, op1=ALU.mult)
                        ins.then_inc(*P_.emptied["dve"].up())
                elif s == "vT":
                    for h in range(2):
                        bank = take(dve, P_, pP, i, "vT", h)
                        dve.wait_ge(*v_hi_ready(i, h + 1))
                        nc.vector.tensor_tensor(v_lo[par][:, 2 * h:2 * h + 2, :], bank.rearrange("p (m n) -> p m n", m=2),
                                                v_hi[par][:, 2 * h:2 * h + 2, :].bitcast(F32), ALU.subtract).then_inc(*P_.emptied["dve"].up())
                elif s[0] == "g":
                    h = int(s[1])
                    bank = take(dve, P_, pP, i, "g", h)
                    dve.wait_ge(*tanh_g(i, h + 1))
                    gate = gT[par][:, 2 * h:2 * h + 2, :].rearrange("p m n -> p (m n)")
                    nc.vector.scalar_tensor_tensor(out=gate, in0=gate, scalar=1.0, in1=bank, op0=ALU.add, op1=ALU.mult).then_inc(*P_.emptied["dve"].up())
                elif s == "u":
                    dve.wait_ge(*P_.out(i, "r", 1))
                    for c in range(KC):
                        ins = nc.vector.scalar_tensor_tensor(out=ruk[:, c, :], in0=rT[par][:, c, :], scalar=col("L2_xattn_u", c), in1=kT[par][:, c, :],
                                                             op0=ALU.mult, op1=ALU.mult)
                    ins.then_inc(*ruk_ready.up())

            def scan(i, par, n):
                if n == 0:
                    dve.wait_ge(*decay_ready.all(i))
                    dve.wait_ge(*s0_loaded.all(i))
                if n < STEPS:
                    c, j = divmod(n * JS, HD)
                    bank = take(dve, S_, pS, i, "v", n)
                    if n >= 2 or (i + -1).exists():
                        dve.wait_ge(*(summed(i, n - 1) if n >= 2 else summed(i + -1, STEPS - 1 + n)))
                    nc.vector.tensor_tensor(a_kv[:, n % 2, :, :], kT[par][:, c, :].unsqueeze(1).to_broadcast([P, JS, TOK]),
                                            bank.rearrange("p (j n) -> p j n", j=JS), ALU.mult).then_inc(*S_.emptied["dve"].up())
                    dve.wait_ge(*S_.out(i, "v", n))
                    if n >= 2 or (i + -1).exists():
                        dve.wait_ge(*(rs_ready(i, n - 1) if n >= 2 else rs_ready(i + -1, STEPS - 1 + n)))
                    for m in range(JS):
                        for g in range(G):
                            ins = nc.vector.tensor_tensor_scan(S[:, n % 2, m, g, 1:T + 1], wT[par][:, c, g * T:g * T + T],
                                                               a_kv[:, n % 2, m, g * T:g * T + T], s0[par][:, c, g, j + m:j + m + 1], ALU.mult, ALU.add)
                    ins.then_inc(*scanned.up())
                    return
                if (i + -1).exists():
                    dve.wait_ge(*F_.full(i + -1, "gn", 1))
                dve.wait_ge(*P_.out(i, "u", 0))
                nc.vector.tensor_tensor(o[:, :, :].rearrange("p g (h j) -> p (g h) j", j=HD), v_tm[par][:, :, :].rearrange("p g (h j) -> p (g h) j", j=HD),
                                        usum[par][:, :, :].rearrange("p g h -> p (g h)").unsqueeze(2).to_broadcast([P, G * NH, HD]), ALU.mult)\
                    .then_inc(*own_ready.up())
                dve.wait_ge(*own_ready(i, 1))
                dve.wait_ge(*summed.all(i))
                for g in range(G):
                    view = o[:, g, :].rearrange("p (c h j) -> p c h j", c=KC, j=HD)
                    ins = nc.vector.tensor_tensor(view, view, pO[:, g, :].rearrange("p (c j h) -> p c h j", c=KC, j=HD), ALU.add)
                ins.then_inc(*out_ready.up())

            def finish(i, par, s):
                heads_ = o[:, :, :].rearrange("p g (h j) -> p (g h) j", j=HD)
                if s == "gn_mean":
                    dve.wait_ge(*out_ready(i, 1))
                    nc.vector.tensor_reduce(gsum[:, :], heads_, AX.X, ALU.add).then_inc(*gn_step.up())
                    dve.wait_ge(*gn_step.last(i))
                    nc.vector.scalar_tensor_tensor(out=heads_, in0=gsum[:, :].unsqueeze(2).to_broadcast([P, G * NH, HD]), scalar=-1.0 / HD, in1=heads_,
                                                   op0=ALU.mult, op1=ALU.add).then_inc(*gn_centred.up())
                elif s == "gn_var":
                    dve.wait_ge(*gn_squared(i, 1))
                    nc.vector.tensor_reduce(gvar[:, :], sq.rearrange("p (h j) -> p h j", j=HD), AX.X, ALU.add).then_inc(*gn_step.up())
                    dve.wait_ge(*gn_step.last(i))
                    nc.vector.tensor_scalar(gvar[:, :], gvar[:, :], 1.0 / HD, 1e-5, ALU.mult, ALU.add).then_inc(*gn_var.up())
                elif s == "gn_div":
                    dve.wait_ge(*gn_root(i, 1))
                    nc.vector.reciprocal(grstd[:, :], grstd[:, :]).then_inc(*gn_step.up())
                    dve.wait_ge(*gn_step.last(i))
                    nc.vector.tensor_tensor(gnewt, grstd[:, :], grstd[:, :], ALU.mult).then_inc(*gn_step.up())
                    dve.wait_ge(*gn_step.last(i))
                    nc.vector.tensor_tensor(gnewt, gnewt, gvar[:, :], ALU.mult).then_inc(*gn_step.up())
                    dve.wait_ge(*gn_step.last(i))
                    nc.vector.tensor_scalar(gnewt, gnewt, -0.5, 1.5, ALU.mult, ALU.add).then_inc(*gn_step.up())
                    dve.wait_ge(*gn_step.last(i))
                    nc.vector.tensor_tensor(grstd[:, :], grstd[:, :], gnewt, ALU.mult).then_inc(*gn_step.up())
                    dve.wait_ge(*gn_step.last(i))
                    nc.vector.tensor_tensor(heads_, heads_, grstd[:, :].unsqueeze(2).to_broadcast([P, G * NH, HD]), ALU.mult).then_inc(*gn_ready.up())
                elif s == "gate":
                    for h in range(2):
                        dve.wait_ge(*F_.out(i, "gn", h))
                        part = z[:, 2 * h:2 * h + 2, :].rearrange("p m n -> p (m n)")
                        nc.vector.scalar_tensor_tensor(out=part, in0=part, scalar=0.5, in1=gT[par][:, 2 * h:2 * h + 2, :].rearrange("p m n -> p (m n)"),
                                                       op0=ALU.mult, op1=ALU.mult).then_inc(*z_ready.up())
                elif s[0] == "o":
                    g = int(s[1])
                    bank = take(dve, F_, pF, i, "o", g)
                    if g == 0:
                        dve.wait_ge(*x2_saved(i, 1))
                    nc.vector.tensor_tensor(x2[par][:, g, :], x2[par][:, g, :], bank, ALU.add).then_inc(*F_.emptied["dve"].up())
                elif s == "stats":
                    dve.wait_ge(*F_.out(i, "o", 1))
                    statistics(i, x2[par], 1)
                elif s == "whiten":
                    if (i + -1).exists():
                        dve.wait_ge(*F_.full(i + -1, "fr", 1))
                    whiten(i, x2[par], 1)
                elif s == "shift":
                    if (i + -1).exists():
                        dve.wait_ge(*x4_ready.all(i + -1))
                    shift(F_, i, 1)
                    mix(xk, "L2_xattn_ffn_maa_k", 1).then_inc(*xk_ready.up())
                    mix(xr, "L2_xattn_ffn_maa_r", 1).then_inc(*xr_ready.up())
                elif s[:2] == "fv":
                    g = int(s[2])
                    dve.wait_ge(*F_.out(i, "fr", g))
                    bank = take(dve, F_, pF, i, "fv", g)
                    nc.vector.scalar_tensor_tensor(out=rt[:, g, :], in0=rt[:, g, :], scalar=1.0, in1=bank, op0=ALU.add, op1=ALU.mult)\
                        .then_inc(*F_.emptied["dve"].up())
                    dve.wait_ge(*F_.out(i, "fv", g))
                    nc.vector.scalar_tensor_tensor(out=x2[par][:, g, :], in0=rt[:, g, :], scalar=0.5, in1=x2[par][:, g, :], op0=ALU.mult, op1=ALU.add)\
                        .then_inc(*x4_ready.up())

            run(dve, scan, project, finish)

        @block.gpsimd
        def _(pool):
            pool.wait_ge(consts.sem, 3)

            def deviation(i, k):
                pool.wait_ge(*var_ready[k](i, 1))
                nc.gpsimd.tensor_tensor(rstd[k][:, :], veps[k][:, :], half[:, 0:1].to_broadcast([P, G]), ALU.pow).then_inc(*rstd_ready[k].up())

            def project(i, par, s):
                if s == "x2":
                    for g in range(G):
                        pool.wait_ge(*wy_normed(i, g + 1))
                        nc.gpsimd.tensor_tensor(wyg[:, g, :], wyg[:, g, :], x1g[:, g, :], ALU.add).then_inc(*x2_ready.up())
                elif s == "stats":
                    deviation(i, 0)
                elif s[0] == "m":
                    j = int(s[1])
                    for h in range(2):
                        pool.wait_ge(*P_.out(i, s, h))
                        part = xm[j % 2][:, 2 * h:2 * h + 2, :].rearrange("p k (g t) -> p (k g) t", g=G)
                        nc.gpsimd.tensor_tensor(part, part, xT[0][:, 2 * h:2 * h + 2, :, 1:T + 1].rearrange("p k g t -> p (k g) t"), ALU.add)\
                            .then_inc(*xm_ready.up())

            def scan(i, par, n):
                if n == STEPS:
                    return
                if n == 0:
                    pool.wait_ge(*P_.out(i, "r", 1))
                c = n * JS // HD
                pool.wait_ge(*s_first(i, n + 1))
                pool.wait_ge(*scanned(i, n + 1))
                nc.gpsimd.tensor_tensor(rs[:, n % 2, :, :].rearrange("p j (g t) -> p j g t", g=G), S[:, n % 2, :, :, 0:T],
                                        rT[par][:, c, :].rearrange("p (g t) -> p g t", g=G).unsqueeze(1).to_broadcast([P, JS, G, T]), ALU.mult).then_inc(*rs_ready.up())

            def finish(i, par, s):
                if s == "stats":
                    deviation(i, 1)

            run(pool, scan, project, finish)

        wrong = {s.sem.name: (s.per, s.seen) for s in signals if s.per and s.seen % s.per}
        assert not wrong, wrong


def phase_c(nc, dram):
    NH, HD = 16, 32
    HV = HD + 1
    PH = NH // 2
    FC = 4 * D // P
    items = [(("cT", c), "dve") for c in range(KC)] + [(("k", c), "act") for c in range(KC)] + [(("v", g), "dve") for g in range(G)]
    items += [(("n1", c), "act") for c in range(KC)] + [(("q", c), "act") for c in range(KC)]
    for g in range(G):
        items += [(("pT", g, b), "act" if b % 2 else "dve") for b in range(4)] + [(("pv", g, h), "dve") for h in range(2)]
        if g:
            items += [(("aT", g - 1), "act"), (("o", g - 1), "dve")]
    items += [(("aT", G - 1), "act"), (("o", G - 1), "dve")]
    items += [(("n2", c), "act") for c in range(KC)] + [(("fc", m), "act") for m in range(FC)] + [(("pr", g), "dve") for g in range(G)]

    with ExitStack() as ctx:
        def sb(name, shape, dt=F32):
            return ctx.enter_context(nc.sbuf_tensor("c_" + name, shape, dt))

        def sig(name, per):
            return Signal(ctx.enter_context(nc.semaphore("c_" + name)), per)

        W = {n: sb(n, [P, KC, D]) for n in ("q_w", "k_w", "v_w", "cproj_w")}
        fc_w, proj_w = sb("fc_w", [P, KC, 4 * D]), sb("proj_w", [P, FC, D])
        vec = sb("vec", [P, dram["vecs"].shape[1]])
        rows, ident = sb("rows", [P, 3 * D]), sb("ident", [P, P])
        v_b, cproj_b, proj_b = (rows[:, i * D:i * D + D] for i in range(3))
        half = sb("half", [P, G])
        x, c_tm, xn = sb("x", [P, G, D]), sb("c", [P, G, D]), sb("xn", [P, G, D])
        xT, cT, qT, kT = (sb(n, [P, KC, TOK]) for n in ("xT", "cT", "qT", "kT"))
        attT = cT
        v_ext = sb("v_ext", [P, G, NH, HV])
        wide = sb("wide", [P, 4, NH * T])
        S = [wide[:, 0, :].rearrange("p (h t) -> p h t", t=T), wide[:, 1, :].rearrange("p (h t) -> p h t", t=T),
             xn[:, :, :].rearrange("p g d -> p (g d)").rearrange("p (h t) -> p h t", t=T)]
        probsT = wide[:, 2:4, :].rearrange("p a (h t) -> p a h t", t=T)
        fcT = wide[:, :, :].rearrange("p a (m n) -> p (a m) n", n=TOK)
        mask_u8, limit = sb("mask_u8", [P, G, T], U8), sb("limit", [P, G, T])
        smax, rden = sb("smax", [P, 2, NH]), sb("rden", [P, 2, PH])
        att = sb("att", [P, 2, D])
        bn, mv = sb("bn", [P, G, 6]), sb("mv", [P, G, 2])
        veps, rstd = sb("veps", [P, G]), sb("rstd", [P, G])
        pS = ctx.enter_context(nc.psum_tensor("c_pS", [P, 4, 512], F32))
        pR = ctx.enter_context(nc.psum_tensor("c_pR", [P, RING, 512], F32))

        loaded_w, loaded_q, loaded_mlp = sig("loaded_w", 0), sig("loaded_q", 0), sig("loaded_mlp", 0)
        consts, held = sig("consts", 0), sig("held", 0)
        x_loaded, c_loaded, mask_loaded, stored = sig("x_loaded", 16), sig("c_loaded", 16), sig("mask_loaded", 16), sig("stored", 16 * G)
        filled = sig("filled", len(items))
        emptied = {w: sig("emptied_" + w, [i[1] for i in items].count(w)) for w in ("act", "dve")}
        ring = Ring(items, filled, emptied)
        limit_sign, limit_ready = sig("limit_sign", 1), sig("limit_ready", 1)
        scored, masked, max_found, centred, exp_done = (sig(n, G) for n in ("scored", "masked", "max_found", "centred", "exp_done"))
        var_ready, rstd_ready, xn_ready = sig("var_ready", 2 * G), sig("rstd_ready", 2 * G), sig("xn_ready", 2 * G)
        xb_ready, hb_ready, out_ready = sig("xb_ready", 1), sig("hb_ready", 1), sig("out_ready", G)
        dve_step = sig("dve_step", 24)
        signals = [s for s in locals().values() if isinstance(s, Signal)] + list(emptied.values())
        x_v, c_v = dram["x4"].rearrange("b t d -> t b d"), dram["ctx_2048"].rearrange("b t d -> t b d")
        block = ctx.enter_context(nc.Block())

        def col(name, c):
            at = vec_column(name) + c
            return vec[:, at:at + 1]

        @block.sync
        def _(sp):
            for s in signals:
                if s.per:
                    sp.sem_inc(s.sem, s.per)

            def load_context(turn, guard):
                if guard:
                    sp.wait_ge(*ring.full_before(turn, "cT", KC - 1))
                    sp.sem_inc(held.sem, 1)
                sp.dma_start(c_tm[:, :, :], c_v[:, bass.ds(turn.times(G), G), :]).then_inc(*c_loaded.up(16))
                if guard:
                    sp.wait_ge(*limit_sign.before(turn))
                    sp.sem_inc(held.sem, 1)
                sp.dma_start(mask_u8[:, :, :], dram["mask_rows"][:, bass.ds(turn.times(G), G), :]).then_inc(*mask_loaded.up(16))

            def load_rows(turn):
                sp.wait_ge(*stored.before(turn))
                sp.sem_inc(held.sem, 1)
                sp.dma_start(x[:, :, :], x_v[:, bass.ds(turn.times(G), G), :]).then_inc(*x_loaded.up(16))

            def store(turn):
                for g in range(G):
                    sp.wait_ge(*out_ready(turn, g + 1))
                    sp.sem_inc(held.sem, 1)
                    sp.dma_start(dram["out"][bass.ds(turn.times(G, g), 1), :, :].rearrange("b t d -> t (b d)"),
                                 x[:, g, :]).then_inc(*stored.up(16))

            for tile, name in [(vec, "vecs"), (ident, "ident"), (rows, "rows_c")]:
                sp.dma_start(tile[:, :], dram[name]).then_inc(*loaded_w.up(16))
            load_context(Turn(None), False)
            for signal, tile, name in [(loaded_w, W["k_w"], "k_w"), (loaded_w, W["v_w"], "v_w"), (loaded_q, W["q_w"], "q_w"),
                                       (loaded_q, W["cproj_w"], "cproj_w"), (loaded_mlp, fc_w, "fc_w"), (loaded_mlp, proj_w, "proj_w")]:
                sp.dma_start(tile[:, :, :], dram["L3_xattn_" + name].rearrange("(k p) n -> p k n", p=P)).then_inc(*signal.up(16))
                if name == "v_w":
                    load_rows(Turn(None))
            with sp.Fori(0, NG - 1) as reg:
                turn = Turn(reg)
                load_context(turn + 1, True)
                store(turn)
                load_rows(turn + 1)
            store(Turn(None, add=NG - 1))
            sp.wait_ge(*stored.all(NG - 1))

        @block.tensor
        def _(pe):
            pe.wait_ge(loaded_w.sem, loaded_w.seen)

            def fill(turn, *name, moved=()):
                for wait in ring.ready(turn, name, moved):
                    pe.wait_ge(*wait)
                return pR[:, ring.bank(*name), :]

            def turned(turn, name, src):
                for c in range(KC):
                    bank = fill(turn, name, c)
                    for g in range(G):
                        mm = nc.tensor.transpose(bank[:, g * T:g * T + T], src[:, g, c * P:c * P + P], ident[:, :])
                    mm.then_inc(*filled.up())

            def linear(turn, name, w, src, chunks, turned):
                for m in range(chunks):
                    bank = fill(turn, name, m, moved=[(turned, KC - 1)])
                    for c in range(KC):
                        mm = nc.tensor.matmul(bank, w[:, c, m * P:m * P + P], src[:, c, :], start=(c == 0), stop=(c == KC - 1))
                    mm.then_inc(*filled.up())

            def scores(turn, g):
                if g:
                    pe.wait_ge(*masked(turn, g))
                else:
                    pe.wait_ge(*masked.before(turn))
                for c in range(KC):
                    for r in range(4):
                        at = slice(HD * r, HD * r + HD)
                        mm = nc.tensor.matmul(pS[:, r, c * T:c * T + T], qT[at, c, g * T:g * T + T], kT[at, c, g * T:g * T + T],
                                              start=True, stop=True)
                mm.then_inc(*scored.up())

            def project(turn, g):
                bank = fill(turn, "aT", g, moved=[("pv", g, 1)])
                for c in range(KC):
                    mm = nc.tensor.transpose(bank[:, c * P:c * P + P], att[:, g % 2, c * P:c * P + P], ident[:, :])
                mm.then_inc(*filled.up())
                bank = fill(turn, "o", g, moved=[("aT", g)])
                for c in range(KC):
                    mm = nc.tensor.matmul(bank, attT[:, c, g * T:g * T + T], W["cproj_w"][:, c, :], start=(c == 0), stop=(c == KC - 1))
                mm.then_inc(*filled.up())

            with pe.Fori(0, NG) as turn:
                pe.wait_ge(*c_loaded(turn, 16))
                turned(turn, "cT", c_tm)
                linear(turn, "k", W["k_w"], cT, KC, "cT")
                for g in range(G):
                    bank = fill(turn, "v", g)
                    for c in range(KC):
                        mm = nc.tensor.matmul(bank, cT[:, c, g * T:g * T + T], W["v_w"][:, c, :], start=(c == 0), stop=(c == KC - 1))
                    mm.then_inc(*filled.up())
                pe.wait_ge(*xn_ready(turn, G))
                turned(turn, "n1", xn)
                pe.wait_ge(loaded_q.sem, loaded_q.seen)
                linear(turn, "q", W["q_w"], xT, KC, "n1")
                pe.wait_ge(*ring.out(turn, "q", KC - 1))
                scores(turn, 0)
                scores(turn, 1)
                for g in range(G):
                    pe.wait_ge(*exp_done(turn, g + 1))
                    for b in range(4):
                        bank = fill(turn, "pT", g, b)
                        for i in range(4):
                            mm = nc.tensor.transpose(bank[:, i * T:i * T + T], S[g % 3][:, 4 * b + i, :], ident[:, :])
                        mm.then_inc(*filled.up())
                    if g + 2 < G:
                        scores(turn, g + 2)
                    for h2 in range(2):
                        bank = fill(turn, "pv", g, h2, moved=[("v", G - 1)] + [("pT", g, b) for b in range(4)])
                        for i in range(PH):
                            h = PH * h2 + i
                            mm = nc.tensor.matmul(bank[:, i * HV:i * HV + HV], probsT[:, g % 2, h % 4 * 4 + h // 4, :], v_ext[:, g, h, :],
                                                  start=True, stop=True)
                        mm.then_inc(*filled.up())
                    if g:
                        project(turn, g - 1)
                project(turn, G - 1)
                pe.wait_ge(*xn_ready(turn, 2 * G))
                turned(turn, "n2", xn)
                pe.wait_ge(loaded_mlp.sem, loaded_mlp.seen)
                linear(turn, "fc", fc_w, xT, FC, "n2")
                for g in range(G):
                    bank = fill(turn, "pr", g, moved=[("fc", FC - 1)])
                    for m in range(FC):
                        mm = nc.tensor.matmul(bank, fcT[:, m, g * T:g * T + T], proj_w[:, m, :], start=(m == 0), stop=(m == FC - 1))
                    mm.then_inc(*filled.up())

        @block.scalar
        def _(act):
            act.wait_ge(loaded_w.sem, loaded_w.seen)

            def drain(turn, dst, *name, func=ACT.Copy, **kw):
                act.wait_ge(*ring.full(turn, *name))
                nc.scalar.activation(dst, pR[:, ring.bank(*name), :], func, **kw).then_inc(*emptied["act"].up())

            def exp_round(turn, g):
                act.wait_ge(*centred(turn, g + 1))
                nc.scalar.activation(S[g % 3], S[g % 3], ACT.Exp).then_inc(*exp_done.up())

            def turn_att(turn, g):
                act.wait_ge(*ring.full(turn, "aT", g))
                nc.scalar.activation(attT[:, :, g * T:g * T + T], pR[:, ring.bank("aT", g), :].rearrange("p (k t) -> p k t", k=KC), ACT.Copy)\
                    .then_inc(*emptied["act"].up())

            with act.Fori(0, NG) as turn:
                act.wait_ge(*scored.before(turn))
                for c in range(KC):
                    drain(turn, kT[:, c, :], "k", c, func=ACT.Identity, bias=col("L3_xattn_k_b", c))
                for c in range(KC):
                    drain(turn, xT[:, c, :], "n1", c, func=ACT.Identity, bias=col("L3_xattn_ln1_b", c), scale=col("L3_xattn_ln1_w", c))
                for c in range(KC):
                    drain(turn, qT[:, c, :], "q", c, func=ACT.Identity, bias=col("L3_xattn_q_b", c))
                exp_round(turn, 0)
                for g in range(G):
                    for b in (1, 3):
                        drain(turn, wide[:, 2 + g % 2, b * 512:b * 512 + 512], "pT", g, b)
                    if g + 1 < G:
                        exp_round(turn, g + 1)
                    if g:
                        turn_att(turn, g - 1)
                turn_att(turn, G - 1)
                for c in range(KC):
                    drain(turn, xT[:, c, :], "n2", c, func=ACT.Identity, bias=col("L3_xattn_ln2_b", c), scale=col("L3_xattn_ln2_w", c))
                for m in range(FC):
                    drain(turn, fcT[:, m, :], "fc", m, func=ACT.Gelu_apprx_tanh, bias=col("L3_xattn_fc_b", m))

        @block.vector
        def _(dve):
            dve.wait_ge(loaded_w.sem, loaded_w.seen)
            nc.vector.memset(half[:, :], -0.5).then_inc(*consts.up())
            nc.vector.memset(v_ext[:, :, :, HD:HV], 1.0).then_inc(*consts.up())

            def take(turn, *name):
                dve.wait_ge(*ring.full(turn, *name))
                return pR[:, ring.bank(*name), :]

            def statistics(turn, g):
                nc.vector.bn_stats(bn[:, g, :], x[:, g, :]).then_inc(*dve_step.up())
                dve.wait_ge(*dve_step.last(turn))
                dve.sem_inc(held.sem, 1)
                nc.vector.bn_aggr(mv[:, g, :], bn[:, g, :]).then_inc(*dve_step.up())
                dve.wait_ge(*dve_step.last(turn))
                nc.vector.tensor_scalar(veps[:, g:g + 1], mv[:, g, 1:2], 1e-5, None, ALU.add).then_inc(*var_ready.up())

            def whiten(turn, which, g):
                dve.wait_ge(*rstd_ready(turn, which * G + g + 1))
                nc.vector.tensor_scalar(xn[:, g, :], x[:, g, :], mv[:, g, 0:1], rstd[:, g:g + 1], ALU.subtract, ALU.mult).then_inc(*xn_ready.up())

            def softmax_max(turn, g):
                dve.wait_ge(*scored(turn, g + 1))
                dve.wait_ge(*(ring.full(turn, "pT", g - 3, 3) if g >= 3 else ring.full_before(turn, "pr", G - 1) if g < 2 else ring.full(turn, "n1", KC - 1)))
                nc.vector.scalar_tensor_tensor(out=S[g % 3], in0=pS[:, :, :].rearrange("p r (h t) -> p (r h) t", t=T),
                                               scalar=float(np.float32(1) / np.sqrt(HD).astype(np.float32)),
                                               in1=limit[:, g:g + 1, :].to_broadcast([P, NH, T]), op0=ALU.mult, op1=ALU.min)\
                    .then_inc(*masked.up())
                dve.wait_ge(*masked(turn, g + 1))
                if g >= 2:
                    dve.wait_ge(*centred(turn, g - 1))
                nc.vector.tensor_reduce(smax[:, g % 2, :], S[g % 3], AX.X, ALU.max).then_inc(*max_found.up())

            def normalise(turn, g, h2):
                bank = take(turn, "pv", g, h2)[:, 0:PH * HV].rearrange("p (h e) -> p h e", e=HV)
                nc.vector.reciprocal(rden[:, h2, :].unsqueeze(2), bank[:, :, HD:HV]).then_inc(*dve_step.up())
                dve.wait_ge(*dve_step.last(turn))
                nc.vector.tensor_tensor(att[:, g % 2, h2 * 256:h2 * 256 + 256].rearrange("p (h d) -> p h d", d=HD), bank[:, :, 0:HD],
                                        rden[:, h2, :].unsqueeze(2).to_broadcast([P, PH, HD]), ALU.mult).then_inc(*emptied["dve"].up())

            def residual(turn, g):
                bank = take(turn, "o", g)
                if g == 0:
                    dve.wait_ge(*xb_ready(turn, 1))
                nc.vector.tensor_tensor(x[:, g, :], x[:, g, :], bank, ALU.add).then_inc(*emptied["dve"].up())
                dve.wait_ge(*ring.out(turn, "o", g))
                statistics(turn, g)

            dve.wait_ge(consts.sem, 2)
            with dve.Fori(0, NG) as turn:
                for c in range(KC):
                    bank = take(turn, "cT", c)
                    nc.vector.tensor_copy(cT[:, c, :], bank).then_inc(*emptied["dve"].up())
                dve.wait_ge(*x_loaded(turn, 16))
                dve.wait_ge(*ring.full_before(turn, "n2", KC - 1))
                for g in range(G):
                    statistics(turn, g)
                for g in range(G):
                    whiten(turn, 0, g)
                for g in range(G):
                    bank = take(turn, "v", g)
                    nc.vector.tensor_tensor(v_ext[:, g, :, 0:HD], bank.rearrange("p (h d) -> p h d", d=HD),
                                            v_b.rearrange("p (h d) -> p h d", d=HD), ALU.add).then_inc(*emptied["dve"].up())
                dve.wait_ge(*mask_loaded(turn, 16))
                nc.vector.tensor_scalar(limit[:, :, :], mask_u8[:, :, :], 2.0, -1.0, ALU.mult, ALU.add).then_inc(*limit_sign.up())
                dve.wait_ge(*limit_sign(turn, 1))
                nc.vector.tensor_scalar(limit[:, :, :], limit[:, :, :], FMAX, None, ALU.mult).then_inc(*limit_ready.up())
                dve.wait_ge(*limit_ready(turn, 1))
                softmax_max(turn, 0)
                softmax_max(turn, 1)
                for g in range(G):
                    for b in (0, 2):
                        bank = take(turn, "pT", g, b)
                        nc.vector.tensor_copy(wide[:, 2 + g % 2, b * 512:b * 512 + 512], bank).then_inc(*emptied["dve"].up())
                    if g + 2 < G:
                        softmax_max(turn, g + 2)
                    normalise(turn, g, 0)
                    normalise(turn, g, 1)
                    if g:
                        residual(turn, g - 1)
                residual(turn, G - 1)
                for g in range(G):
                    whiten(turn, 1, g)
                dve.wait_ge(*hb_ready(turn, 1))
                for g in range(G):
                    bank = take(turn, "pr", g)
                    nc.vector.tensor_tensor(x[:, g, :], x[:, g, :], bank, ALU.add).then_inc(*emptied["dve"].up())
                    out_ready_after = ring.out(turn, "pr", g)
                    dve.wait_ge(*out_ready_after)
                    nc.vector.memset(bn[:, 0, 0:1], 0.0).then_inc(*out_ready.up())

        @block.gpsimd
        def _(pool):
            pool.wait_ge(loaded_w.sem, loaded_w.seen)
            pool.wait_ge(consts.sem, 2)

            def deviation(turn, which, g):
                pool.wait_ge(*var_ready(turn, which * G + g + 1))
                nc.gpsimd.tensor_tensor(rstd[:, g:g + 1], veps[:, g:g + 1], half[:, 0:1], ALU.pow).then_inc(*rstd_ready.up())

            with pool.Fori(0, NG) as turn:
                for g in range(G):
                    deviation(turn, 0, g)
                pool.wait_ge(*xn_ready(turn, G))
                nc.gpsimd.tensor_tensor(x[:, :, :], x[:, :, :], cproj_b.unsqueeze(1).to_broadcast([P, G, D]), ALU.add).then_inc(*xb_ready.up())
                for g in range(G):
                    if g == 3:
                        deviation(turn, 1, 0)
                    pool.wait_ge(*max_found(turn, g + 1))
                    nc.gpsimd.tensor_tensor(S[g % 3], S[g % 3], smax[:, g % 2, :].unsqueeze(2).to_broadcast([P, NH, T]),
                                            ALU.subtract).then_inc(*centred.up())
                for g in range(1, G):
                    deviation(turn, 1, g)
                pool.wait_ge(*xn_ready(turn, 2 * G))
                nc.gpsimd.tensor_tensor(x[:, :, :], x[:, :, :], proj_b.unsqueeze(1).to_broadcast([P, G, D]), ALU.add).then_inc(*hb_ready.up())

        wrong = {s.sem.name: (s.per, s.seen) for s in signals if s.per and s.seen % s.per}
        assert not wrong, wrong


def phase_norm(nc, dram, stats, norm):
    with ExitStack() as ctx:
        par, mv = ctx.enter_context(nc.sbuf_tensor("n_par", [P, 2], F32)), ctx.enter_context(nc.sbuf_tensor("n_mv", [P, 2], F32))
        half, rstd = ctx.enter_context(nc.sbuf_tensor("n_half", [P, 1], F32)), ctx.enter_context(nc.sbuf_tensor("n_rstd", [P, 1], F32))
        loaded, var_ready, rstd_ready, step = (ctx.enter_context(nc.semaphore("n_" + n)) for n in ("loaded", "var", "rstd", "step"))
        block = ctx.enter_context(nc.Block())

        @block.sync
        def _(sp):
            sp.dma_start(par[:, :], dram["L1_affine"]).then_inc(loaded, 16)

        @block.gpsimd
        def _(pool):
            pool.wait_ge(var_ready, 2)
            nc.gpsimd.tensor_tensor(rstd[:, :], mv[:, 1:2], half[:, :], ALU.pow).then_inc(rstd_ready, 1)

        @block.vector
        def _(dve):
            nc.vector.memset(half[:, :], -0.5).then_inc(var_ready, 1)
            nc.vector.bn_aggr(mv[:, :], stats[:, :]).then_inc(step, 1)
            dve.wait_ge(step, 1)
            nc.vector.tensor_scalar(mv[:, 1:2], mv[:, 1:2], 1e-5, None, ALU.add).then_inc(var_ready, 1)
            dve.wait_ge(loaded, 16)
            dve.wait_ge(rstd_ready, 1)
            nc.vector.tensor_tensor(norm[:, 0:1], rstd[:, :], par[:, 0:1], ALU.mult).then_inc(step, 1)
            dve.wait_ge(step, 2)
            nc.vector.tensor_tensor(mv[:, 0:1], mv[:, 0:1], norm[:, 0:1], ALU.mult).then_inc(step, 1)
            dve.wait_ge(step, 3)
            nc.vector.tensor_tensor(norm[:, 1:2], par[:, 1:2], mv[:, 0:1], ALU.subtract).then_inc(step, 1)
            dve.wait_ge(step, 4)


def program(nc, dram):
    with ExitStack() as ctx:
        stats = ctx.enter_context(nc.sbuf_tensor("stats", [P, B * 6], F32))
        norm = ctx.enter_context(nc.sbuf_tensor("norm", [P, 2], F32))
        phase_a(nc, dram, stats)
        phase_norm(nc, dram, stats, norm)
        phase_b(nc, dram, norm)
        phase_c(nc, dram)


def _layout(inputs):
    a = {n: np.asarray(v) for n, v in inputs.items()}
    out = {n: a[n] for n in ("x", "ctx_2048", "mask_Bx1xSxS2_ff0", "L0_xattn_Wq", "L0_xattn_Wk", "L0_xattn_Wv", "L0_xattn_Wo",
                             "L2_xattn_maa_w1", "L2_xattn_maa_w2", "L2_xattn_td_w1", "L2_xattn_td_w2",
                             "L3_xattn_q_w", "L3_xattn_k_w", "L3_xattn_v_w", "L3_xattn_cproj_w", "L3_xattn_fc_w", "L3_xattn_proj_w")}
    for n in ("Wg", "Wtheta", "Wphi", "Wz"):
        out["L1_" + n + "T"] = a["L1_xattn_" + n].T
    for n in ("Wk", "Wv", "Wr", "Wg", "Wo", "Wfk", "Wfr", "Wfv"):
        out["L2_" + n + "T"] = a["L2_xattn_" + n].T
    out["vecs"] = np.concatenate([a[n].reshape(-1, P).T for n in VECS], axis=1)
    out["bk_wide"] = np.broadcast_to(a["L0_xattn_bk"].reshape(8, 1, 16), (8, 4, 16)).reshape(KC, P).T
    out["rows_a"] = np.concatenate([np.broadcast_to(a[n][None, :], (P, a[n].size)) for n in ROWS_A], axis=1)
    out["rows_c"] = np.concatenate([np.broadcast_to(a[n][None, :], (P, a[n].size)) for n in ROWS_C], axis=1)
    out["L1_ci"] = np.stack([a["L1_xattn_bphi"], a["L1_xattn_btheta"]], axis=1)
    out["L1_bz"] = a["L1_xattn_bz"].reshape(P, 1)
    out["L1_affine"] = np.stack([a["L1_xattn_gamma"], a["L1_xattn_beta"]], axis=1)
    out["mask_rows"] = np.broadcast_to(np.ascontiguousarray(a["mask_BxS2_bf1"]).view(np.uint8)[None], (P, B, T))
    state = a["ctx_2048"]
    out["state_rows"] = state[:, 0:2].reshape(B, 2, KC, P).transpose(3, 0, 1, 2)
    out["state_heads"] = state[:, 2:18].reshape(B // 2, 2, KC, P, 16).transpose(3, 0, 2, 1, 4).reshape(P, B // 2 * KC, 2, 16)
    out["ident"] = np.eye(P, dtype=np.float32)
    p = np.arange(P)
    out["parity"] = (p[:, None] // 16 % 2 == np.arange(2)[None, :]).astype(np.float32)
    out["heads"] = (p[:, None] // 16 == np.arange(P // 16)[None, :]).astype(np.float32)
    out["pick"] = ((p[:, None, None] // 16 == p[None, None, :] // 16)
                   & (p[:, None, None] % 16 == np.arange(16)[None, :, None])).astype(np.float32).reshape(P, -1)
    return {n: np.ascontiguousarray(v) for n, v in out.items()}


def kernel(**inputs):
    import concourse.bacc as bacc
    from concourse.bass_utils import run_bass_kernel_spmd as run

    arrays = _layout(inputs)
    nc = bacc.Bacc("TRN2", target_bir_lowering=False, num_devices=1)
    dram = {n: nc.dram_tensor(n, v.shape, mybir.dt.from_np(v.dtype), kind="ExternalInput").ap() for n, v in arrays.items()}
    for n in ("x1", "wy", "x4"):
        dram[n] = nc.dram_tensor("mid_" + n, (B, T, D), F32, kind="Internal").ap()
    dram["out"] = nc.dram_tensor("out", (B, T, D), F32, kind="ExternalOutput").ap()
    program(nc, dram)
    return run(nc, [arrays], core_ids=[0]).results[0]["out"]
```

```python
from contextlib import ExitStack

import numpy as np

import concourse.bass as bass
from concourse import mybir

F32 = mybir.dt.float32
F32R = mybir.dt.float32r
U8 = mybir.dt.uint8
ALU = mybir.AluOpType
ACT = mybir.ActivationFunctionType
AX = mybir.AxisListType

B, T, D = 32, 128, 512
P = 128
KC = D // P
G = 4
NG = B // G
TOK = G * T
RING = 4
FMAX = 3.4028234663852886e38

VECS = ["L0_xattn_bq", "L2_xattn_ln1_w", "L2_xattn_ln1_b", "L2_xattn_ln2_w", "L2_xattn_ln2_b", "L2_xattn_maa_x",
        "L2_xattn_time_decay", "L2_xattn_u", "L2_xattn_gn_w", "L2_xattn_gn_b", "L2_xattn_ffn_maa_k",
        "L2_xattn_ffn_maa_r", "L3_xattn_ln1_w", "L3_xattn_ln1_b", "L3_xattn_q_b", "L3_xattn_k_b",
        "L3_xattn_ln2_w", "L3_xattn_ln2_b", "L3_xattn_fc_b", "L2_xattn_maa_stack"]
ROWS_A = ["L0_xattn_bo", "L0_xattn_gamma", "L0_xattn_beta", "L0_xattn_bv", "L1_xattn_bg"]
ROWS_C = ["L3_xattn_v_b", "L3_xattn_cproj_b", "L3_xattn_proj_b"]


class Turn:

    def __init__(self, reg, mult=1, add=0):
        self.reg, self.mult, self.add = reg, mult, add

    def __add__(self, n):
        return Turn(self.reg, self.mult, self.add + n)

    def times(self, n, more=0):
        return self.add * n + more if self.reg is None else self.reg * (self.mult * n) + (self.add * n + more)

    def exists(self):
        return self.reg is not None or self.add >= 0


class Signal:

    def __init__(self, sem, per):
        self.sem, self.per, self.seen = sem, per, 0

    def up(self, n=1):
        self.seen += n
        return self.sem, n

    def __call__(self, turn, k):
        turn = turn if isinstance(turn, Turn) else Turn(turn)
        return self.sem, turn.times(self.per, self.per + k)

    def all(self, turn):
        return self(turn, self.per)

    def last(self, turn):
        return self(turn, (self.seen - 1) % self.per + 1)

    def before(self, turn, k=None):
        turn = turn if isinstance(turn, Turn) else Turn(turn)
        return self(turn + -1, self.per if k is None else k)


class Ring:

    def __init__(self, items, filled, emptied, banks=RING):
        assert len(items) % banks == 0, len(items)
        self.at = {name: n for n, (name, _) in enumerate(items)}
        self.who = [who for _, who in items]
        self.filled, self.emptied, self.banks = filled, emptied, banks
        self.nth = [self.who[:n + 1].count(w) for n, w in enumerate(self.who)]

    def bank(self, *name):
        return self.at[name] % self.banks

    def ready(self, turn, name, moved=()):
        n = self.at[name] - self.banks
        last = {self.who[n]: self.nth[n] if n >= 0 else self.nth[n] - self.emptied[self.who[n]].per}
        for other in moved:
            n = self.at[other]
            last[self.who[n]] = max(last.get(self.who[n], -10**9), self.nth[n])
        return [self.emptied[w](turn, k) for w, k in last.items()]

    def full(self, turn, *name):
        return self.filled(turn, self.at[name] + 1)

    def full_before(self, turn, *name):
        return self.filled.before(turn, self.at[name] + 1)

    def out(self, turn, *name):
        n = self.at[name]
        return self.emptied[self.who[n]](turn, self.nth[n])


def vec_column(name):
    at = VECS.index(name)
    wide = VECS.index("L3_xattn_fc_b")
    return KC * at if at <= wide else KC * wide + 4 * D // P


def phase_a(nc, dram, stats):
    NH, KVH, HD = 32, 8, 16
    RH = NH // 2
    SLOTS = P // HD
    PAD = P - HD
    NR = 2 * G
    AHEAD = 3
    CI = 64
    MIXED = ["phi0", "phi1", "phi2", "phi3", "xT", "o3", "q0", "q1", "th0", "th1", "th2", "q2", "q3", "th3", "f0", "cT", "k0", "f1", "fT0",
             "k1", "y0", "f2", "wy0", "fT1", "k2", "y1", "f3", "wy1", "fT2", "k3", "y2", "s0", "v0", "wy2", "v1", "fT3", "v2", "y3", "v3", "wy3"]
    FRONT = [s for s in MIXED if s[0] in "xcqkvs"]
    y_items = []
    for s in FRONT:
        if s == "s0":
            continue
        who = "act" if s[0] in "xq" else "dve"
        y_items += [((s, c), who) for c in range(KC)] if s[1] == "T" else [((s,), who)]
    x_items = []
    for n in range(NR):
        x_items += [(("pT", n, 0), "dve"), (("pT", n, 1), "act")]
        y_items += [(("pT", n, 2), "dve"), (("pT", n, 3), "act"), (("pv", n), "dve")]
        if n >= 2 and n % 2 == 0:
            x_items.append((("o", n // 2 - 1), "dve"))
    for s in MIXED:
        if s[:3] == "phi":
            x_items.append((("phi", int(s[3])), "act"))
        elif s[:2] == "th":
            x_items += [(("th", int(s[2])), "act"), (("gx", int(s[2])), "dve")]
        elif s[:2] == "fT":
            x_items += [(("fT", int(s[2]), j), "act" if j % 2 else "dve") for j in range(KC)]
        elif s[0] in "oyw":
            x_items.append(((s[:-1], int(s[-1])), "dve" if s[0] == "o" else "act"))

    with ExitStack() as ctx:
        def sb(name, shape, dt=F32):
            return ctx.enter_context(nc.sbuf_tensor("a_" + name, shape, dt))

        def sig(name, per):
            return Signal(ctx.enter_context(nc.semaphore("a_" + name)), per)

        wq, wo = sb("wq", [P, KC, D]), sb("wo", [P, KC, D])
        wk, wv = sb("wk", [P, KC, 128]), sb("wv", [P, KC, 128])
        wkr = sb("wkr", [P, KC, D])
        wgT, wthT, wphT = sb("wgT", [P, CI]), sb("wthT", [P, CI]), sb("wphT", [P, CI])
        wzT = sb("wzT", [CI, P])
        vec = sb("vec", [P, KC])
        bk = sb("bk", [P, KC])
        ci = sb("ci", [CI, 2])
        bz = sb("bz", [P, 1])
        rows = sb("rows", [P, 3 * D + 128 + CI])
        parity, ident = sb("parity", [P, 2]), sb("ident", [P, P])
        bo, gamma, beta = rows[:, 0:D], rows[:, D:2 * D], rows[:, 2 * D:3 * D]
        bv, bg = rows[:, 3 * D:3 * D + 128], rows[:, 3 * D + 128:]
        half = sb("half", [P, 1])

        x, c_tm, mask = sb("x", [P, G, D]), sb("c", [P, G, D]), sb("mask", [P, G, T])
        xT, cT, qT = sb("xT", [P, KC, TOK]), sb("cT", [P, KC, TOK]), sb("qT", [P, KC, TOK])
        kexp = sb("kexp", [P, KC, 2, TOK])
        v_pad = sb("v_pad", [P, G, KVH * P + PAD])
        S = sb("S", [P, AHEAD, RH, T])
        probsT = sb("probsT", [P, 2, RH, T])
        negmax, wsum, rden = (sb(n, [P, AHEAD, RH]) for n in ("negmax", "wsum", "rden"))
        attT = sb("attT", [P, KC, TOK])
        xbo, x1 = sb("xbo", [P, G, D]), sb("x1", [P, G, D])
        bn, mv = sb("bn", [P, 6]), sb("mv", [P, 2])
        veps, rstd = sb("veps", [P, 1]), sb("rstd", [P, 1])
        phi, theta = sb("phi", [CI, G, D]), sb("theta", [CI, G, D])
        gx = sb("gx", [P, G, KC, CI])
        nmax, fsum = sb("nmax", [P, 2, KC]), sb("fsum", [P, 2, KC])
        yT, wy = sb("yT", [CI, 2, D]), sb("wy", [P, 2, D])
        f_sb = S[:, 0:2, :, :].rearrange("p a (i k) t -> p a i (k t)", i=KC)
        fT = probsT[:, :, :, :].rearrange("p a (i k) t -> p a i (k t)", i=KC)
        pS = ctx.enter_context(nc.psum_tensor("a_pS", [P, 4, 512], F32))
        pX, pY = (ctx.enter_context(nc.psum_tensor("a_p" + n, [P, 2, 512], F32)) for n in "XY")

        loaded_w, loaded_rest = sig("loaded_w", 0), sig("loaded_rest", 0)
        x_loaded, c_loaded, mask_loaded = sig("x_loaded", 16), sig("c_loaded", 16), sig("mask_loaded", 16)
        x1_stored, wy_stored = sig("x1_stored", 16 * G), [sig("wy_stored%d" % i, 16 * G // 2) for i in range(2)]

        def ring_of(name, items):
            emptied = {w: sig(name + "_emptied_" + w, [i[1] for i in items].count(w)) for w in ("act", "dve")}
            return Ring(items, sig(name + "_filled", len(items)), emptied, banks=2)

        X, Y = ring_of("x", x_items), ring_of("y", y_items)
        ones_set, wk_wide = sig("ones_set", 0), sig("wk_wide", 0)
        scored, masked = sig("scored", NR + G), sig("masked", NR)
        max_found, exp_done, sums_inverted, weighed = (sig(n, NR) for n in ("max_found", "exp_done", "sums_inverted", "weighed"))
        xbo_ready, var_ready, rstd_ready = sig("xbo_ready", 1), sig("var_ready", G), sig("rstd_ready", G)
        whitened, x1_ready = sig("whitened", G), sig("x1_ready", G)
        f_max, f_exp, f_scaled, y_stats = sig("f_max", G), sig("f_exp", G), sig("f_scaled", G), sig("y_stats", G)
        held, k_half = sig("held", 0), sig("k_half", KC)
        dve_step, pool_step = sig("dve_step", 12), sig("pool_step", G)
        signals = [s for s in locals().values() if isinstance(s, Signal)] + wy_stored
        for ring in (X, Y):
            signals += [ring.filled] + list(ring.emptied.values())
        x_v, c_v = dram["x"].rearrange("b t d -> t b d"), dram["ctx_2048"].rearrange("b t d -> t b d")
        m_v = dram["mask_Bx1xSxS2_ff0"].rearrange("b o l s -> l (b o) s")
        block = ctx.enter_context(nc.Block())

        @block.sync
        def _(sp):
            for s in signals:
                if s.per:
                    sp.sem_inc(s.sem, s.per)

            def load(turn, tile, src, signal, free):
                if free:
                    sp.wait_ge(*free)
                    sp.sem_inc(held.sem, 1)
                sp.dma_start(tile[:, :, :], src[:, bass.ds(turn.times(G), G), :]).then_inc(*signal.up(16))

            def store_x1(turn):
                for g in range(G):
                    sp.wait_ge(*x1_ready(turn, g + 1))
                    sp.sem_inc(held.sem, 1)
                    sp.dma_start(dram["x1"][bass.ds(turn.times(G, g), 1), :, :].rearrange("b t d -> t (b d)"),
                                 x1[:, g, :]).then_inc(*x1_stored.up(16))

            def store_wy(turn):
                for g in range(G):
                    sp.wait_ge(*X.out(turn, "wy", g))
                    sp.sem_inc(held.sem, 1)
                    sp.dma_start(dram["wy"][bass.ds(turn.times(G, g), 1), :, :].rearrange("b t d -> t (b d)"),
                                 wy[:, g % 2, :]).then_inc(*wy_stored[g % 2].up(16))

            sp.dma_start(ident[:, :], dram["ident"]).then_inc(*loaded_w.up(16))
            sp.dma_start(wk[:, :, :], dram["L0_xattn_Wk"].rearrange("(k p) n -> p k n", p=P)).then_inc(*loaded_w.up(16))
            load(Turn(None), x, x_v, x_loaded, None)
            load(Turn(None), c_tm, c_v, c_loaded, None)
            for tile, name in [(wq, "L0_xattn_Wq"), (wv, "L0_xattn_Wv"), (wo, "L0_xattn_Wo")]:
                sp.dma_start(tile[:, :, :], dram[name].rearrange("(k p) n -> p k n", p=P)).then_inc(*loaded_rest.up(16))
            for tile, name in [(bk, "bk_wide"), (parity, "parity"), (rows, "rows_a"), (wgT, "L1_WgT"), (wthT, "L1_WthetaT"),
                               (wphT, "L1_WphiT"), (wzT, "L1_WzT"), (ci, "L1_ci"), (bz, "L1_bz")]:
                sp.dma_start(tile[:, :], dram[name]).then_inc(*loaded_rest.up(16))
            sp.dma_start(vec[:, :], dram["vecs"][:, 0:KC]).then_inc(*loaded_rest.up(16))
            load(Turn(None), mask, m_v, mask_loaded, None)
            with sp.Fori(0, NG - 1) as reg:
                turn = Turn(reg)
                load(turn + 1, x, x_v, x_loaded, xbo_ready.all(turn))
                store_x1(turn)
                load(turn + 1, c_tm, c_v, c_loaded, X.full(turn, "phi", G - 1))
                load(turn + 1, mask, m_v, mask_loaded, masked.all(turn))
                store_wy(turn)
            store_x1(Turn(None, add=NG - 1))
            store_wy(Turn(None, add=NG - 1))
            sp.wait_ge(*x1_stored(NG - 1, 16 * G))
            for half_stored in wy_stored:
                sp.wait_ge(*half_stored(NG - 1, 16 * G // 2))

        def fill(pe, ring, turn, *name, moved=()):
            for wait in ring.ready(turn, name, moved):
                pe.wait_ge(*wait)
            return (pX if ring is X else pY)[:, ring.bank(*name), :]

        def take(eng, ring, turn, *name):
            eng.wait_ge(*ring.full(turn, *name))
            return (pX if ring is X else pY)[:, ring.bank(*name), :]

        def ring_at(b):
            return X if b < 2 else Y

        def run(eng, front, rounds, inner):
            for s in FRONT:
                front(Turn(None), s)
            with eng.Fori(0, NG - 1) as reg:
                rounds(Turn(reg))
                for s in MIXED:
                    front(Turn(reg) + 1, s) if s in FRONT else inner(Turn(reg), s)
            rounds(Turn(None, add=NG - 1))
            for s in MIXED:
                if s not in FRONT:
                    inner(Turn(None, add=NG - 1), s)

        @block.tensor
        def _(pe):
            pe.wait_ge(loaded_w.sem, loaded_w.seen)

            def front(turn, s):
                if s == "s0":
                    pe.wait_ge(*Y.out(turn, "q3"))
                    pe.wait_ge(*Y.out(turn, "k3"))
                    scores(turn, 0)
                elif s[1] == "T":
                    src, signal = (x, x_loaded) if s == "xT" else (c_tm, c_loaded)
                    for c in range(KC):
                        bank = fill(pe, Y, turn, s, c)
                        if c == 0:
                            pe.wait_ge(*signal(turn, 16))
                        for g in range(G):
                            mm = nc.tensor.transpose(bank[:, g * T:g * T + T], src[:, g, c * P:c * P + P], ident[:, :])
                        mm.then_inc(*Y.filled.up())
                elif s[0] == "v":
                    g = int(s[1])
                    bank = fill(pe, Y, turn, s)
                    for c in range(KC):
                        mm = nc.tensor.matmul(bank[:, 0:P], cT[:, c, g * T:g * T + T], wv[:, c, :], start=(c == 0), stop=(c == KC - 1))
                    mm.then_inc(*Y.filled.up())
                else:
                    m = int(s[1])
                    w, src, turned = (wq, xT, "xT") if s[0] == "q" else (wkr, cT, "cT")
                    if s[0] == "q":
                        pe.wait_ge(loaded_rest.sem, loaded_rest.seen)
                    else:
                        pe.wait_ge(wk_wide.sem, KC)
                    bank = fill(pe, Y, turn, s, moved=[(turned, KC - 1)])
                    for c in range(KC):
                        mm = nc.tensor.matmul(bank, w[:, c, m * P:m * P + P], src[:, c, :], start=(c == 0), stop=(c == KC - 1))
                    mm.then_inc(*Y.filled.up())

            def scores(turn, n):
                g, half_ = n // 2, n % 2
                pe.wait_ge(*(masked(turn, n) if n else f_exp.before(turn)))
                for cc in range(2):
                    c = 2 * half_ + cc
                    for r in range(4):
                        at = slice(32 * r, 32 * r + 32)
                        mm = nc.tensor.matmul(pS[:, r, cc * 256:cc * 256 + 256].rearrange("p (a t) -> p a t", a=2), qT[at, c, g * T:g * T + T],
                                              kexp[at, c, :, g * T:g * T + T], start=True, stop=True)
                mm.then_inc(*scored.up())

            def project_att(turn, g):
                bank = fill(pe, X, turn, "o", g)
                pe.wait_ge(*Y.out(turn, "pv", 2 * g + 1))
                for c in range(KC):
                    mm = nc.tensor.matmul(bank[:, :], attT[:, c, g * T:g * T + T], wo[:, c, :], start=(c == 0), stop=(c == KC - 1))
                mm.then_inc(*X.filled.up())

            def rounds(turn):
                pe.wait_ge(*Y.out(turn, "v3"))
                scores(turn, 1)
                for n in range(NR):
                    pe.wait_ge(*weighed(turn, n + 1))
                    for b in range(4):
                        bank = fill(pe, ring_at(b), turn, "pT", n, b)
                        for i in range(4):
                            mm = nc.tensor.transpose(bank[:, i * T:i * T + T], S[:, n % AHEAD, 4 * b + i, :], ident[:, :])
                        mm.then_inc(*ring_at(b).filled.up())
                    if n + 2 < NR:
                        scores(turn, n + 2)
                    if n >= 2 and n % 2 == 0:
                        project_att(turn, n // 2 - 1)
                    bank = fill(pe, Y, turn, "pv", n, moved=[("pT", n, 2), ("pT", n, 3)])
                    for b in range(2):
                        pe.wait_ge(*X.out(turn, "pT", n, b))
                    for cc in range(2):
                        for slot in range(SLOTS):
                            at = slot // 2 * 4 + 2 * cc + slot % 2
                            kv = (n % 2 * RH + cc * SLOTS + slot) // (NH // KVH)
                            left = kv * P + PAD - slot * HD
                            mm = nc.tensor.matmul(bank[:, cc * T:cc * T + T], v_pad[:, n // 2, left:left + P], probsT[:, n % 2, at, :],
                                                  start=(slot == 0), stop=(slot == SLOTS - 1))
                    mm.then_inc(*Y.filled.up())

            def inner(turn, s):
                g = int(s[-1])
                if s[:3] == "phi":
                    bank = fill(pe, X, turn, "phi", g)
                    nc.tensor.matmul(bank[0:CI, :], wphT[:, :], c_tm[:, g, :], start=True, stop=True).then_inc(*X.filled.up())
                elif s[:2] == "th":
                    bank = fill(pe, X, turn, "th", g)
                    pe.wait_ge(*x1_ready(turn, g + 1))
                    nc.tensor.matmul(bank[0:CI, :], wthT[:, :], x1[:, g, :], start=True, stop=True).then_inc(*X.filled.up())
                    bank = fill(pe, X, turn, "gx", g)
                    for j in range(KC):
                        mm = nc.tensor.matmul(bank[:, j * CI:j * CI + CI], x1[:, g, j * P:j * P + P], wgT[:, :], start=True, stop=True)
                    mm.then_inc(*X.filled.up())
                elif s[:2] == "fT":
                    pe.wait_ge(*f_scaled(turn, g + 1))
                    for j in range(KC):
                        bank = fill(pe, X, turn, "fT", g, j)
                        for i in range(KC):
                            mm = nc.tensor.transpose(bank[:, i * P:i * P + P], f_sb[:, g % 2, i, j * P:j * P + P], ident[:, :])
                        mm.then_inc(*X.filled.up())
                elif s[0] == "f":
                    pe.wait_ge(*(f_exp(turn, g) if g else masked(turn, NR)))
                    pe.wait_ge(*X.out(turn, "th", g))
                    for i in range(KC):
                        mm = nc.tensor.matmul(pS[:, i, :], phi[:, g, i * P:i * P + P], theta[:, g, :], start=True, stop=True)
                    mm.then_inc(*scored.up())
                elif s[0] == "o":
                    project_att(turn, g)
                elif s[0] == "y":
                    bank = fill(pe, X, turn, "y", g, moved=[("gx", g)] + [("fT", g, j) for j in range(KC)])
                    for j in range(KC):
                        mm = nc.tensor.matmul(bank[0:CI, :], gx[:, g, j, :], fT[:, g % 2, j, :], start=(j == 0), stop=(j == KC - 1))
                    mm.then_inc(*X.filled.up())
                else:
                    bank = fill(pe, X, turn, "wy", g, moved=[("y", g)])
                    nc.tensor.matmul(bank[:, :], wzT[:, :], yT[:, g % 2, :], start=True, stop=True).then_inc(*X.filled.up())

            run(pe, front, rounds, inner)

        @block.scalar
        def _(act):
            def front(turn, s):
                if s == "xT":
                    for c in range(KC):
                        bank = take(act, Y, turn, "xT", c)
                        nc.scalar.activation(xT[:, c, :], bank, ACT.Copy).then_inc(*Y.emptied["act"].up())
                elif s[0] == "q":
                    c = int(s[1])
                    if c == 0:
                        act.wait_ge(loaded_rest.sem, loaded_rest.seen)
                        act.wait_ge(*scored.before(turn, NR))
                    bank = take(act, Y, turn, s)
                    nc.scalar.activation(qT[:, c, :], bank, ACT.Identity, bias=vec[:, c:c + 1]).then_inc(*Y.emptied["act"].up())
                elif s in ("v1", "v3"):
                    exp_half(turn, 0, int(s[1]) // 2)

            def exp_half(turn, n, part):
                k = n % AHEAD
                if part == 0:
                    act.wait_ge(*max_found(turn, n + 1))
                for h in range(part * RH // 2, (part + 1) * RH // 2):
                    ins = nc.scalar.activation(S[:, k, h, :], S[:, k, h, :], ACT.Exp, bias=negmax[:, k, h:h + 1], accum_out=wsum[:, k, h:h + 1])
                if part:
                    ins.then_inc(*exp_done.up())

            def rounds(turn):
                for n in range(NR):
                    if n + 1 < NR:
                        exp_half(turn, n + 1, 0)
                    for b in (1, 3):
                        bank = take(act, ring_at(b), turn, "pT", n, b)
                        nc.scalar.activation(probsT[:, n % 2, 4 * b:4 * b + 4, :], bank.rearrange("p (h t) -> p h t", h=4), ACT.Copy)\
                            .then_inc(*ring_at(b).emptied["act"].up())
                    if n + 1 < NR:
                        exp_half(turn, n + 1, 1)

            def exp_f(turn, g):
                act.wait_ge(*f_max(turn, g + 1))
                if g >= 2:
                    act.wait_ge(*X.full(turn, "fT", g - 2, KC - 1))
                else:
                    act.wait_ge(*Y.full(turn, "pT", NR - 1, 3))
                for i in range(KC):
                    ins = nc.scalar.activation(f_sb[:, g % 2, i, :], pS[:, i, :], ACT.Exp, bias=nmax[:, g % 2, i:i + 1],
                                               accum_out=fsum[:, g % 2, i:i + 1])
                ins.then_inc(*f_exp.up())

            def inner(turn, s):
                g = int(s[-1])
                if s[:3] == "phi":
                    if g == 0:
                        act.wait_ge(*scored.before(turn, NR + G))
                    bank = take(act, X, turn, "phi", g)
                    nc.scalar.activation(phi[:, g, :], bank[0:CI, :], ACT.Identity, bias=ci[:, 0:1]).then_inc(*X.emptied["act"].up())
                elif s[:2] == "th":
                    bank = take(act, X, turn, "th", g)
                    nc.scalar.activation(theta[:, g, :], bank[0:CI, :], ACT.Identity, bias=ci[:, 1:2]).then_inc(*X.emptied["act"].up())
                elif s[:2] == "fT":
                    for j in (1, 3):
                        bank = take(act, X, turn, "fT", g, j)
                        nc.scalar.activation(fT[:, g % 2, j, :], bank, ACT.Copy).then_inc(*X.emptied["act"].up())
                    if g + 1 < G:
                        exp_f(turn, g + 1)
                elif s == "f0":
                    exp_f(turn, 0)
                elif s[0] == "y":
                    bank = take(act, X, turn, "y", g)
                    nc.scalar.activation(yT[:, g % 2, :], bank[0:CI, :], ACT.Copy).then_inc(*X.emptied["act"].up())
                elif s[0] == "w":
                    bank = take(act, X, turn, "wy", g)
                    act.wait_ge(*(wy_stored[g % 2](turn, 16) if g >= 2 else wy_stored[g % 2].before(turn)))
                    act.wait_ge(*(y_stats(turn, g - 1) if g >= 2 else y_stats.before(turn)))
                    nc.scalar.activation(wy[:, g % 2, :], bank, ACT.Identity, bias=bz[:, 0:1]).then_inc(*X.emptied["act"].up())

            run(act, front, rounds, inner)

        @block.vector
        def _(dve):
            dve.wait_ge(loaded_w.sem, loaded_w.seen)
            nc.vector.memset(v_pad[:, :, :], 0.0).then_inc(*ones_set.up())
            nc.vector.memset(half[:, :], -0.5).then_inc(*ones_set.up())
            for c in range(KC):
                src = wk[:, c, :].rearrange("p (v d) -> p v d", v=KVH).unsqueeze(2).to_broadcast([P, KVH, NH // KVH, HD])
                nc.vector.tensor_copy(wkr[:, c, :].rearrange("p (v g d) -> p v g d", v=KVH, d=HD), src).then_inc(*wk_wide.up())
            dve.wait_ge(ones_set.sem, 2)

            def front(turn, s):
                if s == "s0":
                    dve.wait_ge(*mask_loaded(turn, 16))
                    softmax_max(turn, 0)
                elif s == "cT":
                    for c in range(KC):
                        bank = take(dve, Y, turn, "cT", c)
                        nc.vector.tensor_copy(cT[:, c, :], bank).then_inc(*Y.emptied["dve"].up())
                elif s[0] == "k":
                    c = int(s[1])
                    if c == 0:
                        dve.wait_ge(loaded_rest.sem, loaded_rest.seen)
                        dve.wait_ge(*scored.before(turn, NR))
                    bank = take(dve, Y, turn, s)
                    nc.vector.tensor_scalar(kexp[:, c, 0, :], bank, bk[:, c:c + 1], parity[:, 0:1], ALU.add, ALU.mult).then_inc(*k_half.up())
                    nc.vector.tensor_scalar(kexp[:, c, 1, :], bank, bk[:, c:c + 1], parity[:, 1:2], ALU.add, ALU.mult)\
                        .then_inc(*Y.emptied["dve"].up())
                elif s[0] == "v":
                    bank = take(dve, Y, turn, s)
                    nc.vector.tensor_tensor(v_pad[:, int(s[1]), PAD:].rearrange("p (v e) -> p v e", e=P)[:, :, 0:HD], bank[:, 0:P].rearrange("p (v d) -> p v d", d=HD),
                                            bv.rearrange("p (v d) -> p v d", d=HD), ALU.add).then_inc(*Y.emptied["dve"].up())

            def softmax_max(turn, n):
                dve.wait_ge(*scored(turn, n + 1))
                if n >= AHEAD:
                    dve.wait_ge(*Y.full(turn, "pT", n - AHEAD, 3))
                else:
                    dve.wait_ge(*X.full_before(turn, "fT", G - 1 if n else G - 2, KC - 1))
                nc.vector.scalar_tensor_tensor(out=S[:, n % AHEAD, :, :], in0=pS[:, :, :].rearrange("p r (h t) -> p (r h) t", t=T),
                                               scalar=float(HD) ** -0.5, in1=mask[:, n // 2:n // 2 + 1, :].to_broadcast([P, RH, T]),
                                               op0=ALU.mult, op1=ALU.add).then_inc(*masked.up())
                dve.wait_ge(*masked(turn, n + 1))
                nc.vector.tensor_reduce(negmax[:, n % AHEAD, :], S[:, n % AHEAD, :, :], AX.X, ALU.max, negate=True).then_inc(*max_found.up())

            def invert(turn, n):
                dve.wait_ge(*exp_done(turn, n + 1))
                nc.vector.reciprocal(rden[:, n % AHEAD, :], wsum[:, n % AHEAD, :]).then_inc(*sums_inverted.up())

            def keep(turn, n):
                bank = take(dve, Y, turn, "pv", n)
                nc.vector.tensor_copy(attT[:, 2 * (n % 2):2 * (n % 2) + 2, n // 2 * T:n // 2 * T + T],
                                      bank[:, 0:2 * T].rearrange("p (c t) -> p c t", c=2)).then_inc(*Y.emptied["dve"].up())

            def norm_out(turn, g):
                if g == 0:
                    dve.wait_ge(*xbo_ready(turn, 1))
                bank = take(dve, X, turn, "o", g)
                nc.vector.tensor_tensor(xbo[:, g, :], bank, xbo[:, g, :], ALU.add).then_inc(*X.emptied["dve"].up())
                dve.wait_ge(*X.out(turn, "o", g))
                nc.vector.bn_stats(bn[:, :], xbo[:, g, :]).then_inc(*dve_step.up())
                dve.wait_ge(*dve_step.last(turn))
                dve.sem_inc(held.sem, 1)
                nc.vector.bn_aggr(mv[:, :], bn[:, :]).then_inc(*dve_step.up())
                dve.wait_ge(*dve_step.last(turn))
                nc.vector.tensor_scalar(veps[:, :], mv[:, 1:2], 1e-6, None, ALU.add).then_inc(*var_ready.up())
                dve.wait_ge(*rstd_ready(turn, g + 1))
                nc.vector.tensor_scalar(xbo[:, g, :], xbo[:, g, :], mv[:, 0:1], rstd[:, 0:1], ALU.subtract, ALU.mult)\
                    .then_inc(*whitened.up())

            def rounds(turn):
                invert(turn, 0)
                softmax_max(turn, 1)
                for n in range(NR):
                    for b in (0, 2):
                        bank = take(dve, ring_at(b), turn, "pT", n, b)
                        nc.vector.tensor_copy(probsT[:, n % 2, 4 * b:4 * b + 4, :], bank.rearrange("p (h t) -> p h t", h=4))\
                            .then_inc(*ring_at(b).emptied["dve"].up())
                    if n + 1 < NR:
                        invert(turn, n + 1)
                    if n + 2 < NR:
                        softmax_max(turn, n + 2)
                    keep(turn, n)
                    if n >= 2 and n % 2 == 0:
                        norm_out(turn, n // 2 - 1)

            def inner(turn, s):
                g = int(s[-1])
                if s[0] == "o":
                    norm_out(turn, g)
                elif s[:2] == "th":
                    bank = take(dve, X, turn, "gx", g)
                    nc.vector.tensor_tensor(gx[:, g, :, :], bank[:, 0:KC * CI].rearrange("p (j o) -> p j o", o=CI),
                                            bg.unsqueeze(1).to_broadcast([P, KC, CI]), ALU.add).then_inc(*X.emptied["dve"].up())
                elif s[:2] == "fT":
                    for j in (0, 2):
                        bank = take(dve, X, turn, "fT", g, j)
                        nc.vector.tensor_copy(fT[:, g % 2, j, :], bank).then_inc(*X.emptied["dve"].up())
                elif s[0] == "f":
                    if g:
                        scale(turn, g - 1)
                    dve.wait_ge(*scored(turn, NR + g + 1))
                    nc.vector.tensor_reduce(nmax[:, g % 2, :], pS[:, :, :], AX.X, ALU.max, negate=True).then_inc(*f_max.up())
                elif s == "y%d" % (G - 2):
                    scale(turn, G - 1)
                elif s[0] == "w":
                    dve.wait_ge(*X.out(turn, "wy", g))
                    nc.vector.bn_stats(stats[:, bass.ds(turn.times(G * 6, g * 6), 6)], wy[:, g % 2, :]).then_inc(*y_stats.up())

            def scale(turn, g):
                dve.wait_ge(*f_exp(turn, g + 1))
                nc.vector.reciprocal(rden[:, g % 2, 0:KC], fsum[:, g % 2, :]).then_inc(*dve_step.up())
                dve.wait_ge(*dve_step.last(turn))
                for i in range(KC):
                    ins = nc.vector.tensor_scalar(f_sb[:, g % 2, i, :], f_sb[:, g % 2, i, :], rden[:, g % 2, i:i + 1], None, ALU.mult)
                ins.then_inc(*f_scaled.up())

            run(dve, front, rounds, inner)

        @block.gpsimd
        def _(pool):
            pool.wait_ge(loaded_rest.sem, loaded_rest.seen)
            pool.wait_ge(ones_set.sem, 2)

            def divide(turn, n):
                pool.wait_ge(*sums_inverted(turn, n + 1))
                nc.gpsimd.tensor_tensor(S[:, n % AHEAD, :, :], S[:, n % AHEAD, :, :],
                                        rden[:, n % AHEAD, :].unsqueeze(2).to_broadcast([P, RH, T]), ALU.mult).then_inc(*weighed.up())

            def front(turn, s):
                if s == "xT":
                    pool.wait_ge(*Y.full(turn, "xT", KC - 1))
                    pool.wait_ge(*x1_ready.before(turn))
                    nc.gpsimd.tensor_tensor(xbo[:, :, :], x[:, :, :], bo.unsqueeze(1).to_broadcast([P, G, D]), ALU.add).then_inc(*xbo_ready.up())

            def rounds(turn):
                def finish(g):
                    pool.wait_ge(*var_ready(turn, g + 1))
                    nc.gpsimd.tensor_tensor(rstd[:, :], veps[:, :], half[:, :], ALU.pow).then_inc(*rstd_ready.up())
                    if g == 0:
                        pool.wait_ge(*x1_stored.before(turn))
                        pool.wait_ge(*X.full_before(turn, "gx", G - 1))
                    pool.wait_ge(*whitened(turn, g + 1))
                    nc.gpsimd.tensor_tensor(xbo[:, g, :], xbo[:, g, :], gamma, ALU.mult).then_inc(*pool_step.up())
                    pool.wait_ge(*pool_step.last(turn))
                    nc.gpsimd.tensor_tensor(x1[:, g, :], xbo[:, g, :], beta, ALU.add).then_inc(*x1_ready.up())

                divide(turn, 0)
                for n in range(NR):
                    if n + 1 < NR:
                        divide(turn, n + 1)
                    if n >= 2 and n % 2 == 0:
                        finish(n // 2 - 1)
                finish(G - 1)

            run(pool, front, rounds, lambda turn, s: None)

        wrong = {s.sem.name: (s.per, s.seen) for s in signals if s.per and s.seen % s.per}
        assert not wrong, wrong


def phase_b(nc, dram, norm):
    G = 2
    N = B // G
    TOK = G * T
    NH, HD = 32, 16
    HC = P // HD
    JS = 2
    STEPS = KC * HD // JS
    DM, DD = 32, 64
    LORA = ["k", "w", "v", "r", "g"]
    PROJECT = {0: ["x2"], 1: ["stats"], 4: ["whiten"], 6: ["n1"], 7: ["shift"], 10: ["h"], 11: ["m0"], 12: ["m1"], 13: ["k0"], 14: ["k1", "m2"], 15: ["td"], 16: ["m3"], 17: ["w"], 18: ["v0"], 20: ["v1"], 22: ["vT"], 24: ["m4"], 26: ["r0"], 28: ["r1"],
               30: ["g0"], 31: ["save"]}
    LATE_PRODUCTS, LATE_ACT, LATE_DVE = {0: ["g1"], 4: ["u"]}, {3: ["g0", "g1"], 4: ["u"]}, {3: ["g0", "g1", "u"]}
    FINISH = {0: ["gn_mean"], 1: ["gn_var"], 2: ["gn_div"], 4: ["gate"], 6: ["o0"], 8: ["o1"], 9: ["stats"], 11: ["whiten"], 12: ["n2"],
              13: ["shift"], 16: ["fk0"], 19: ["fk1"], 21: ["fr0"], 23: ["fr1"], 25: ["fv0"], 27: ["fv1"]}
    p_items = [(("n1", 0), "act"), (("n1", 1), "act"), (("h", 0), "act"), (("h", 1), "act")]
    for name in ("m0", "m1", "k", "m2", "td", "m3", "w", "v", "vT", "m4", "r", "g", "u"):
        who = "dve" if name[0] in "mg" or name == "vT" else "act"
        p_items += [((name, 0), who)] + ([((name, 1), who)] if name not in ("td", "u") else [])
    f_items = [((name, h), who) for name, who in (("gn", "act"), ("o", "dve"), ("n2", "act"), ("fk", "act"), ("fr", "act"), ("fv", "dve"))
               for h in range(2)]
    s_items = [(("v", n), "dve") for n in range(STEPS)]

    with ExitStack() as ctx:
        def sb(name, shape, dt=F32):
            return ctx.enter_context(nc.sbuf_tensor("b_" + name, shape, dt))

        def sig(name, per):
            return Signal(ctx.enter_context(nc.semaphore("b_" + name)), per)

        def pair(name, shape, dt=F32):
            return [sb(name + str(i), shape, dt) for i in range(2)]

        W = {n: sb("w" + n, [P, KC, D]) for n in ("Wk", "Wv", "Wr", "Wg", "Wo", "Wfk", "Wfr", "Wfv")}
        w1, w2a, w2b = sb("w1", [P, KC, 5 * DM]), sb("w2a", [P, D]), sb("w2b", [DM, D])
        td1, td2 = sb("td1", [P, KC, DD]), sb("td2", [DD, D])
        vec = sb("vec", [P, dram["vecs"].shape[1]])
        ident, heads, pick = sb("ident", [P, P]), sb("heads", [P, HC]), sb("pick", [P, HD, P], F32R)
        half = sb("half", [P, 1])
        state = sb("state", [P, B, 2, KC])

        def col(name, c, j=0):
            at = vec_column(name) + KC * j + c
            return vec[:, at:at + 1]

        x1g, wyg, x2 = sb("x1g", [P, G, D]), sb("wyg", [P, G, D]), pair("x2", [P, G, D])
        xn = [sb("xn0", [P, G, D]), sb("xn1", [P, G, D])]
        xT = [sb("xT0", [P, KC, G, T + 1]), sb("xT1", [P, KC, G, T + 1])]
        sx = [sb("sx0", [P, KC, TOK]), sb("sx1", [P, KC, TOK])]
        xm = [sb("xm0", [P, KC, TOK]), sb("xm1", [P, KC, TOK])]
        hid = sb("hid", [P, TOK])
        kT, wT, rT, gT = (pair(n, [P, KC, TOK]) for n in ("kT", "wT", "rT", "gT"))
        v_tm, v_hi, v_lo = pair("v_tm", [P, G, D]), pair("v_hi", [P, KC, TOK], F32R), pair("v_lo", [P, KC, TOK], F32R)
        usum, s0 = pair("usum", [P, G, NH]), pair("s0", [P, KC, G, HD])
        a_kv, S = sb("a_kv", [P, 2, JS, TOK]), sb("S", [P, 2, JS, G, T + 1])
        o, z = sb("o", [P, G, D]), sb("z", [P, KC, TOK])
        bn, mv = [sb("bn0", [P, G, 6]), sb("bn1", [P, G, 6])], [sb("mv0", [P, G, 2]), sb("mv1", [P, G, 2])]
        veps, rstd = [sb("veps0", [P, G]), sb("veps1", [P, G])], [sb("rstd0", [P, G]), sb("rstd1", [P, G])]
        gsum, grstd = sb("gsum", [P, G * NH]), sb("grstd", [P, G * NH])
        gvar = gsum
        flat = [t[:, :, :].rearrange("p g d -> p (g d)").rearrange("p (k n) -> p k n", k=KC) for t in xn]
        u0 = ruk = flat[0]
        hid4, th = x1g[0:DM, 0, 0:TOK], x1g[0:DD, 1, 0:TOK]
        rs = a_kv
        xr, xk = flat[1], z
        rt = sx[1][:, :, :].rearrange("p k n -> p (k n)").rearrange("p (g d) -> p g d", g=G)
        kk = xT[1][:, :, :, :].rearrange("p k g t -> p (k g t)")[:, 0:KC * TOK].rearrange("p (k n) -> p k n", k=KC)
        sq = z[:, :, :].rearrange("p k n -> p (k n)")
        gnewt = sq[:, 0:G * NH]
        pO = ctx.enter_context(nc.psum_tensor("b_pO", [P, G, 512], F32))
        pS, pP, pF = (ctx.enter_context(nc.psum_tensor("b_p" + n, [P, 2, 512], F32)) for n in "SPF")

        def ring_of(name, items):
            emptied = {w: sig(name + "_emptied_" + w, k) for w in ("act", "dve") for k in [[i[1] for i in items].count(w)] if k}
            return Ring(items, sig(name + "_filled", len(items)), emptied, banks=2)

        loaded_w, loaded_k, loaded_v, loaded_f, consts, held = (sig(n, 0) for n in ("loaded_w", "loaded_k", "loaded_v", "loaded_f", "consts", "held"))
        y_loaded, s0_loaded, stored = sig("y_loaded", 32), sig("s0_loaded", 16), sig("stored", 16 * G)
        P_, F_, S_ = ring_of("p", p_items), ring_of("f", f_items), ring_of("s", s_items)
        wy_normed, x2_ready, x2_saved = sig("wy_normed", G), sig("x2_ready", G), sig("x2_saved", 1)
        var_ready, rstd_ready, xn_ready, first_set, shifted = ([sig(n + str(i), k) for i in range(2)] for n, k in
                                                               (("var", 1), ("rstd", 1), ("xn", G), ("first", 1), ("shifted", 1)))
        u0_ready, xm_ready = sig("u0_ready", 1), sig("xm_ready", 2 * len(LORA))
        decay_ready, v_hi_ready, tanh_g, ruk_ready = sig("decay", 2), sig("v_hi_ready", 2), sig("tanh_g", 2), sig("ruk", 1)
        s_first, scanned, rs_ready, summed = (sig(n, STEPS) for n in ("s_first", "scanned", "rs_ready", "summed"))
        own_ready, out_ready = sig("own", 1), sig("out_ready", 1)
        gn_centred, gn_squared, gn_var, gn_root, gn_ready = (sig("gn" + n, 1) for n in ("c", "s", "v", "r", "o"))
        z_ready, xk_ready, xr_ready = sig("z_ready", 2), sig("xk_ready", 1), sig("xr_ready", 1)
        squared, x4_ready = sig("squared", 2), sig("x4_ready", G)
        gn_step, ln_step = sig("gn_step", 7), [sig("ln_step%d" % i, 2 * G) for i in range(2)]
        signals = [loaded_w, loaded_k, loaded_v, loaded_f, consts, held, y_loaded, s0_loaded, stored, wy_normed, x2_ready, x2_saved, u0_ready, xm_ready, decay_ready, v_hi_ready, tanh_g,
                   ruk_ready, s_first, scanned, rs_ready, summed, own_ready, out_ready, gn_centred, gn_squared, gn_var, gn_root, gn_ready,
                   z_ready, xk_ready, xr_ready, squared, x4_ready, gn_step] + ln_step + var_ready + rstd_ready + xn_ready + first_set + shifted
        for ring in (P_, F_, S_):
            signals += [ring.filled] + list(ring.emptied.values())
        x1_v, wy_v = dram["x1"].rearrange("b t d -> t b d"), dram["wy"].rearrange("b t d -> t b d")
        block = ctx.enter_context(nc.Block())

        def fill(pe, ring, psum, turn, *name, moved=()):
            for wait in ring.ready(turn, name, moved):
                pe.wait_ge(*wait)
            return psum[:, ring.bank(*name), :]

        def take(eng, ring, psum, turn, *name):
            eng.wait_ge(*ring.full(turn, *name))
            return psum[:, ring.bank(*name), :]

        def run(eng, scan, project, finish, late={}):
            behind = [s for steps in late.values() for s in steps]

            def turn(i, par, last, next_):
                for n in range(STEPS):
                    scan(i, par, n)
                    for s in FINISH.get(n, ()) if last else ():
                        finish(i + -1, 1 - par, s)
                    for s in late.get(n, ()):
                        project(i, par, s)
                    for s in PROJECT.get(n, ()) if next_ else ():
                        if s not in behind:
                            project(i + 1, 1 - par, s)
                scan(i, par, STEPS)

            for steps in PROJECT.values():
                for s in steps:
                    if s not in behind:
                        project(Turn(None), 0, s)
            turn(Turn(None), 0, False, True)
            with eng.Fori(0, (N - 2) // 2) as reg:
                for u in range(2):
                    turn(Turn(reg, 2, 1 + u), (1 + u) % 2, True, True)
            turn(Turn(None, add=N - 1), (N - 1) % 2, True, False)
            for steps in FINISH.values():
                for s in steps:
                    finish(Turn(None, add=N - 1), (N - 1) % 2, s)

        @block.sync
        def _(sp):
            for s in signals:
                if s.per:
                    sp.sem_inc(s.sem, s.per)

            def wait(value):
                sp.wait_ge(*value)
                sp.sem_inc(held.sem, 1)

            def load(i):
                if (i + -1).exists():
                    wait(x2_saved.all(i + -1))
                sp.dma_start(x1g[:, :, :], x1_v[:, bass.ds(i.times(G), G), :]).then_inc(*y_loaded.up(16))
                sp.dma_start(wyg[:, :, :], wy_v[:, bass.ds(i.times(G), G), :]).then_inc(*y_loaded.up(16))

            def load_state(i, par):
                if (i + -2).exists():
                    wait(rs_ready.all(i + -2))
                sp.dma_start(s0[par][:, :, :, :], dram["state_heads"][:, bass.ds(i.times(KC), KC), :, :]).then_inc(*s0_loaded.up(16))

            def store(i, par):
                for g in range(G):
                    wait(x4_ready(i, g + 1))
                    sp.dma_start(dram["x4"][bass.ds(i.times(G, g), 1), :, :].rearrange("b t d -> t (b d)"), x2[par][:, g, :])\
                        .then_inc(*stored.up(16))

            for tile, name in [(vec, "vecs"), (ident, "ident"), (heads, "heads")]:
                sp.dma_start(tile[:, :], dram[name]).then_inc(*loaded_w.up(16))
            sp.dma_start(state[:, :, :, :], dram["state_rows"]).then_inc(*loaded_w.up(16))
            for h in range(2):
                sp.dma_start(xm[h][:, :, :].rearrange("p k n -> p (k n)"), dram["pick"][:, h * KC * TOK:(h + 1) * KC * TOK]).then_inc(*loaded_w.up(16))
            load(Turn(None))
            load_state(Turn(None), 0)
            load_state(Turn(None, add=1), 1)

            def load_weights(signal, tile, name):
                sp.dma_start(tile[:, :, :], dram[name].rearrange("(k p) n -> p k n", p=P)).then_inc(*signal.up(16))

            load_weights(loaded_k, w1, "L2_xattn_maa_w1")
            w2 = dram["L2_xattn_maa_w2"].rearrange("f d e -> (f d) e")
            for tile, src in [(w2a, w2[0:4 * DM, :]), (w2b, w2[4 * DM:5 * DM, :]), (td2, dram["L2_xattn_td_w2"])]:
                sp.dma_start(tile[:, :], src).then_inc(*loaded_k.up(16))
            load_weights(loaded_k, W["Wk"], "L2_WkT")
            load_weights(loaded_v, td1, "L2_xattn_td_w1")
            for signal, n in [(loaded_v, "Wv"), (loaded_v, "Wr"), (loaded_v, "Wg"), (loaded_f, "Wo"), (loaded_f, "Wfk"), (loaded_f, "Wfr"),
                              (loaded_f, "Wfv")]:
                load_weights(signal, W[n], "L2_%sT" % n)
            load(Turn(None, add=1))
            load(Turn(None, add=2))
            load_state(Turn(None, add=2), 0)
            with sp.Fori(0, (N - 4) // 2) as reg:
                for u in range(2):
                    i = Turn(reg, 2, 1 + u)
                    store(i + -1, u % 2)
                    load(i + 2)
                    load_state(i + 2, (1 + u) % 2)
            store(Turn(None, add=N - 4), 0)
            load(Turn(None, add=N - 1))
            load_state(Turn(None, add=N - 1), 1)
            for i in range(N - 3, N):
                store(Turn(None, add=i), i % 2)
            sp.wait_ge(*stored.all(Turn(None, add=N - 1)))

        @block.tensor
        def _(pe):
            pe.wait_ge(loaded_w.sem, loaded_w.seen)
            pe.wait_ge(consts.sem, 3)

            def two_chunks(ring, psum, i, name, h, w, src, moved=()):
                bank = fill(pe, ring, psum, i, name, h, moved=moved)
                for m in range(2):
                    at = (2 * h + m) * P
                    for c in range(KC):
                        mm = nc.tensor.matmul(bank[:, m * TOK:m * TOK + TOK], w[:, c, at:at + P], src[:, c, :],
                                              start=(c == 0), stop=(c == KC - 1))
                mm.then_inc(*ring.filled.up())

            def tokens(ring, psum, i, name, g, w, src):
                bank = fill(pe, ring, psum, i, name, g)
                for c in range(KC):
                    mm = nc.tensor.matmul(bank, src[:, c, g * T:g * T + T], w[:, c, :], start=(c == 0), stop=(c == KC - 1))
                mm.then_inc(*ring.filled.up())

            def turned(ring, psum, i, name, src):
                for h in range(2):
                    bank = fill(pe, ring, psum, i, name, h)
                    for m in range(2):
                        for g in range(G):
                            mm = nc.tensor.transpose(bank[:, (m * G + g) * T:(m * G + g + 1) * T],
                                                     src[:, g, (2 * h + m) * P:(2 * h + m + 1) * P], ident[:, :])
                    mm.then_inc(*ring.filled.up())

            def project(i, par, s):
                if s == "n1":
                    pe.wait_ge(*xn_ready[0].all(i))
                    turned(P_, pP, i, "n1", xn[0])
                elif s == "h":
                    pe.wait_ge(loaded_k.sem, loaded_k.seen)
                    pe.wait_ge(*u0_ready(i, 1))
                    for k, (lo, size) in enumerate(((0, 4 * DM), (4 * DM, DM))):
                        bank = fill(pe, P_, pP, i, "h", k)
                        for c in range(KC):
                            mm = nc.tensor.matmul(bank[0:size, 0:TOK], w1[:, c, lo:lo + size], u0[:, c, :], start=(c == 0), stop=(c == KC - 1))
                        mm.then_inc(*P_.filled.up())
                elif s[0] == "m":
                    j = int(s[1])
                    for h in range(2):
                        bank = fill(pe, P_, pP, i, s, h, moved=[("h", 1)])
                        for m in range(2):
                            at = (2 * h + m) * P
                            w, src = (w2a[j * DM:j * DM + DM, at:at + P], hid[j * DM:j * DM + DM, :]) if j < 4 else (w2b[:, at:at + P], hid4)
                            mm = nc.tensor.matmul(bank[:, m * TOK:m * TOK + TOK], w, src, start=True, stop=True)
                        mm.then_inc(*P_.filled.up())
                elif s[0] in "krg":
                    j = LORA.index(s[0])
                    pe.wait_ge(*xm_ready(i, 2 * j + 2))
                    two_chunks(P_, pP, i, s[0], int(s[1]), W["W" + s[0]], xm[j % 2])
                elif s == "vT":
                    pe.wait_ge(*P_.out(i, "v", 1))
                    turned(P_, pP, i, "vT", v_tm[par])
                elif s[0] == "v":
                    pe.wait_ge(*xm_ready(i, 6))
                    tokens(P_, pP, i, "v", int(s[1]), W["Wv"], xm[0])
                elif s == "td":
                    pe.wait_ge(loaded_v.sem, loaded_v.seen)
                    pe.wait_ge(*xm_ready(i, 4))
                    bank = fill(pe, P_, pP, i, "td", 0)
                    for c in range(KC):
                        mm = nc.tensor.matmul(bank[0:DD, 0:TOK], td1[:, c, :], xm[1][:, c, :], start=(c == 0), stop=(c == KC - 1))
                    mm.then_inc(*P_.filled.up())
                elif s == "w":
                    for h in range(2):
                        bank = fill(pe, P_, pP, i, "w", h, moved=[("td", 0)])
                        for m in range(2):
                            at = (2 * h + m) * P
                            mm = nc.tensor.matmul(bank[:, m * TOK:m * TOK + TOK], td2[:, at:at + P], th, start=True, stop=True)
                        mm.then_inc(*P_.filled.up())
                elif s == "u":
                    bank = fill(pe, P_, pP, i, "u", 0)
                    pe.wait_ge(*ruk_ready(i, 1))
                    for g in range(G):
                        for c in range(KC):
                            at = g * NH + c * HC
                            mm = nc.tensor.matmul(bank[:, at:at + HC], ruk[:, c, g * T:g * T + T], heads[:, :], start=True, stop=True)
                    mm.then_inc(*P_.filled.up())

            def spread(i, par, n):
                c, j = divmod(n * JS, HD)
                bank = fill(pe, S_, pS, i, "v", n)
                for m in range(JS):
                    nc.tensor.matmul(bank[:, m * TOK:m * TOK + TOK], pick[:, j + m, :], v_hi[par][:, c, :], start=True, stop=False)
                    mm = nc.tensor.matmul(bank[:, m * TOK:m * TOK + TOK], pick[:, j + m, :], v_lo[par][:, c, :], start=False, stop=True)
                mm.then_inc(*S_.filled.up())

            def scan(i, par, n):
                if n == 0:
                    pe.wait_ge(*P_.out(i, "vT", 1))
                    spread(i, par, 0)
                if n + 1 < STEPS:
                    spread(i, par, n + 1)
                if n == 0:
                    return
                if n == 1 and (i + -1).exists():
                    pe.wait_ge(*out_ready(i + -1, 1))
                pe.wait_ge(*rs_ready(i, n))
                for m in range(JS):
                    for g in range(G):
                        at = ((n - 1) * JS + m) * HC
                        mm = nc.tensor.matmul(pO[:, g, at:at + HC], rs[:, (n - 1) % 2, m, g * T:g * T + T], heads[:, :], start=True, stop=True)
                mm.then_inc(*summed.up())

            def finish(i, par, s):
                if s == "gate":
                    pe.wait_ge(loaded_f.sem, loaded_f.seen)
                    pe.wait_ge(*gn_ready(i, 1))
                    turned(F_, pF, i, "gn", o)
                elif s[0] == "o":
                    pe.wait_ge(*z_ready(i, 2))
                    tokens(F_, pF, i, "o", int(s[1]), W["Wo"], z)
                elif s == "n2":
                    pe.wait_ge(*xn_ready[1].all(i))
                    turned(F_, pF, i, "n2", xn[1])
                elif s[:2] == "fk":
                    pe.wait_ge(*xk_ready(i, 1))
                    two_chunks(F_, pF, i, "fk", int(s[2]), W["Wfk"], xk)
                elif s[:2] == "fr":
                    pe.wait_ge(*xr_ready(i, 1))
                    tokens(F_, pF, i, "fr", int(s[2]), W["Wfr"], xr)
                elif s[:2] == "fv":
                    pe.wait_ge(*squared(i, 2))
                    tokens(F_, pF, i, "fv", int(s[2]), W["Wfv"], kk)

            run(pe, scan, project, finish, LATE_PRODUCTS)

        @block.scalar
        def _(act):
            act.wait_ge(loaded_w.sem, loaded_w.seen)

            def affine_norm(ring, psum, i, k, free):
                ln = "L2_xattn_ln%d" % (k + 1)
                if (i + -1).exists():
                    act.wait_ge(*free.all(i + -1))
                nc.scalar.activation(xT[k][:, :, :, 0:1], state[:, bass.ds(i.times(G), G), 1 - k, :].rearrange("p g k -> p k g").unsqueeze(3), ACT.Copy)\
                    .then_inc(*first_set[k].up())
                for h in range(2):
                    bank = take(act, ring, psum, i, "n%d" % (k + 1), h)
                    for m in range(2):
                        c = 2 * h + m
                        ins = nc.scalar.activation(xT[k][:, c, :, 1:T + 1], bank[:, m * TOK:m * TOK + TOK].rearrange("p (g t) -> p g t", g=G),
                                                   ACT.Identity, bias=col(ln + "_b", c), scale=col(ln + "_w", c))
                    ins.then_inc(*ring.emptied["act"].up())

            def project(i, par, s):
                if s == "x2":
                    act.wait_ge(*y_loaded.all(i))
                    for g in range(G):
                        nc.scalar.activation(wyg[:, g, :], wyg[:, g, :], ACT.Identity, bias=norm[:, 1:2], scale=norm[:, 0:1]).then_inc(*wy_normed.up())
                elif s == "n1":
                    affine_norm(P_, pP, i, 0, xm_ready)
                elif s == "h":
                    for k, tile in enumerate((hid[:, :], hid4)):
                        bank = take(act, P_, pP, i, "h", k)
                        nc.scalar.activation(tile, bank[0:tile.shape[0], 0:TOK], ACT.Tanh).then_inc(*P_.emptied["act"].up())
                elif s[0] in "kr":
                    h = int(s[1])
                    bank = take(act, P_, pP, i, s[0], h)
                    if h == 0 and (i + -2).exists():
                        act.wait_ge(*rs_ready.all(i + -2))
                    dst = (kT if s[0] == "k" else rT)[par]
                    nc.scalar.activation(dst[:, 2 * h:2 * h + 2, :], bank.rearrange("p (m n) -> p m n", m=2), ACT.Copy)\
                        .then_inc(*P_.emptied["act"].up())
                elif s == "td":
                    bank = take(act, P_, pP, i, "td", 0)
                    nc.scalar.activation(th, bank[0:DD, 0:TOK], ACT.Tanh).then_inc(*P_.emptied["act"].up())
                elif s == "w":
                    for h in range(2):
                        bank = take(act, P_, pP, i, "w", h)
                        for m in range(2):
                            c = 2 * h + m
                            ins = nc.scalar.activation(wT[par][:, c, :], bank[:, m * TOK:m * TOK + TOK], ACT.Exp, bias=col("L2_xattn_time_decay", c))
                        ins.then_inc(*P_.emptied["act"].up())
                    act.wait_ge(*P_.out(i, "w", 1))
                    for h in range(2):
                        nc.scalar.activation(wT[par][:, 2 * h:2 * h + 2, :], wT[par][:, 2 * h:2 * h + 2, :], ACT.Exp, scale=-1.0).then_inc(*decay_ready.up())
                elif s == "vT":
                    for h in range(2):
                        bank = take(act, P_, pP, i, "vT", h)
                        nc.scalar.activation(v_hi[par][:, 2 * h:2 * h + 2, :], bank.rearrange("p (m n) -> p m n", m=2), ACT.Copy)\
                            .then_inc(*v_hi_ready.up())
                elif s[0] == "v":
                    g = int(s[1])
                    bank = take(act, P_, pP, i, "v", g)
                    if g == 0 and (i + -2).exists():
                        act.wait_ge(*out_ready.all(i + -2))
                    nc.scalar.activation(v_tm[par][:, g, :], bank, ACT.Copy).then_inc(*P_.emptied["act"].up())
                elif s[0] == "g":
                    h = int(s[1])
                    bank = take(act, P_, pP, i, "g", h)
                    if h == 0 and (i + -2).exists():
                        act.wait_ge(*z_ready.all(i + -2))
                    nc.scalar.activation(gT[par][:, 2 * h:2 * h + 2, :], bank.rearrange("p (m n) -> p m n", m=2), ACT.Tanh, scale=0.5)\
                        .then_inc(*tanh_g.up())
                elif s == "u":
                    bank = take(act, P_, pP, i, "u", 0)
                    nc.scalar.activation(usum[par][:, :, :], bank[:, 0:G * NH].rearrange("p (g h) -> p g h", g=G), ACT.Copy)\
                        .then_inc(*P_.emptied["act"].up())

                elif s == "save":
                    if (i + -2).exists():
                        act.wait_ge(*stored.all(i + -2))
                    act.wait_ge(*x2_ready.all(i))
                    nc.scalar.activation(x2[par][:, :, :], wyg[:, :, :], ACT.Copy).then_inc(*x2_saved.up())

            def scan(i, par, n):
                if n == STEPS:
                    return
                if n == 0:
                    act.wait_ge(*s0_loaded.all(i))
                c, j = divmod(n * JS, HD)
                if n >= 2 or (i + -1).exists():
                    act.wait_ge(*(rs_ready(i, n - 1) if n >= 2 else rs_ready(i + -1, STEPS - 1 + n)))
                nc.scalar.activation(S[:, n % 2, :, :, 0:1], s0[par][:, c, :, j:j + JS].rearrange("p g j -> p j g").unsqueeze(3), ACT.Copy).then_inc(*s_first.up())

            def finish(i, par, s):
                if s == "gn_mean":
                    act.wait_ge(*gn_centred(i, 1))
                    if (i + -1).exists():
                        act.wait_ge(*F_.full(i + -1, "fk", 1))
                    nc.scalar.activation(sq, o[:, :, :].rearrange("p g d -> p (g d)"), ACT.Square).then_inc(*gn_squared.up())
                elif s == "gn_var":
                    act.wait_ge(*gn_var(i, 1))
                    nc.scalar.activation(grstd[:, :], gvar[:, :], ACT.Sqrt).then_inc(*gn_root.up())
                elif s == "gate":
                    act.wait_ge(*gn_var(i, 1))
                    for h in range(2):
                        bank = take(act, F_, pF, i, "gn", h)
                        for m in range(2):
                            c = 2 * h + m
                            ins = nc.scalar.activation(z[:, c, :], bank[:, m * TOK:m * TOK + TOK], ACT.Identity,
                                                       bias=col("L2_xattn_gn_b", c), scale=col("L2_xattn_gn_w", c))
                        ins.then_inc(*F_.emptied["act"].up())
                elif s == "n2":
                    affine_norm(F_, pF, i, 1, x4_ready)
                elif s[:2] == "fk":
                    h = int(s[2])
                    bank = take(act, F_, pF, i, "fk", h)
                    if h == 0:
                        act.wait_ge(*xr_ready(i, 1))
                    nc.scalar.activation(kk[:, 2 * h:2 * h + 2, :], bank.rearrange("p (m n) -> p m n", m=2), ACT.Relu).then_inc(*F_.emptied["act"].up())
                    act.wait_ge(*F_.out(i, "fk", h))
                    nc.scalar.activation(kk[:, 2 * h:2 * h + 2, :], kk[:, 2 * h:2 * h + 2, :], ACT.Square).then_inc(*squared.up())
                elif s[:2] == "fr":
                    g = int(s[2])
                    bank = take(act, F_, pF, i, "fr", g)
                    nc.scalar.activation(rt[:, g, :], bank, ACT.Tanh, scale=0.5).then_inc(*F_.emptied["act"].up())

            run(act, scan, project, finish, LATE_ACT)

        @block.vector
        def _(dve):
            dve.wait_ge(loaded_w.sem, loaded_w.seen)
            nc.vector.memset(half[:, :], -0.5).then_inc(*consts.up())
            for h in range(2):
                nc.vector.tensor_copy(pick[:, h * HD // 2:(h + 1) * HD // 2, :], xm[h][:, :, :].rearrange("p k n -> p (k n)").rearrange("p (j q) -> p j q", q=P))\
                    .then_inc(*consts.up())
            dve.wait_ge(consts.sem, 3)

            def statistics(i, x, k):
                for g in range(G):
                    nc.vector.bn_stats(bn[k][:, g, :], x[:, g, :]).then_inc(*ln_step[k].up())
                dve.wait_ge(*ln_step[k].last(i))
                dve.sem_inc(held.sem, 1)
                for g in range(G):
                    nc.vector.bn_aggr(mv[k][:, g, :], bn[k][:, g, :]).then_inc(*ln_step[k].up())
                dve.wait_ge(*ln_step[k].last(i))
                nc.vector.tensor_scalar(veps[k][:, :].unsqueeze(2), mv[k][:, :, 1:2], 1e-5, None, ALU.add).then_inc(*var_ready[k].up())

            def whiten(i, x, k):
                dve.wait_ge(*rstd_ready[k](i, 1))
                for g in range(G):
                    nc.vector.tensor_scalar(xn[k][:, g, :], x[:, g, :], mv[k][:, g, 0:1], rstd[k][:, g:g + 1], ALU.subtract, ALU.mult)\
                        .then_inc(*xn_ready[k].up())

            def shift(ring, i, k):
                dve.wait_ge(*first_set[k](i, 1))
                dve.wait_ge(*ring.out(i, "n%d" % (k + 1), 1))
                nc.vector.tensor_tensor(sx[k][:, :, :].rearrange("p k (g t) -> p (k g) t", g=G), xT[k][:, :, :, 0:T].rearrange("p k g t -> p (k g) t"),
                                        xT[k][:, :, :, 1:T + 1].rearrange("p k g t -> p (k g) t"), ALU.subtract).then_inc(*shifted[k].up())
                dve.wait_ge(*shifted[k](i, 1))

            def mix(dst, name, k):
                for c in range(KC):
                    ins = nc.vector.scalar_tensor_tensor(out=dst[:, c, :].rearrange("p (g t) -> p g t", g=G),
                                                         in0=sx[k][:, c, :].rearrange("p (g t) -> p g t", g=G), scalar=col(name, c),
                                                         in1=xT[k][:, c, :, 1:T + 1], op0=ALU.mult, op1=ALU.add)
                return ins

            def project(i, par, s):
                if s == "stats":
                    dve.wait_ge(*x2_ready.all(i))
                    statistics(i, wyg, 0)
                elif s == "whiten":
                    if (i + -1).exists():
                        dve.wait_ge(*P_.full(i + -1, "u", 0))
                    whiten(i, wyg, 0)
                elif s == "shift":
                    if (i + -1).exists():
                        dve.wait_ge(*xm_ready.all(i + -1))
                    shift(P_, i, 0)
                    mix(u0, "L2_xattn_maa_x", 0).then_inc(*u0_ready.up())
                elif s[0] == "m":
                    j = int(s[1])
                    for h in range(2):
                        bank = take(dve, P_, pP, i, s, h)
                        for m in range(2):
                            c = 2 * h + m
                            ins = nc.vector.scalar_tensor_tensor(out=xm[j % 2][:, c, :], in0=bank[:, m * TOK:m * TOK + TOK],
                                                                 scalar=col("L2_xattn_maa_stack", c, j), in1=sx[0][:, c, :], op0=ALU.add, op1=ALU.mult)
                        ins.then_inc(*P_.emptied["dve"].up())
                elif s == "vT":
                    for h in range(2):
                        bank = take(dve, P_, pP, i, "vT", h)
                        dve.wait_ge(*v_hi_ready(i, h + 1))
                        nc.vector.tensor_tensor(v_lo[par][:, 2 * h:2 * h + 2, :], bank.rearrange("p (m n) -> p m n", m=2),
                                                v_hi[par][:, 2 * h:2 * h + 2, :].bitcast(F32), ALU.subtract).then_inc(*P_.emptied["dve"].up())
                elif s[0] == "g":
                    h = int(s[1])
                    bank = take(dve, P_, pP, i, "g", h)
                    dve.wait_ge(*tanh_g(i, h + 1))
                    gate = gT[par][:, 2 * h:2 * h + 2, :].rearrange("p m n -> p (m n)")
                    nc.vector.scalar_tensor_tensor(out=gate, in0=gate, scalar=1.0, in1=bank, op0=ALU.add, op1=ALU.mult).then_inc(*P_.emptied["dve"].up())
                elif s == "u":
                    dve.wait_ge(*P_.out(i, "r", 1))
                    for c in range(KC):
                        ins = nc.vector.scalar_tensor_tensor(out=ruk[:, c, :], in0=rT[par][:, c, :], scalar=col("L2_xattn_u", c), in1=kT[par][:, c, :],
                                                             op0=ALU.mult, op1=ALU.mult)
                    ins.then_inc(*ruk_ready.up())

            def scan(i, par, n):
                if n == 0:
                    dve.wait_ge(*decay_ready.all(i))
                    dve.wait_ge(*s0_loaded.all(i))
                if n < STEPS:
                    c, j = divmod(n * JS, HD)
                    bank = take(dve, S_, pS, i, "v", n)
                    if n >= 2 or (i + -1).exists():
                        dve.wait_ge(*(summed(i, n - 1) if n >= 2 else summed(i + -1, STEPS - 1 + n)))
                    nc.vector.tensor_tensor(a_kv[:, n % 2, :, :], kT[par][:, c, :].unsqueeze(1).to_broadcast([P, JS, TOK]),
                                            bank.rearrange("p (j n) -> p j n", j=JS), ALU.mult).then_inc(*S_.emptied["dve"].up())
                    dve.wait_ge(*S_.out(i, "v", n))
                    if n >= 2 or (i + -1).exists():
                        dve.wait_ge(*(rs_ready(i, n - 1) if n >= 2 else rs_ready(i + -1, STEPS - 1 + n)))
                    for m in range(JS):
                        for g in range(G):
                            ins = nc.vector.tensor_tensor_scan(S[:, n % 2, m, g, 1:T + 1], wT[par][:, c, g * T:g * T + T],
                                                               a_kv[:, n % 2, m, g * T:g * T + T], s0[par][:, c, g, j + m:j + m + 1], ALU.mult, ALU.add)
                    ins.then_inc(*scanned.up())
                    return
                if (i + -1).exists():
                    dve.wait_ge(*F_.full(i + -1, "gn", 1))
                dve.wait_ge(*P_.out(i, "u", 0))
                nc.vector.tensor_tensor(o[:, :, :].rearrange("p g (h j) -> p (g h) j", j=HD), v_tm[par][:, :, :].rearrange("p g (h j) -> p (g h) j", j=HD),
                                        usum[par][:, :, :].rearrange("p g h -> p (g h)").unsqueeze(2).to_broadcast([P, G * NH, HD]), ALU.mult)\
                    .then_inc(*own_ready.up())
                dve.wait_ge(*own_ready(i, 1))
                dve.wait_ge(*summed.all(i))
                for g in range(G):
                    view = o[:, g, :].rearrange("p (c h j) -> p c h j", c=KC, j=HD)
                    ins = nc.vector.tensor_tensor(view, view, pO[:, g, :].rearrange("p (c j h) -> p c h j", c=KC, j=HD), ALU.add)
                ins.then_inc(*out_ready.up())

            def finish(i, par, s):
                heads_ = o[:, :, :].rearrange("p g (h j) -> p (g h) j", j=HD)
                if s == "gn_mean":
                    dve.wait_ge(*out_ready(i, 1))
                    nc.vector.tensor_reduce(gsum[:, :], heads_, AX.X, ALU.add).then_inc(*gn_step.up())
                    dve.wait_ge(*gn_step.last(i))
                    nc.vector.scalar_tensor_tensor(out=heads_, in0=gsum[:, :].unsqueeze(2).to_broadcast([P, G * NH, HD]), scalar=-1.0 / HD, in1=heads_,
                                                   op0=ALU.mult, op1=ALU.add).then_inc(*gn_centred.up())
                elif s == "gn_var":
                    dve.wait_ge(*gn_squared(i, 1))
                    nc.vector.tensor_reduce(gvar[:, :], sq.rearrange("p (h j) -> p h j", j=HD), AX.X, ALU.add).then_inc(*gn_step.up())
                    dve.wait_ge(*gn_step.last(i))
                    nc.vector.tensor_scalar(gvar[:, :], gvar[:, :], 1.0 / HD, 1e-5, ALU.mult, ALU.add).then_inc(*gn_var.up())
                elif s == "gn_div":
                    dve.wait_ge(*gn_root(i, 1))
                    nc.vector.reciprocal(grstd[:, :], grstd[:, :]).then_inc(*gn_step.up())
                    dve.wait_ge(*gn_step.last(i))
                    nc.vector.tensor_tensor(gnewt, grstd[:, :], grstd[:, :], ALU.mult).then_inc(*gn_step.up())
                    dve.wait_ge(*gn_step.last(i))
                    nc.vector.tensor_tensor(gnewt, gnewt, gvar[:, :], ALU.mult).then_inc(*gn_step.up())
                    dve.wait_ge(*gn_step.last(i))
                    nc.vector.tensor_scalar(gnewt, gnewt, -0.5, 1.5, ALU.mult, ALU.add).then_inc(*gn_step.up())
                    dve.wait_ge(*gn_step.last(i))
                    nc.vector.tensor_tensor(grstd[:, :], grstd[:, :], gnewt, ALU.mult).then_inc(*gn_step.up())
                    dve.wait_ge(*gn_step.last(i))
                    nc.vector.tensor_tensor(heads_, heads_, grstd[:, :].unsqueeze(2).to_broadcast([P, G * NH, HD]), ALU.mult).then_inc(*gn_ready.up())
                elif s == "gate":
                    for h in range(2):
                        dve.wait_ge(*F_.out(i, "gn", h))
                        part = z[:, 2 * h:2 * h + 2, :].rearrange("p m n -> p (m n)")
                        nc.vector.scalar_tensor_tensor(out=part, in0=part, scalar=0.5, in1=gT[par][:, 2 * h:2 * h + 2, :].rearrange("p m n -> p (m n)"),
                                                       op0=ALU.mult, op1=ALU.mult).then_inc(*z_ready.up())
                elif s[0] == "o":
                    g = int(s[1])
                    bank = take(dve, F_, pF, i, "o", g)
                    if g == 0:
                        dve.wait_ge(*x2_saved(i, 1))
                    nc.vector.tensor_tensor(x2[par][:, g, :], x2[par][:, g, :], bank, ALU.add).then_inc(*F_.emptied["dve"].up())
                elif s == "stats":
                    dve.wait_ge(*F_.out(i, "o", 1))
                    statistics(i, x2[par], 1)
                elif s == "whiten":
                    if (i + -1).exists():
                        dve.wait_ge(*F_.full(i + -1, "fr", 1))
                    whiten(i, x2[par], 1)
                elif s == "shift":
                    if (i + -1).exists():
                        dve.wait_ge(*x4_ready.all(i + -1))
                    shift(F_, i, 1)
                    mix(xk, "L2_xattn_ffn_maa_k", 1).then_inc(*xk_ready.up())
                    mix(xr, "L2_xattn_ffn_maa_r", 1).then_inc(*xr_ready.up())
                elif s[:2] == "fv":
                    g = int(s[2])
                    dve.wait_ge(*F_.out(i, "fr", g))
                    bank = take(dve, F_, pF, i, "fv", g)
                    nc.vector.scalar_tensor_tensor(out=rt[:, g, :], in0=rt[:, g, :], scalar=1.0, in1=bank, op0=ALU.add, op1=ALU.mult)\
                        .then_inc(*F_.emptied["dve"].up())
                    dve.wait_ge(*F_.out(i, "fv", g))
                    nc.vector.scalar_tensor_tensor(out=x2[par][:, g, :], in0=rt[:, g, :], scalar=0.5, in1=x2[par][:, g, :], op0=ALU.mult, op1=ALU.add)\
                        .then_inc(*x4_ready.up())

            run(dve, scan, project, finish, LATE_DVE)

        @block.gpsimd
        def _(pool):
            pool.wait_ge(consts.sem, 3)

            def deviation(i, k):
                pool.wait_ge(*var_ready[k](i, 1))
                nc.gpsimd.tensor_tensor(rstd[k][:, :], veps[k][:, :], half[:, 0:1].to_broadcast([P, G]), ALU.pow).then_inc(*rstd_ready[k].up())

            def project(i, par, s):
                if s == "x2":
                    for g in range(G):
                        pool.wait_ge(*wy_normed(i, g + 1))
                        nc.gpsimd.tensor_tensor(wyg[:, g, :], wyg[:, g, :], x1g[:, g, :], ALU.add).then_inc(*x2_ready.up())
                elif s == "stats":
                    deviation(i, 0)
                elif s[0] == "m":
                    j = int(s[1])
                    for h in range(2):
                        pool.wait_ge(*P_.out(i, s, h))
                        part = xm[j % 2][:, 2 * h:2 * h + 2, :].rearrange("p k (g t) -> p (k g) t", g=G)
                        nc.gpsimd.tensor_tensor(part, part, xT[0][:, 2 * h:2 * h + 2, :, 1:T + 1].rearrange("p k g t -> p (k g) t"), ALU.add)\
                            .then_inc(*xm_ready.up())

            def scan(i, par, n):
                if n == STEPS:
                    return
                if n == 0:
                    pool.wait_ge(*P_.out(i, "r", 1))
                c = n * JS // HD
                pool.wait_ge(*s_first(i, n + 1))
                pool.wait_ge(*scanned(i, n + 1))
                nc.gpsimd.tensor_tensor(rs[:, n % 2, :, :].rearrange("p j (g t) -> p j g t", g=G), S[:, n % 2, :, :, 0:T],
                                        rT[par][:, c, :].rearrange("p (g t) -> p g t", g=G).unsqueeze(1).to_broadcast([P, JS, G, T]), ALU.mult).then_inc(*rs_ready.up())

            def finish(i, par, s):
                if s == "stats":
                    deviation(i, 1)

            run(pool, scan, project, finish)

        wrong = {s.sem.name: (s.per, s.seen) for s in signals if s.per and s.seen % s.per}
        assert not wrong, wrong


def phase_c(nc, dram):
    NH, HD = 16, 32
    SLOTS = P // HD
    FC = 4 * D // P
    items = [(("cT", c), "dve") for c in range(KC)] + [(("k", c), "act") for c in range(KC)]
    items += [(("n1", c), "act") for c in range(KC)] + [(("q", c), "act") for c in range(KC)] + [(("v", g), "dve") for g in range(G)]
    for g in range(G):
        items += [(("pT", g, b), "act" if b % 2 else "dve") for b in range(4)]
        items += ([(("o", g - 1), "dve")] if g else []) + [(("pv", g), "dve")]
    items.append((("o", G - 1), "dve"))
    items += [(("n2", c), "act") for c in range(KC)] + [(("fc", m), "act") for m in range(FC)] + [(("pr", g), "dve") for g in range(G)]

    with ExitStack() as ctx:
        def sb(name, shape, dt=F32):
            return ctx.enter_context(nc.sbuf_tensor("c_" + name, shape, dt))

        def sig(name, per):
            return Signal(ctx.enter_context(nc.semaphore("c_" + name)), per)

        W = {n: sb(n, [P, KC, D]) for n in ("q_w", "k_w", "v_w", "cproj_w")}
        fc_w, proj_w = sb("fc_w", [P, KC, 4 * D]), sb("proj_w", [P, FC, D])
        vec = sb("vec", [P, dram["vecs"].shape[1]])
        rows, ident = sb("rows", [P, 3 * D]), sb("ident", [P, P])
        v_b, cproj_b, proj_b = (rows[:, i * D:i * D + D] for i in range(3))
        half = sb("half", [P, G])
        x, c_tm, xn = sb("x", [P, G, D]), sb("c", [P, G, D]), sb("xn", [P, G, D])
        xT, cT, qT, kT = (sb(n, [P, KC, TOK]) for n in ("xT", "cT", "qT", "kT"))
        attT = cT
        v_tm = sb("v_tm", [P, G, D])
        wide = sb("wide", [P, 4, NH * T])
        S = [wide[:, 0, :].rearrange("p (h t) -> p h t", t=T), wide[:, 1, :].rearrange("p (h t) -> p h t", t=T),
             xn[:, :, :].rearrange("p g d -> p (g d)").rearrange("p (h t) -> p h t", t=T)]
        probsT = wide[:, 2:4, :].rearrange("p a (h t) -> p a h t", t=T)
        fcT = wide[:, :, :].rearrange("p a (m n) -> p (a m) n", n=TOK)
        mask_u8, limit = sb("mask_u8", [P, G, T], U8), sb("limit", [P, G, T])
        negmax, wsum, rden = (sb(n, [P, 3, NH]) for n in ("negmax", "wsum", "rden"))
        bn, mv = sb("bn", [P, G, 6]), sb("mv", [P, G, 2])
        veps, rstd = sb("veps", [P, G]), sb("rstd", [P, G])
        pS = ctx.enter_context(nc.psum_tensor("c_pS", [P, 4, 512], F32))
        pR = ctx.enter_context(nc.psum_tensor("c_pR", [P, RING, 512], F32))

        loaded_w, loaded_q, loaded_mlp = sig("loaded_w", 0), sig("loaded_q", 0), sig("loaded_mlp", 0)
        consts, held = sig("consts", 0), sig("held", 0)
        x_loaded, c_loaded, mask_loaded, stored = sig("x_loaded", 16), sig("c_loaded", 16), sig("mask_loaded", 16), sig("stored", 16 * G)
        filled = sig("filled", len(items))
        emptied = {w: sig("emptied_" + w, [i[1] for i in items].count(w)) for w in ("act", "dve")}
        ring = Ring(items, filled, emptied)
        limit_sign, limit_ready = sig("limit_sign", 1), sig("limit_ready", 1)
        scored, masked, max_found, exp_done = (sig(n, G) for n in ("scored", "masked", "max_found", "exp_done"))
        sums_inverted, weighed = sig("sums_inverted", G), sig("weighed", G)
        var_ready, rstd_ready, xn_ready = sig("var_ready", 2 * G), sig("rstd_ready", 2 * G), sig("xn_ready", 2 * G)
        xb_ready, hb_ready, out_ready = sig("xb_ready", 1), sig("hb_ready", 1), sig("out_ready", G)
        dve_step = sig("dve_step", 16)
        signals = [s for s in locals().values() if isinstance(s, Signal)] + list(emptied.values())
        x_v, c_v = dram["x4"].rearrange("b t d -> t b d"), dram["ctx_2048"].rearrange("b t d -> t b d")
        block = ctx.enter_context(nc.Block())

        def col(name, c):
            at = vec_column(name) + c
            return vec[:, at:at + 1]

        @block.sync
        def _(sp):
            for s in signals:
                if s.per:
                    sp.sem_inc(s.sem, s.per)

            def load_context(turn, guard):
                if guard:
                    sp.wait_ge(*ring.full_before(turn, "cT", KC - 1))
                    sp.sem_inc(held.sem, 1)
                sp.dma_start(c_tm[:, :, :], c_v[:, bass.ds(turn.times(G), G), :]).then_inc(*c_loaded.up(16))
                if guard:
                    sp.wait_ge(*limit_sign.before(turn))
                    sp.sem_inc(held.sem, 1)
                sp.dma_start(mask_u8[:, :, :], dram["mask_rows"][:, bass.ds(turn.times(G), G), :]).then_inc(*mask_loaded.up(16))

            def load_rows(turn):
                sp.wait_ge(*stored.before(turn))
                sp.sem_inc(held.sem, 1)
                sp.dma_start(x[:, :, :], x_v[:, bass.ds(turn.times(G), G), :]).then_inc(*x_loaded.up(16))

            def store(turn):
                for g in range(G):
                    sp.wait_ge(*out_ready(turn, g + 1))
                    sp.sem_inc(held.sem, 1)
                    sp.dma_start(dram["out"][bass.ds(turn.times(G, g), 1), :, :].rearrange("b t d -> t (b d)"),
                                 x[:, g, :]).then_inc(*stored.up(16))

            for tile, name in [(vec, "vecs"), (ident, "ident"), (rows, "rows_c")]:
                sp.dma_start(tile[:, :], dram[name]).then_inc(*loaded_w.up(16))
            load_context(Turn(None), False)
            for signal, tile, name in [(loaded_w, W["k_w"], "k_w"), (loaded_w, W["v_w"], "v_w"), (loaded_q, W["q_w"], "q_w"),
                                       (loaded_q, W["cproj_w"], "cproj_w"), (loaded_mlp, fc_w, "fc_w"), (loaded_mlp, proj_w, "proj_w")]:
                sp.dma_start(tile[:, :, :], dram["L3_xattn_" + name].rearrange("(k p) n -> p k n", p=P)).then_inc(*signal.up(16))
                if name == "v_w":
                    load_rows(Turn(None))
            with sp.Fori(0, NG - 1) as reg:
                turn = Turn(reg)
                load_context(turn + 1, True)
                store(turn)
                load_rows(turn + 1)
            store(Turn(None, add=NG - 1))
            sp.wait_ge(*stored.all(NG - 1))

        @block.tensor
        def _(pe):
            pe.wait_ge(loaded_w.sem, loaded_w.seen)

            def fill(turn, *name, moved=()):
                for wait in ring.ready(turn, name, moved):
                    pe.wait_ge(*wait)
                return pR[:, ring.bank(*name), :]

            def turned(turn, name, src):
                for c in range(KC):
                    bank = fill(turn, name, c)
                    for g in range(G):
                        mm = nc.tensor.transpose(bank[:, g * T:g * T + T], src[:, g, c * P:c * P + P], ident[:, :])
                    mm.then_inc(*filled.up())

            def linear(turn, name, w, src, chunks, turned):
                for m in range(chunks):
                    bank = fill(turn, name, m, moved=[(turned, KC - 1)])
                    for c in range(KC):
                        mm = nc.tensor.matmul(bank, w[:, c, m * P:m * P + P], src[:, c, :], start=(c == 0), stop=(c == KC - 1))
                    mm.then_inc(*filled.up())

            def scores(turn, g):
                if g:
                    pe.wait_ge(*masked(turn, g))
                else:
                    pe.wait_ge(*masked.before(turn))
                for c in range(KC):
                    for r in range(4):
                        at = slice(HD * r, HD * r + HD)
                        mm = nc.tensor.matmul(pS[:, r, c * T:c * T + T], qT[at, c, g * T:g * T + T], kT[at, c, g * T:g * T + T],
                                              start=True, stop=True)
                mm.then_inc(*scored.up())

            def project(turn, g):
                bank = fill(turn, "o", g, moved=[("pv", g)])
                for c in range(KC):
                    mm = nc.tensor.matmul(bank, attT[:, c, g * T:g * T + T], W["cproj_w"][:, c, :], start=(c == 0), stop=(c == KC - 1))
                mm.then_inc(*filled.up())

            with pe.Fori(0, NG) as turn:
                pe.wait_ge(*c_loaded(turn, 16))
                turned(turn, "cT", c_tm)
                linear(turn, "k", W["k_w"], cT, KC, "cT")
                pe.wait_ge(*xn_ready(turn, G))
                turned(turn, "n1", xn)
                pe.wait_ge(loaded_q.sem, loaded_q.seen)
                linear(turn, "q", W["q_w"], xT, KC, "n1")
                pe.wait_ge(*ring.out(turn, "q", KC - 1))
                scores(turn, 0)
                for g in range(G):
                    bank = fill(turn, "v", g)
                    for c in range(KC):
                        mm = nc.tensor.matmul(bank, cT[:, c, g * T:g * T + T], W["v_w"][:, c, :], start=(c == 0), stop=(c == KC - 1))
                    mm.then_inc(*filled.up())
                scores(turn, 1)
                for g in range(G):
                    pe.wait_ge(*weighed(turn, g + 1))
                    for b in range(4):
                        bank = fill(turn, "pT", g, b)
                        for i in range(4):
                            mm = nc.tensor.transpose(bank[:, i * T:i * T + T], S[g % 3][:, 4 * b + i, :], ident[:, :])
                        mm.then_inc(*filled.up())
                    if g + 2 < G:
                        scores(turn, g + 2)
                    if g:
                        project(turn, g - 1)
                    bank = fill(turn, "pv", g, moved=[("v", G - 1)] + [("pT", g, b) for b in range(4)])
                    for h in range(NH):
                        c, r = divmod(h, SLOTS)
                        mm = nc.tensor.matmul(bank[r * HD:r * HD + HD, c * T:c * T + T], v_tm[:, g, h * HD:h * HD + HD], probsT[:, g % 2, r * KC + c, :],
                                              start=True, stop=True)
                    mm.then_inc(*filled.up())
                project(turn, G - 1)
                pe.wait_ge(*xn_ready(turn, 2 * G))
                turned(turn, "n2", xn)
                pe.wait_ge(loaded_mlp.sem, loaded_mlp.seen)
                linear(turn, "fc", fc_w, xT, FC, "n2")
                for g in range(G):
                    bank = fill(turn, "pr", g, moved=[("fc", FC - 1)])
                    for m in range(FC):
                        mm = nc.tensor.matmul(bank, fcT[:, m, g * T:g * T + T], proj_w[:, m, :], start=(m == 0), stop=(m == FC - 1))
                    mm.then_inc(*filled.up())

        @block.scalar
        def _(act):
            act.wait_ge(loaded_w.sem, loaded_w.seen)

            def drain(turn, dst, *name, func=ACT.Copy, **kw):
                act.wait_ge(*ring.full(turn, *name))
                nc.scalar.activation(dst, pR[:, ring.bank(*name), :], func, **kw).then_inc(*emptied["act"].up())

            def exp_half(turn, g, part):
                k = g % 3
                if part == 0:
                    act.wait_ge(*max_found(turn, g + 1))
                for h in range(part * NH // 2, (part + 1) * NH // 2):
                    ins = nc.scalar.activation(S[k][:, h, :], S[k][:, h, :], ACT.Exp, bias=negmax[:, k, h:h + 1], accum_out=wsum[:, k, h:h + 1])
                if part:
                    ins.then_inc(*exp_done.up())

            with act.Fori(0, NG) as turn:
                act.wait_ge(*scored.before(turn))
                for c in range(KC):
                    drain(turn, kT[:, c, :], "k", c, func=ACT.Identity, bias=col("L3_xattn_k_b", c))
                for c in range(KC):
                    drain(turn, xT[:, c, :], "n1", c, func=ACT.Identity, bias=col("L3_xattn_ln1_b", c), scale=col("L3_xattn_ln1_w", c))
                for c in range(KC):
                    drain(turn, qT[:, c, :], "q", c, func=ACT.Identity, bias=col("L3_xattn_q_b", c))
                exp_half(turn, 0, 0)
                exp_half(turn, 0, 1)
                for g in range(G):
                    if g + 1 < G:
                        exp_half(turn, g + 1, 0)
                    for b in (1, 3):
                        drain(turn, wide[:, 2 + g % 2, b * 512:b * 512 + 512], "pT", g, b)
                    if g + 1 < G:
                        exp_half(turn, g + 1, 1)
                for c in range(KC):
                    drain(turn, xT[:, c, :], "n2", c, func=ACT.Identity, bias=col("L3_xattn_ln2_b", c), scale=col("L3_xattn_ln2_w", c))
                for m in range(FC):
                    drain(turn, fcT[:, m, :], "fc", m, func=ACT.Gelu_apprx_tanh, bias=col("L3_xattn_fc_b", m))

        @block.vector
        def _(dve):
            dve.wait_ge(loaded_w.sem, loaded_w.seen)
            nc.vector.memset(half[:, :], -0.5).then_inc(*consts.up())

            def take(turn, *name):
                dve.wait_ge(*ring.full(turn, *name))
                return pR[:, ring.bank(*name), :]

            def statistics(turn, g):
                nc.vector.bn_stats(bn[:, g, :], x[:, g, :]).then_inc(*dve_step.up())
                dve.wait_ge(*dve_step.last(turn))
                dve.sem_inc(held.sem, 1)
                nc.vector.bn_aggr(mv[:, g, :], bn[:, g, :]).then_inc(*dve_step.up())
                dve.wait_ge(*dve_step.last(turn))
                nc.vector.tensor_scalar(veps[:, g:g + 1], mv[:, g, 1:2], 1e-5, None, ALU.add).then_inc(*var_ready.up())

            def whiten(turn, which, g):
                dve.wait_ge(*rstd_ready(turn, which * G + g + 1))
                nc.vector.tensor_scalar(xn[:, g, :], x[:, g, :], mv[:, g, 0:1], rstd[:, g:g + 1], ALU.subtract, ALU.mult).then_inc(*xn_ready.up())

            def softmax_max(turn, g):
                dve.wait_ge(*scored(turn, g + 1))
                dve.wait_ge(*(ring.full(turn, "pT", g - 3, 3) if g >= 3 else ring.full_before(turn, "pr", G - 1) if g < 2 else ring.full(turn, "n1", KC - 1)))
                nc.vector.scalar_tensor_tensor(out=S[g % 3], in0=pS[:, :, :].rearrange("p r (h t) -> p (r h) t", t=T),
                                               scalar=float(np.float32(1) / np.sqrt(HD).astype(np.float32)),
                                               in1=limit[:, g:g + 1, :].to_broadcast([P, NH, T]), op0=ALU.mult, op1=ALU.min)\
                    .then_inc(*masked.up())
                dve.wait_ge(*masked(turn, g + 1))
                nc.vector.tensor_reduce(negmax[:, g % 3, :], S[g % 3], AX.X, ALU.max, negate=True).then_inc(*max_found.up())

            def invert(turn, g):
                dve.wait_ge(*exp_done(turn, g + 1))
                nc.vector.reciprocal(rden[:, g % 3, :], wsum[:, g % 3, :]).then_inc(*sums_inverted.up())

            def keep(turn, g):
                bank = take(turn, "pv", g)
                nc.vector.tensor_copy(attT[:, :, g * T:g * T + T], bank.rearrange("p (c t) -> p c t", c=KC)).then_inc(*emptied["dve"].up())

            def residual(turn, g):
                bank = take(turn, "o", g)
                if g == 0:
                    dve.wait_ge(*xb_ready(turn, 1))
                nc.vector.tensor_tensor(x[:, g, :], x[:, g, :], bank, ALU.add).then_inc(*emptied["dve"].up())
                dve.wait_ge(*ring.out(turn, "o", g))
                statistics(turn, g)

            dve.wait_ge(consts.sem, 1)
            with dve.Fori(0, NG) as turn:
                for c in range(KC):
                    bank = take(turn, "cT", c)
                    nc.vector.tensor_copy(cT[:, c, :], bank).then_inc(*emptied["dve"].up())
                dve.wait_ge(*x_loaded(turn, 16))
                dve.wait_ge(*ring.full_before(turn, "n2", KC - 1))
                for g in range(G):
                    statistics(turn, g)
                for g in range(G):
                    whiten(turn, 0, g)
                dve.wait_ge(*mask_loaded(turn, 16))
                nc.vector.tensor_scalar(limit[:, :, :], mask_u8[:, :, :], 2.0, -1.0, ALU.mult, ALU.add).then_inc(*limit_sign.up())
                dve.wait_ge(*limit_sign(turn, 1))
                nc.vector.tensor_scalar(limit[:, :, :], limit[:, :, :], FMAX, None, ALU.mult).then_inc(*limit_ready.up())
                dve.wait_ge(*limit_ready(turn, 1))
                softmax_max(turn, 0)
                for g in range(G):
                    bank = take(turn, "v", g)
                    nc.vector.tensor_tensor(v_tm[:, g, :], bank, v_b, ALU.add).then_inc(*emptied["dve"].up())
                invert(turn, 0)
                softmax_max(turn, 1)
                for g in range(G):
                    for b in (0, 2):
                        bank = take(turn, "pT", g, b)
                        nc.vector.tensor_copy(wide[:, 2 + g % 2, b * 512:b * 512 + 512], bank).then_inc(*emptied["dve"].up())
                    if g + 1 < G:
                        invert(turn, g + 1)
                    if g + 2 < G:
                        softmax_max(turn, g + 2)
                    if g:
                        residual(turn, g - 1)
                    keep(turn, g)
                residual(turn, G - 1)
                for g in range(G):
                    whiten(turn, 1, g)
                dve.wait_ge(*hb_ready(turn, 1))
                for g in range(G):
                    bank = take(turn, "pr", g)
                    nc.vector.tensor_tensor(x[:, g, :], x[:, g, :], bank, ALU.add).then_inc(*emptied["dve"].up())
                    out_ready_after = ring.out(turn, "pr", g)
                    dve.wait_ge(*out_ready_after)
                    nc.vector.memset(bn[:, 0, 0:1], 0.0).then_inc(*out_ready.up())

        @block.gpsimd
        def _(pool):
            pool.wait_ge(loaded_w.sem, loaded_w.seen)
            pool.wait_ge(consts.sem, 1)

            def deviation(turn, which, g):
                pool.wait_ge(*var_ready(turn, which * G + g + 1))
                nc.gpsimd.tensor_tensor(rstd[:, g:g + 1], veps[:, g:g + 1], half[:, 0:1], ALU.pow).then_inc(*rstd_ready.up())

            with pool.Fori(0, NG) as turn:
                for g in range(G):
                    deviation(turn, 0, g)
                pool.wait_ge(*xn_ready(turn, G))
                nc.gpsimd.tensor_tensor(x[:, :, :], x[:, :, :], cproj_b.unsqueeze(1).to_broadcast([P, G, D]), ALU.add).then_inc(*xb_ready.up())
                for g in range(G):
                    if g == 3:
                        deviation(turn, 1, 0)
                    pool.wait_ge(*sums_inverted(turn, g + 1))
                    nc.gpsimd.tensor_tensor(S[g % 3], S[g % 3], rden[:, g % 3, :].unsqueeze(2).to_broadcast([P, NH, T]),
                                            ALU.mult).then_inc(*weighed.up())
                for g in range(1, G):
                    deviation(turn, 1, g)
                pool.wait_ge(*xn_ready(turn, 2 * G))
                nc.gpsimd.tensor_tensor(x[:, :, :], x[:, :, :], proj_b.unsqueeze(1).to_broadcast([P, G, D]), ALU.add).then_inc(*hb_ready.up())

        wrong = {s.sem.name: (s.per, s.seen) for s in signals if s.per and s.seen % s.per}
        assert not wrong, wrong


def phase_norm(nc, dram, stats, norm):
    with ExitStack() as ctx:
        par, mv = ctx.enter_context(nc.sbuf_tensor("n_par", [P, 2], F32)), ctx.enter_context(nc.sbuf_tensor("n_mv", [P, 2], F32))
        half, rstd = ctx.enter_context(nc.sbuf_tensor("n_half", [P, 1], F32)), ctx.enter_context(nc.sbuf_tensor("n_rstd", [P, 1], F32))
        loaded, var_ready, rstd_ready, step = (ctx.enter_context(nc.semaphore("n_" + n)) for n in ("loaded", "var", "rstd", "step"))
        block = ctx.enter_context(nc.Block())

        @block.sync
        def _(sp):
            sp.dma_start(par[:, :], dram["L1_affine"]).then_inc(loaded, 16)

        @block.gpsimd
        def _(pool):
            pool.wait_ge(var_ready, 2)
            nc.gpsimd.tensor_tensor(rstd[:, :], mv[:, 1:2], half[:, :], ALU.pow).then_inc(rstd_ready, 1)

        @block.vector
        def _(dve):
            nc.vector.memset(half[:, :], -0.5).then_inc(var_ready, 1)
            nc.vector.bn_aggr(mv[:, :], stats[:, :]).then_inc(step, 1)
            dve.wait_ge(step, 1)
            nc.vector.tensor_scalar(mv[:, 1:2], mv[:, 1:2], 1e-5, None, ALU.add).then_inc(var_ready, 1)
            dve.wait_ge(loaded, 16)
            dve.wait_ge(rstd_ready, 1)
            nc.vector.tensor_tensor(norm[:, 0:1], rstd[:, :], par[:, 0:1], ALU.mult).then_inc(step, 1)
            dve.wait_ge(step, 2)
            nc.vector.tensor_tensor(mv[:, 0:1], mv[:, 0:1], norm[:, 0:1], ALU.mult).then_inc(step, 1)
            dve.wait_ge(step, 3)
            nc.vector.tensor_tensor(norm[:, 1:2], par[:, 1:2], mv[:, 0:1], ALU.subtract).then_inc(step, 1)
            dve.wait_ge(step, 4)


def program(nc, dram):
    with ExitStack() as ctx:
        stats = ctx.enter_context(nc.sbuf_tensor("stats", [P, B * 6], F32))
        norm = ctx.enter_context(nc.sbuf_tensor("norm", [P, 2], F32))
        phase_a(nc, dram, stats)
        phase_norm(nc, dram, stats, norm)
        phase_b(nc, dram, norm)
        phase_c(nc, dram)


def _layout(inputs):
    a = {n: np.asarray(v) for n, v in inputs.items()}
    out = {n: a[n] for n in ("x", "ctx_2048", "mask_Bx1xSxS2_ff0", "L0_xattn_Wq", "L0_xattn_Wk", "L0_xattn_Wv", "L0_xattn_Wo",
                             "L2_xattn_maa_w1", "L2_xattn_maa_w2", "L2_xattn_td_w1", "L2_xattn_td_w2",
                             "L3_xattn_q_w", "L3_xattn_k_w", "L3_xattn_v_w", "L3_xattn_cproj_w", "L3_xattn_fc_w", "L3_xattn_proj_w")}
    for n in ("Wg", "Wtheta", "Wphi", "Wz"):
        out["L1_" + n + "T"] = a["L1_xattn_" + n].T
    for n in ("Wk", "Wv", "Wr", "Wg", "Wo", "Wfk", "Wfr", "Wfv"):
        out["L2_" + n + "T"] = a["L2_xattn_" + n].T
    out["vecs"] = np.concatenate([a[n].reshape(-1, P).T for n in VECS], axis=1)
    out["bk_wide"] = np.broadcast_to(a["L0_xattn_bk"].reshape(8, 1, 16), (8, 4, 16)).reshape(KC, P).T
    out["rows_a"] = np.concatenate([np.broadcast_to(a[n][None, :], (P, a[n].size)) for n in ROWS_A], axis=1)
    out["rows_c"] = np.concatenate([np.broadcast_to(a[n][None, :], (P, a[n].size)) for n in ROWS_C], axis=1)
    out["L1_ci"] = np.stack([a["L1_xattn_bphi"], a["L1_xattn_btheta"]], axis=1)
    out["L1_bz"] = a["L1_xattn_bz"].reshape(P, 1)
    out["L1_affine"] = np.stack([a["L1_xattn_gamma"], a["L1_xattn_beta"]], axis=1)
    out["mask_rows"] = np.broadcast_to(np.ascontiguousarray(a["mask_BxS2_bf1"]).view(np.uint8)[None], (P, B, T))
    state = a["ctx_2048"]
    out["state_rows"] = state[:, 0:2].reshape(B, 2, KC, P).transpose(3, 0, 1, 2)
    out["state_heads"] = state[:, 2:18].reshape(B // 2, 2, KC, P, 16).transpose(3, 0, 2, 1, 4).reshape(P, B // 2 * KC, 2, 16)
    out["ident"] = np.eye(P, dtype=np.float32)
    p = np.arange(P)
    out["parity"] = (p[:, None] // 16 % 2 == np.arange(2)[None, :]).astype(np.float32)
    out["heads"] = (p[:, None] // 16 == np.arange(P // 16)[None, :]).astype(np.float32)
    out["pick"] = ((p[:, None, None] // 16 == p[None, None, :] // 16)
                   & (p[:, None, None] % 16 == np.arange(16)[None, :, None])).astype(np.float32).reshape(P, -1)
    return {n: np.ascontiguousarray(v) for n, v in out.items()}


def kernel(**inputs):
    import concourse.bacc as bacc
    from concourse.bass_utils import run_bass_kernel_spmd as run

    arrays = _layout(inputs)
    nc = bacc.Bacc("TRN2", target_bir_lowering=False, num_devices=1)
    dram = {n: nc.dram_tensor(n, v.shape, mybir.dt.from_np(v.dtype), kind="ExternalInput").ap() for n, v in arrays.items()}
    for n in ("x1", "wy", "x4"):
        dram[n] = nc.dram_tensor("mid_" + n, (B, T, D), F32, kind="Internal").ap()
    dram["out"] = nc.dram_tensor("out", (B, T, D), F32, kind="ExternalOutput").ap()
    program(nc, dram)
    return run(nc, [arrays], core_ids=[0]).results[0]["out"]
```
